# Optimizing a Trainium2 kernel written in Bass

```python
import numpy as np
import jax
import jax.numpy as jnp

def _softmax(x, axis=-1):
    return jax.nn.softmax(x, axis=axis)

def _gelu(x):
    return jax.nn.gelu(x, approximate=True)

def _silu(x):
    return jax.nn.silu(x)

def _sigmoid(x):
    return jax.nn.sigmoid(x)

def _layernorm(x, axis=-1, eps=1e-05):
    m = jnp.mean(x, axis=axis, keepdims=True)
    v = jnp.var(x, axis=axis, keepdims=True)
    return (x - m) / jnp.sqrt(v + eps)

def _scatter_add(tgt, idx, src, axis=0):
    return tgt.at[idx].add(src)

def _segment_sum(src, seg, n):
    return jax.ops.segment_sum(src, seg, n)
kernel_name = 'mk_seq_preln_d2_jaxref_r8_545c63'

def setup_inputs(seed: int=0):
    np.random.seed(seed)
    _w = jnp.asarray

    def _L0_attn_setup():
        import jax, jax.numpy as jnp
        import numpy as np
        import math
        D_MODEL, N_HEADS, D_K, D_C, D_HR = (128, 8, 128, 32, 32)
        B, S = (4, 256)
        key = jax.random.key(seed)
        ks = jax.random.split(key, 17)

        def lin(k, fan_in, fan_out):
            lim = 1.0 / math.sqrt(fan_in)
            kw, kb = jax.random.split(k)
            W = jax.random.uniform(kw, (fan_in, fan_out), jnp.float32, -lim, lim)
            b = jax.random.uniform(kb, (fan_out,), jnp.float32, -lim, lim)
            return (W, b)
        W_DQ, b_DQ = lin(ks[0], D_MODEL, D_C)
        W_UQ, b_UQ = lin(ks[1], D_C, N_HEADS * D_K)
        W_DKV, b_DKV = lin(ks[2], D_MODEL, D_C)
        W_UK, b_UK = lin(ks[3], D_C, N_HEADS * D_K)
        W_UV, b_UV = lin(ks[4], D_C, N_HEADS * D_K)
        W_QR, b_QR = lin(ks[5], D_C, N_HEADS * D_HR)
        W_KR, b_KR = lin(ks[6], D_MODEL, D_HR)
        W_O, b_O = lin(ks[7], N_HEADS * D_K, D_MODEL)
        h_t = jax.random.normal(ks[8], (B, S, D_MODEL), jnp.float32)
        return {'h_t': h_t, 'W_DQ': W_DQ, 'b_DQ': b_DQ, 'W_UQ': W_UQ, 'b_UQ': b_UQ, 'W_DKV': W_DKV, 'b_DKV': b_DKV, 'W_UK': W_UK, 'b_UK': b_UK, 'W_UV': W_UV, 'b_UV': b_UV, 'W_QR': W_QR, 'b_QR': b_QR, 'W_KR': W_KR, 'b_KR': b_KR, 'W_O': W_O, 'b_O': b_O}
    _L0_attn_in = _L0_attn_setup()

    def _L0_ffn_setup():
        import jax, jax.numpy as jnp
        import numpy as np
        TOP_K = 2

        def _ffn(x, gw, uw, dw):
            return jax.nn.silu(x @ gw.T) * (x @ uw.T) @ dw.T
        key = jax.random.key(seed)
        ks = jax.random.split(key, 8)
        w = lambda k, shape: jax.random.normal(k, shape, jnp.float32) * 0.02
        return dict(x=jax.random.normal(ks[0], (4, 256, 128), jnp.float32), gate_w=w(ks[1], (8, 128)), expert_gate=w(ks[2], (8, 352, 128)), expert_up=w(ks[3], (8, 352, 128)), expert_down=w(ks[4], (8, 128, 352)), shared_gate=w(ks[5], (352, 128)), shared_up=w(ks[6], (352, 128)), shared_down=w(ks[7], (128, 352)))
    _L0_ffn_in = _L0_ffn_setup()

    def _L1_attn_setup():
        import jax, jax.numpy as jnp
        import numpy as np
        N_HEADS = 16
        ROPE_BASE = 10000.0

        def _rope_tables(seq_len, d_head, dtype):
            inv_freq = 1.0 / ROPE_BASE ** (jnp.arange(0, d_head, 2, dtype=jnp.float32) / d_head)
            t = jnp.arange(seq_len, dtype=jnp.float32)
            freqs = t[:, None] * inv_freq[None, :]
            return (jnp.cos(freqs).astype(dtype), jnp.sin(freqs).astype(dtype))

        def _apply_rope(x, cos, sin):
            half = x.shape[-1] // 2
            x1, x2 = (x[..., :half], x[..., half:])
            return jnp.concatenate([x1 * cos - x2 * sin, x2 * cos + x1 * sin], axis=-1)
        key = jax.random.key(seed)
        k1, k2, k3 = jax.random.split(key, 3)
        d_model = 128
        x = jax.random.normal(k1, (2, 256, d_model), dtype=jnp.float32)
        w_qkv = jax.random.normal(k2, (d_model, 3 * d_model), dtype=jnp.float32) * d_model ** (-0.5)
        w_out = jax.random.normal(k3, (d_model, d_model), dtype=jnp.float32) * d_model ** (-0.5)
        return {'x': x, 'w_qkv': w_qkv, 'w_out': w_out}
    _L1_attn_in = _L1_attn_setup()

    def _L1_ffn_setup():
        import jax, jax.numpy as jnp
        import numpy as np
        TOP_K = 2
        key = jax.random.key(seed)
        ks = jax.random.split(key, 6)
        B, S, D, E = (8, 512, 128, 8)
        s = 1.0 / np.sqrt(D)
        return {'x': jax.random.normal(ks[0], (B, S, D), dtype=jnp.float32), 'Wr': jax.random.normal(ks[1], (D, E), dtype=jnp.float32) * s, 'br': jnp.zeros((E,), dtype=jnp.float32), 'W1': jax.random.normal(ks[2], (E, D, D), dtype=jnp.float32) * s, 'b1': jnp.zeros((E, D), dtype=jnp.float32), 'W2': jax.random.normal(ks[3], (E, D, D), dtype=jnp.float32) * s, 'b2': jnp.zeros((E, D), dtype=jnp.float32)}
    _L1_ffn_in = _L1_ffn_setup()
    _d = {'L0_attn_h_t': _L0_attn_in['h_t'], 'L0_attn_W_DQ': _L0_attn_in['W_DQ'], 'L0_attn_b_DQ': _L0_attn_in['b_DQ'], 'L0_attn_W_UQ': _L0_attn_in['W_UQ'], 'L0_attn_b_UQ': _L0_attn_in['b_UQ'], 'L0_attn_W_DKV': _L0_attn_in['W_DKV'], 'L0_attn_b_DKV': _L0_attn_in['b_DKV'], 'L0_attn_W_UK': _L0_attn_in['W_UK'], 'L0_attn_b_UK': _L0_attn_in['b_UK'], 'L0_attn_W_UV': _L0_attn_in['W_UV'], 'L0_attn_b_UV': _L0_attn_in['b_UV'], 'L0_attn_W_QR': _L0_attn_in['W_QR'], 'L0_attn_b_QR': _L0_attn_in['b_QR'], 'L0_attn_W_KR': _L0_attn_in['W_KR'], 'L0_attn_b_KR': _L0_attn_in['b_KR'], 'L0_attn_W_O': _L0_attn_in['W_O'], 'L0_attn_b_O': _L0_attn_in['b_O'], 'L0_ffn_gate_w': _L0_ffn_in['gate_w'], 'L0_ffn_expert_gate': _L0_ffn_in['expert_gate'], 'L0_ffn_expert_up': _L0_ffn_in['expert_up'], 'L0_ffn_expert_down': _L0_ffn_in['expert_down'], 'L0_ffn_shared_gate': _L0_ffn_in['shared_gate'], 'L0_ffn_shared_up': _L0_ffn_in['shared_up'], 'L0_ffn_shared_down': _L0_ffn_in['shared_down'], 'L1_attn_w_qkv': _L1_attn_in['w_qkv'], 'L1_attn_w_out': _L1_attn_in['w_out'], 'L1_ffn_Wr': _L1_ffn_in['Wr'], 'L1_ffn_br': _L1_ffn_in['br'], 'L1_ffn_W1': _L1_ffn_in['W1'], 'L1_ffn_b1': _L1_ffn_in['b1'], 'L1_ffn_W2': _L1_ffn_in['W2'], 'L1_ffn_b2': _L1_ffn_in['b2']}
    _x0 = _d['L0_attn_h_t']
    _d['L0_attn_h_t'] = jax.random.normal(jax.random.fold_in(jax.random.key(seed), 1), (2, 1024, 128), dtype=_x0.dtype)
    del _x0
    return _d

def reference(L0_attn_h_t, L0_attn_W_DQ, L0_attn_b_DQ, L0_attn_W_UQ, L0_attn_b_UQ, L0_attn_W_DKV, L0_attn_b_DKV, L0_attn_W_UK, L0_attn_b_UK, L0_attn_W_UV, L0_attn_b_UV, L0_attn_W_QR, L0_attn_b_QR, L0_attn_W_KR, L0_attn_b_KR, L0_attn_W_O, L0_attn_b_O, L0_ffn_gate_w, L0_ffn_expert_gate, L0_ffn_expert_up, L0_ffn_expert_down, L0_ffn_shared_gate, L0_ffn_shared_up, L0_ffn_shared_down, L1_attn_w_qkv, L1_attn_w_out, L1_ffn_Wr, L1_ffn_br, L1_ffn_W1, L1_ffn_b1, L1_ffn_W2, L1_ffn_b2):

    def _L0_attn_ref(h_t, W_DQ, b_DQ, W_UQ, b_UQ, W_DKV, b_DKV, W_UK, b_UK, W_UV, b_UV, W_QR, b_QR, W_KR, b_KR, W_O, b_O):
        import jax, jax.numpy as jnp
        import numpy as np
        import math
        D_MODEL, N_HEADS, D_K, D_C, D_HR = (128, 8, 128, 32, 32)
        B, S = (4, 256)
        b, s, _ = h_t.shape
        c_q = h_t @ W_DQ + b_DQ
        c_kv = h_t @ W_DKV + b_DKV
        q_c = (c_q @ W_UQ + b_UQ).reshape(b, s, N_HEADS, D_K).transpose(0, 2, 1, 3)
        k_c = (c_kv @ W_UK + b_UK).reshape(b, s, N_HEADS, D_K).transpose(0, 2, 1, 3)
        v_c = (c_kv @ W_UV + b_UV).reshape(b, s, N_HEADS, D_K).transpose(0, 2, 1, 3)
        q_r = (c_q @ W_QR + b_QR).reshape(b, s, N_HEADS, D_HR).transpose(0, 2, 1, 3)
        k_r = (h_t @ W_KR + b_KR)[:, None, :, :]
        k_r = jnp.broadcast_to(k_r, (b, N_HEADS, s, D_HR))
        q = jnp.concatenate([q_c, q_r], axis=-1)
        k = jnp.concatenate([k_c, k_r], axis=-1)
        scale = 1.0 / math.sqrt(D_K + D_HR)
        scores = jnp.einsum('bhsd,bhtd->bhst', q, k) * scale
        attn = jax.nn.softmax(scores, axis=-1)
        o = jnp.einsum('bhst,bhtd->bhsd', attn, v_c)
        o = o.transpose(0, 2, 1, 3).reshape(b, s, N_HEADS * D_K)
        return o @ W_O + b_O

    def _L0_ffn_ref(x, gate_w, expert_gate, expert_up, expert_down, shared_gate, shared_up, shared_down):
        import jax, jax.numpy as jnp
        import numpy as np
        TOP_K = 2

        def _ffn(x, gw, uw, dw):
            return jax.nn.silu(x @ gw.T) * (x @ uw.T) @ dw.T
        B, S, H = x.shape
        xf = x.reshape(-1, H)
        T = xf.shape[0]
        E = expert_gate.shape[0]
        shared = _ffn(xf, shared_gate, shared_up, shared_down)
        logits = xf @ gate_w.T
        probs = jax.nn.softmax(logits, axis=-1)
        topw, topi = jax.lax.top_k(probs, TOP_K)
        topw = topw / (topw.sum(-1, keepdims=True) + 1e-20)
        comb = jnp.zeros((T, E), xf.dtype).at[jnp.arange(T)[:, None], topi].add(topw)

        def body(acc, ws):
            gw, uw, dw, wcol = ws
            return (acc + _ffn(xf, gw, uw, dw) * wcol[:, None], None)
        routed, _ = jax.lax.scan(body, jnp.zeros_like(xf), (expert_gate, expert_up, expert_down, comb.T))
        return (shared + routed).reshape(B, S, H)

    def _L1_attn_ref(x, w_qkv, w_out):
        import jax, jax.numpy as jnp
        import numpy as np
        N_HEADS = 16
        ROPE_BASE = 10000.0

        def _rope_tables(seq_len, d_head, dtype):
            inv_freq = 1.0 / ROPE_BASE ** (jnp.arange(0, d_head, 2, dtype=jnp.float32) / d_head)
            t = jnp.arange(seq_len, dtype=jnp.float32)
            freqs = t[:, None] * inv_freq[None, :]
            return (jnp.cos(freqs).astype(dtype), jnp.sin(freqs).astype(dtype))

        def _apply_rope(x, cos, sin):
            half = x.shape[-1] // 2
            x1, x2 = (x[..., :half], x[..., half:])
            return jnp.concatenate([x1 * cos - x2 * sin, x2 * cos + x1 * sin], axis=-1)
        B, S, D = x.shape
        H = N_HEADS
        dh = D // H
        scale = dh ** (-0.5)
        qkv = x @ w_qkv
        q, k, v = jnp.split(qkv, 3, axis=-1)

        def to_heads(t):
            return t.reshape(B, S, H, dh).transpose(0, 2, 1, 3)
        q, k, v = (to_heads(q), to_heads(k), to_heads(v))
        cos, sin = _rope_tables(S, dh, x.dtype)
        q = _apply_rope(q, cos, sin)
        k = _apply_rope(k, cos, sin)
        scores = jnp.einsum('bhqd,bhkd->bhqk', q, k) * scale
        causal = jnp.tril(jnp.ones((S, S), dtype=bool))
        scores = jnp.where(causal, scores, jnp.finfo(scores.dtype).min)
        attn = jax.nn.softmax(scores, axis=-1)
        out = jnp.einsum('bhqk,bhkd->bhqd', attn, v)
        out = out.transpose(0, 2, 1, 3).reshape(B, S, D)
        return out @ w_out

    def _L1_ffn_ref(x, Wr, br, W1, b1, W2, b2):
        import jax, jax.numpy as jnp
        import numpy as np
        TOP_K = 2
        k = TOP_K
        scores0 = x[:, 0, :] @ Wr + br
        _, idx = jax.lax.top_k(scores0, k)
        W1g, b1g = (W1[idx], b1[idx])
        W2g, b2g = (W2[idx], b2[idx])
        h = jnp.einsum('bsd,bkde->bkse', x, W1g) + b1g[:, :, None, :]
        h = jax.nn.gelu(h, approximate=False)
        o = jnp.einsum('bkse,bkef->bksf', h, W2g) + b2g[:, :, None, :]
        return jnp.sum(o, axis=1) / k
    x = L0_attn_h_t
    x = x + _L0_attn_ref(_layernorm(x, axis=-1), L0_attn_W_DQ, L0_attn_b_DQ, L0_attn_W_UQ, L0_attn_b_UQ, L0_attn_W_DKV, L0_attn_b_DKV, L0_attn_W_UK, L0_attn_b_UK, L0_attn_W_UV, L0_attn_b_UV, L0_attn_W_QR, L0_attn_b_QR, L0_attn_W_KR, L0_attn_b_KR, L0_attn_W_O, L0_attn_b_O)
    x = x + _L0_ffn_ref(_layernorm(x, axis=-1), L0_ffn_gate_w, L0_ffn_expert_gate, L0_ffn_expert_up, L0_ffn_expert_down, L0_ffn_shared_gate, L0_ffn_shared_up, L0_ffn_shared_down)
    x = x + _L1_attn_ref(_layernorm(x, axis=-1), L1_attn_w_qkv, L1_attn_w_out)
    x = x + _L1_ffn_ref(_layernorm(x, axis=-1), L1_ffn_Wr, L1_ffn_br, L1_ffn_W1, L1_ffn_b1, L1_ffn_W2, L1_ffn_b2)
    return x

_drawn_inputs = setup_inputs


def setup_inputs(seed=0):
    import zlib

    import numpy as np

    out = dict(_drawn_inputs(seed))
    spreads = {'L1_ffn_br': (0.0, 0.1), 'L1_ffn_b1': (0.0, 0.8), 'L1_ffn_b2': (0.0, 0.652)}
    factors = {'L0_attn_W_DQ': 8.0,
     'L0_attn_b_DQ': 8.0,
     'L0_attn_W_UQ': 8.0,
     'L0_attn_b_UQ': 8.0,
     'L0_attn_W_DKV': 6.382,
     'L0_attn_b_DKV': 3.064,
     'L0_attn_W_UK': 8.0,
     'L0_attn_b_UK': 64.0,
     'L0_attn_W_QR': 8.0,
     'L0_attn_b_QR': 8.0,
     'L0_attn_W_KR': 8.0,
     'L0_attn_b_KR': 64.0,
     'L0_ffn_gate_w': 8.0,
     'L0_ffn_expert_gate': 8.0,
     'L0_ffn_expert_up': 8.0,
     'L0_ffn_expert_down': 8.0,
     'L0_ffn_shared_gate': 5.769,
     'L0_ffn_shared_up': 5.708,
     'L0_ffn_shared_down': 5.756}
    for name, (base, spread) in spreads.items():
        noise = np.random.default_rng([zlib.crc32(name.encode()), seed]).standard_normal(out[name].shape)
        drawn = base * np.exp(spread * noise) if base else spread * noise
        out[name] = jnp.asarray(drawn.astype(out[name].dtype))
    for name, factor in factors.items():
        out[name] = (out[name] * factor).astype(out[name].dtype)
    return out
```

```python
from contextlib import ExitStack

import numpy as np

import concourse.bass as bass
from concourse import mybir

ALU = mybir.AluOpType
ACT = mybir.ActivationFunctionType
AX_X = mybir.AxisListType.X
F32 = mybir.dt.float32
F32R = mybir.dt.float32r
BF16 = mybir.dt.bfloat16
I32 = mybir.dt.int32

P = 128
D = 128
B, S = 2, 1024
T = B * S
NT = T // P
TS = S // P
CH = 512
NCH = T // CH
TC = CH // P
EPS = 1e-5

H0, DK, DC, DR = 8, 128, 32, 32
NZ = 3 * DC + 2
NZM = NZ + 2
HP = 2
U0 = B * H0 // HP
UH = H0 // HP
K0 = (S // CH) * TS
SCALE0 = 1.0 / float(DK + DR) ** 0.5

E0, F0 = 8, 352
NE = E0 + 1
FM = [128, 128, 96]
WCOLS = 2 * F0 + 3 * D

H1, DH = 16, 8
HG = 4
U1 = B * (H1 // HG)
RS = 32
SCALE1 = float(DH) ** -0.5
E1 = 8
NEG = -3.0e38

ST1 = [(j, c) for c in range(S // CH) for j in range((c + 1) * TC)]
K1 = len(ST1)
MX0 = [(h, j, c) for h in range(HP) for j in range(TS) for c in range(S // CH)]
MX1 = [(r, i, c) for r in range(HG) for i in range(TS) for c in range(i // TC + 1)]


class Steps:

    def __init__(self, sem):
        self.sem, self.n = sem, 0

    def mark(self, ins):
        ins.then_inc(self.sem, 1)
        self.n += 1
        return self.n


def build(nc, d, out):
    with ExitStack() as ctx:
        def sb(name, shape, dt=F32):
            return ctx.enter_context(nc.sbuf_tensor(name, shape, dt))

        def sem(name):
            return ctx.enter_context(nc.semaphore(name))

        ps = ctx.enter_context(nc.psum_tensor("ps", [P, 8, CH], F32))
        ps_wide, ps_pair, ps_ctx, ps_misc = ps[:, 0:4, :], ps[:, 4:6, :], ps[:, 6, :], ps[:, 7, :]
        MAX0_BANKS, TURN0_BANKS, ST0_BANKS, CTX_BANK = (0, 1, 7), (2, 3), (4, 5), 6
        MAX1_BANKS, ST1_BANKS, TURN1_BANK = (0, 1), (2, 3, 4, 5), 7

        x = sb("x", [P, NT, D])
        xn = sb("xn", [P, NT, D])
        xnT = sb("xnT", [P, T])
        stats = sb("stats", [P, NT, 6])
        mv = sb("mv", [P, NT, 2])
        lnv = sb("lnv", [P, 5, NT])
        ident = sb("ident", [P, P])
        identr = sb("identr", [P, P], F32R)
        identb = sb("identb", [P, P], BF16)
        mask_qk = sb("mask_qk", [P, P], BF16)
        mask_kq = sb("mask_kq", [P, P], BF16)
        ones = sb("ones", [P, P])

        wdq = sb("wdq", [P, 3 * DC])
        bdq = sb("bdq", [3 * DC, 1])
        wkv = sb("wkv", [P, DC + DR])
        bkv = sb("bkv", [DC + DR, 1])
        bkv_row = sb("bkv_row", [1, DC])
        early = sb("early", [P, H0 * (65 + NZ + DC + 1 + D)])
        e0, e1, e2 = H0 * 65, H0 * (65 + NZ), H0 * (65 + NZ + DC + 1)
        uk = early[:, 0:e0].rearrange("p (h n) -> p h n", h=H0)
        uq = early[:, e0:e1].rearrange("p (h n) -> p h n", h=H0)
        uv = early[:, e1:e2].rearrange("p (h n) -> p h n", h=H0)
        wo = early[:, e2:].rearrange("p (h n) -> p h n", h=H0)
        v1 = early[:, 0:TS * B * H1 * (DH + 1)].rearrange("p (t b h w) -> p t b h w", t=TS, b=B, h=H1)
        zmap = sb("zmap", [65, H0, NZ])
        zcur = sb("zcur", [65, HP, NZ])
        bo = sb("bo", [1, D])
        vo = sb("vo", [P, 2, D])
        vo_bias = sb("vo_bias", [1, D])
        cq = sb("cq", [P, T], F32R)
        half = sb("half", [P, T])
        kvr = half[0:65, :]
        ao = half[:].rearrange("p (t b n) -> p t b n", t=TS, b=B)
        ckv = sb("ckv", [P, TS, B, DC + 1])
        ckv_cur = [sb(f"ckv_cur{i}", [P, TS, DC + 1]) for i in range(2)]
        key_stack = [sb(f"key_stack{i}", [P, HP, S], F32R) for i in range(2)]
        query_stack = [sb(f"query_stack{i}", [P, HP, S], F32R) for i in range(2)]
        cT = sb("cT", [P, 2, CH])
        mstage = sb("mstage", [P, HP, TS, NZM], F32R)
        mx = [sb(f"mx{i}", [P, HG * TS]) for i in range(2)]
        mx_part = [sb(f"mx_part{i}", [P, HG * TS]) for i in range(2)]
        pt = sb("pt", [P, 8, CH])
        rden = sb("rden", [P, HG * TC])
        big = sb("big", [P, 2, TS, B, D])

        gw = sb("gw", [P, E0])
        wm = sb("wm", [P, NE, WCOLS])
        tri = sb("tri", [P, E0, E0])
        comb = sb("comb", [P, NT, NE])
        g8 = sb("g8", [P, 4, NT, E0])
        g64 = pt[:, 0:4, :].rearrange("p a n -> p (a n)").rearrange("p (k t e j) -> p k t e j", k=2, t=NT, e=E0)
        g1 = sb("g1", [P, 4, NT])

        wqkv = sb("wqkv", [P, 3 * D])
        wout = sb("wout", [P, D])
        cos = sb("cos", [P, TS, DH])
        sin = sb("sin", [P, TS, DH])
        v_cur = [sb(f"v_cur{i}", [P, TS, HG, DH + 1]) for i in range(2)]
        kstage = [sb(f"kstage{i}", [P, TS, HG, RS], F32R) for i in range(2)]
        qstage = [sb(f"qstage{i}", [P, TS, HG, RS], F32R) for i in range(2)]
        rawqk = xn[:, 0:4, :].rearrange("p a n -> p (a n)").rearrange("p (k t n) -> p k t n", k=2, t=TS)


        zero = sb("zero", [P, 1])

        wr = sb("wr", [P, E1])
        br = sb("br", [1, E1])
        rt = sb("rt", [1, 6, B, E1])
        rt64 = sb("rt64", [1, 2, B, E1, E1])
        ecount = sb("ecount", [1, E1])
        idx_f = sb("idx_f", [1, B, 2])
        idx_i = sb("idx_i", [1, B, 2], I32)
        w1 = sb("w1", [P, B, 2, D])
        b1 = sb("b1", [P, B, 2])
        w2 = sb("w2", [P, B, 2, D])
        b2 = sb("b2", [2, B, D])

        x_in = [sem(f"x_in{i}") for i in range(NCH)]
        w0_in, wm_in, w1_in, sel_in, out_done = map(sem, ("w0_in", "wm_in", "w1_in", "sel_in", "out_done"))
        consts = sem("consts")
        identr_ok, fixed = sem("identr_ok"), sem("fixed")
        ln_stats, ln_aggr, ln_var, ln_root, ln_step, ln_xn, ln_turn, ln_xT = map(
            sem, ("ln_stats", "ln_aggr", "ln_var", "ln_root", "ln_step", "ln_xn", "ln_turn", "ln_xT"))
        prep_mm, prep_done = sem("prep_mm"), sem("prep_done")
        cq_mm, cq_hi, cq_lo, kv_mm, kv_done, ckv_mm, ckv_done = map(
            sem, ("cq_mm", "cq_hi", "cq_lo", "kv_mm", "kv_done", "ckv_mm", "ckv_done"))
        zcur_ok, cq_copied, ckv_copied, ctx_T = map(sem, ("zcur_ok", "cq_copied", "ckv_copied", "ctx_T"))
        ctx_turn, v_copied, ctx1_T, ctx1_turn = map(sem, ("ctx_turn", "v_copied", "ctx1_T", "ctx1_turn"))
        v_ones = sem("v_ones")
        z_mm, z_hi, z_lo, mx_ok, mx1_ok = map(sem, ("z_mm", "z_hi", "z_lo", "mx_ok", "mx1_ok"))
        s_mm, max_done, m_split, m_turn, m_rows = map(sem, ("s_mm", "max_done", "m_split", "m_turn", "m_rows"))
        st_mm, exp_done, pv_mm, ctx_out = map(sem, ("st_mm", "exp_done", "pv_mm", "ctx_out"))
        o_turn, o_T, o_mm, o_add = map(sem, ("o_turn", "o_T", "o_mm", "o_add"))
        gate_mm, gate_step, gate_exp, comb_ok = map(sem, ("gate_mm", "gate_step", "gate_exp", "comb_ok"))
        eg_mm, eu_mm, silu_done, h_done, ed_mm, moe_add = map(
            sem, ("eg_mm", "eu_mm", "silu_done", "h_done", "ed_mm", "moe_add"))
        qkv_mm, qk_out, v_out, rope_mul, rope_step = map(sem, ("qkv_mm", "qk_out", "v_out", "rope_mul", "rope_step"))
        staged, stack_turn, k_stacked, q_stacked = map(sem, ("staged", "stack_turn", "k_stacked", "q_stacked"))
        s1_mm, max1_done, m1_split, m1_turn, m1_rows = map(
            sem, ("s1_mm", "max1_done", "m1_split", "m1_turn", "m1_rows"))
        st1_mm, exp1_done, pv1_mm, ctx1_out = map(sem, ("st1_mm", "exp1_done", "pv1_mm", "ctx1_out"))
        o1_turn, o1_T, o1_mm, o1_add = map(sem, ("o1_turn", "o1_T", "o1_mm", "o1_add"))
        rt_mm, rt_step, idx_ok = sem("rt_mm"), sem("rt_step"), sem("idx_ok")
        f_mm, gelu_done, y_mm, y_add = map(sem, ("f_mm", "gelu_done", "y_mm", "y_add"))

        N_CONST = 7
        N_FIXED = 9
        W0_LOADS, W1_LOADS = 16, 8

        block = ctx.enter_context(nc.Block())

        @block.sync
        def _(sp):
            xd = d["x"].rearrange("(c t p) m -> c p t m", p=P, t=TC)
            for c in range(NCH):
                sp.dma_start(x[:, c * TC:(c + 1) * TC, :], xd[c]).then_inc(x_in[c], 16)
            loads = [(uk, "uk"), (uq, "uq"), (uv, "uv"), (wo, "wo"), (bo, "bo"), (wdq, "wdq"), (bdq, "bdq"),
                     (wkv, "wkv"), (bkv, "bkv"), (bkv_row, "bkv_row"), (ident, "ident"), (identb, "identb"),
                     (gw, "gw"), (tri, "tri"), (mask_qk, "mask_qk")]
            for t, n in loads:
                sp.dma_start(t[:], d[n]).then_inc(w0_in, 16)
            sp.dma_start(zmap[DC:DC + DR, :, :], d["qr"]).then_inc(w0_in, 16)
            assert len(loads) + 1 == W0_LOADS
            sp.dma_start(wm[:], d["wm"]).then_inc(wm_in, 16)
            loads = [(mask_kq, "mask_kq"), (wqkv, "wqkv"), (wout, "wout"), (cos, "cos"), (sin, "sin"),
                     (wr, "wr"), (br, "br"), (ecount, "ecount")]
            for t, n in loads:
                sp.dma_start(t[:], d[n]).then_inc(w1_in, 16)
            assert len(loads) == W1_LOADS
            sp.wait_ge(idx_ok, 1)
            for b in range(B):
                for k in range(2):
                    e = sp.value_load(idx_i[0:1, b, k:k + 1], min_val=0, max_val=E1 - 1)
                    sp.dma_start(w1[:, b, k, :], d["W1"][bass.ds(e, 1)].rearrange("e p n -> (e p) n")).then_inc(sel_in, 16)
                    sp.dma_start(w2[:, b, k, :], d["W2"][bass.ds(e, 1)].rearrange("e p n -> (e p) n")).then_inc(sel_in, 16)
                    sp.dma_start(b1[:, b, k:k + 1], d["b1"][bass.ds(e, 1)].rearrange("e (p u) -> (e p) u", u=1)).then_inc(sel_in, 16)
                    sp.dma_start(b2[k:k + 1, b, :], d["b2"][bass.ds(e, 1)]).then_inc(sel_in, 16)
            od = out.rearrange("(c t p) m -> c p t m", p=P, t=TC)
            for c in range(NCH):
                sp.wait_ge(y_add, c + 1)
                sp.dma_start(od[c], x[:, c * TC:(c + 1) * TC, :]).then_inc(out_done, 16)
            sp.wait_ge(out_done, 16 * NCH)

        @block.gpsimd
        def _(pool):
            nc.gpsimd.memset(zero[:], 0.0).then_inc(consts, 1)
            nc.gpsimd.memset(ckv[:, :, :, DC:DC + 1], 1.0).then_inc(consts, 1)
            nc.gpsimd.memset(comb[:, :, E0:NE], 1.0).then_inc(consts, 1)
            for i in range(2):
                nc.gpsimd.memset(kstage[i][:].bitcast(F32), 0.0).then_inc(consts, 1)
                nc.gpsimd.memset(qstage[i][:].bitcast(F32), 0.0).then_inc(consts, 1)

            def unit0(u, pp, wait):
                pool.wait_ge(z_mm, u * 4)
                for h in range(HP):
                    nc.gpsimd.tensor_copy(zcur[:, h, :], zmap[:, bass.ds((u % UH) * HP + h, 1), :]
                                          .rearrange("p o n -> p (o n)")).then_inc(zcur_ok, 1)
                if wait:
                    pool.wait_ge(pv_mm, u * K0 - K0)
                nc.gpsimd.tensor_copy(ckv_cur[pp][:], ckv[:].rearrange("p t b n -> p t (b n)")
                                      [:, :, bass.ds((u // UH) * (DC + 1), DC + 1)]).then_inc(ckv_copied, 1)

            pool.wait_ge(prep_done, 5)
            pool.wait_ge(ckv_done, 1)
            pool.wait_ge(consts, N_CONST)
            for u in range(2):
                unit0(u, u, False)
            with pool.Fori(1, U0 // 2) as i:
                for pp in range(2):
                    unit0(i * 2 + pp, pp, True)
            pool.wait_ge(prep_mm, 4)
            nc.gpsimd.memset(v1[:, :, :, :, DH:DH + 1], 1.0).then_inc(v_ones, 1)

            none = zero[:].unsqueeze(2).unsqueeze(3).broadcast_to([P, TS, HG, DH])

            def stage(u, pp, wait):
                if wait:
                    pool.wait_ge(pv1_mm, u * K1 - K1)
                nc.gpsimd.tensor_copy(v_cur[pp][:].rearrange("p t h w -> p t (h w)"),
                                      v1.rearrange("p t b h w -> p t (b h w)")
                                      [:, :, bass.ds(u * (HG * (DH + 1)), HG * (DH + 1))]).then_inc(v_copied, 1)
                for n, (dst, src, cols) in enumerate(((kstage[pp], 1, (0, 8, 16)), (qstage[pp], 0, (0, 16, 8)))):
                    val = big[:, src].rearrange("p t b n -> p t (b n)")[:, :, bass.ds(u * (HG * DH), HG * DH)]
                    raw = rawqk[:, n].rearrange("p t (h w) -> p t h w", w=DH)
                    pool.wait_ge(staged, u * 8 + 4 * n)
                    nc.gpsimd.tensor_copy(rawqk[:, n], val).then_inc(staged, 1)
                    hi_a, hi_b, lo = (dst[:, :, :, c:c + DH] for c in cols)
                    pool.wait_ge(staged, u * 8 + 4 * n + 1)
                    nc.gpsimd.tensor_tensor(hi_a, raw, none, ALU.add).then_inc(staged, 1)
                    nc.gpsimd.tensor_tensor(hi_b, raw, none, ALU.add).then_inc(staged, 1)
                    pool.wait_ge(staged, u * 8 + 4 * n + 2)
                    nc.gpsimd.tensor_tensor(lo, raw, hi_a.bitcast(F32), ALU.subtract).then_inc(staged, 1)

            pool.wait_ge(consts, N_CONST)
            for i in range(2):
                nc.gpsimd.memset(kstage[i][:, :, :, 3 * DH:3 * DH + 2].bitcast(F32), 1.0).then_inc(consts, 1)
            pool.wait_ge(consts, N_CONST + 2)
            pool.wait_ge(rope_step, 2 * NCH)
            pool.wait_ge(v_out, NT)
            pool.wait_ge(v_ones, 1)
            for u in range(2):
                stage(u, u, False)
            with pool.Fori(1, U1 // 2) as i:
                for pp in range(2):
                    stage(i * 2 + pp, pp, True)

        @block.scalar
        def _(act):
            def copy(dst, src):
                return nc.scalar.activation(dst, src, ACT.Copy)

            def ln_act(k):
                act.wait_ge(ln_var, k + 1)
                nc.scalar.activation(lnv[:, 1, :], lnv[:, 0, :], ACT.Sqrt).then_inc(ln_root, 1)

            def ln_evacuate(k, c, bank):
                act.wait_ge(ln_turn, k * NCH + c + 1)
                copy(xnT[:, c * CH:(c + 1) * CH], bank).then_inc(ln_xT, 1)

            act.wait_ge(w0_in, 16 * W0_LOADS)
            copy(identr[:], ident[:]).then_inc(identr_ok, 1)
            for g in range(2):
                act.wait_ge(prep_mm, g + 1)
                v = ps_wide[:, g, 0:4 * NZ].rearrange("p (h n) -> p h n", n=NZ)
                copy(zmap[0:DC, 4 * g:4 * g + 4, :], v[0:DC]).then_inc(prep_done, 1)
                copy(zmap[64:65, 4 * g:4 * g + 4, :], v[64:65]).then_inc(prep_done, 1)
            act.wait_ge(prep_mm, 3)
            copy(vo[:], ps_wide[:, 2, 0:2 * D].rearrange("p (g n) -> p g n", g=2)).then_inc(prep_done, 1)
            act.wait_ge(prep_mm, 4)
            copy(vo_bias[:], ps_wide[0:1, 3, 0:D]).then_inc(prep_done, 1)

            ln_act(0)
            for c in range(NCH):
                ln_evacuate(0, c, ps_pair[:, c % 2, :])
                cols = slice(c * CH, (c + 1) * CH)
                act.wait_ge(cq_mm, c + 1)
                nc.scalar.activation(cq[0:3 * DC, cols], ps_ctx[0:3 * DC, :], ACT.Identity,
                                     bias=bdq[:, 0:1]).then_inc(cq_hi, 1)
                act.wait_ge(kv_mm, c + 1)
                nc.scalar.activation(kvr[0:DC + DR, cols], ps_misc[0:DC + DR, :], ACT.Identity,
                                     bias=bkv[:, 0:1]).then_inc(kv_done, 1)

            def z_hi_copy(u, pp, h, c):
                act.wait_ge(z_mm, u * 4 + (2 * h + c + 1))
                copy(key_stack[pp][0:NZ, h, c * CH:(c + 1) * CH], ps[0:NZ, TURN0_BANKS[c], :]).then_inc(z_hi, 1)

            def exps0(u, t, first):
                for h in range(HP):
                    act.wait_ge(st_mm, u * (HP * K0) + (HP * t + h + 1))
                    if not (first and t < 4):
                        act.wait_ge(pv_mm, u * K0 + (t - 3))
                    nc.scalar.activation(pt[:, (HP * t + h) % 8, :], ps[:, ST0_BANKS[h], :], ACT.Exp,
                                         scale=SCALE0).then_inc(exp_done, 1)

            def context_T(u, c, first):
                act.wait_ge(pv_mm, u * K0 + (c + 1) * TS)
                if not first:
                    act.wait_ge(ctx_turn, u * 2 + (c - 1))
                copy(cT[:, c, :], ps[:, CTX_BANK, :]).then_inc(ctx_T, 1)

            def unit0(u, pp, first=False, z=True):
                for t in range(K0):
                    exps0(u, t, first)
                    if t == TS:
                        context_T(u, 0, first)
                if z:
                    z_hi_copy(u + 2, pp, 0, 0)
                    z_hi_copy(u + 2, pp, 0, 1)
                context_T(u, 1, first)
                if z:
                    z_hi_copy(u + 2, pp, 1, 0)
                    z_hi_copy(u + 2, pp, 1, 1)

            act.wait_ge(fixed, N_FIXED)
            for u in range(2):
                for h in range(HP):
                    for c in range(2):
                        z_hi_copy(u, u, h, c)
            unit0(0, 0, first=True)
            unit0(1, 1)
            with act.Fori(1, U0 // 2 - 1) as i:
                unit0(i * 2, 0)
                unit0(i * 2 + 1, 1)
            unit0(U0 - 2, 0, z=False)
            unit0(U0 - 1, 1, z=False)

            for c in range(NCH):
                act.wait_ge(o_turn, 2 * c + 2)
                if c >= 2:
                    act.wait_ge(o_mm, c - 1)
                copy(pt[:, 4 * (c % 2):4 * (c % 2) + 2, :], ps_wide[:, 2 * (c % 2):2 * (c % 2) + 2, :]).then_inc(o_T, 1)

            ln_act(1)
            for c in range(NCH):
                ln_evacuate(1, c, ps_pair[:, c % 2, :])

            act.wait_ge(gate_step, 1)
            nc.scalar.activation(g8[:, 1], g8[:, 0], ACT.Exp).then_inc(gate_exp, 1)

            def silus(ch):
                for v in range(3 * NE):
                    act.wait_ge(eg_mm, ch * (3 * NE) + (v + 1))
                    m = FM[v % 3]
                    if v >= 2:
                        act.wait_ge(h_done, ch * (3 * NE) + (v - 1))
                    else:
                        act.wait_ge(h_done, ch * (3 * NE))
                    nc.scalar.activation(pt[0:m, 6 + v % 2, :], ps_wide[0:m, v % 2, :], ACT.Silu).then_inc(silu_done, 1)

            silus(0)
            with act.Fori(1, NCH) as ch:
                silus(ch)

            ln_act(2)
            for c in range(NCH):
                ln_evacuate(2, c, ps_pair[:, c % 2, :])
                for t in range(c * TC, (c + 1) * TC):
                    b, i = t // TS, t % TS
                    act.wait_ge(qkv_mm, t + 1)
                    bank = ps_wide[:, t % 4, :]
                    copy(big[:, :, i, b, :], bank[:, 0:2 * D].rearrange("p (k n) -> p k n", k=2)).then_inc(qk_out, 1)
                    copy(v1[:, i, b, :, 0:DH],
                         bank[:, 2 * D:3 * D].rearrange("p (h w) -> p h w", w=DH)).then_inc(v_out, 1)

            def k_stack(u, pp, hf):
                act.wait_ge(stack_turn, u * 4 + (2 * hf + 1))
                copy(key_stack[pp][:, 0, hf * CH:(hf + 1) * CH], ps[:, TURN1_BANK, :]).then_inc(k_stacked, 1)

            def exps1(u, t, first):
                j, c = ST1[t]
                w = (c + 1) * CH - max(j * P, c * CH)
                for g in range(2):
                    act.wait_ge(st1_mm, u * (HG * K1) + (HG * t + 2 * g + 2))
                    if not (first and t < 2):
                        act.wait_ge(pv1_mm, u * K1 + (t - 1))
                    nc.scalar.activation(pt[:, 4 * (t % 2) + 2 * g:4 * (t % 2) + 2 * g + 2, 0:w],
                                         ps[:, ST1_BANKS[2 * g]:ST1_BANKS[2 * g] + 2, 0:w], ACT.Exp,
                                         scale=SCALE1).then_inc(exp1_done, 1)

            def context1_T(u, c, first):
                act.wait_ge(pv1_mm, u * K1 + (TC if c == 0 else K1))
                if not first:
                    act.wait_ge(ctx1_turn, u * 2 + (c - 1))
                copy(cT[:, c, :], ps[:, CTX_BANK, :]).then_inc(ctx1_T, 1)

            def unit1(u, pp, first=False, stack=True):
                for t in range(K1):
                    exps1(u, t, first)
                    if t == TC:
                        context1_T(u, 0, first)
                context1_T(u, 1, first)
                if stack:
                    for hf in range(2):
                        k_stack(u + 2, pp, hf)

            for u in range(2):
                for hf in range(2):
                    k_stack(u, u, hf)
            unit1(0, 0, first=True)
            unit1(1, 1)
            with act.Fori(1, U1 // 2 - 1) as i:
                unit1(i * 2, 0)
                unit1(i * 2 + 1, 1)
            unit1(U1 - 2, 0, stack=False)
            unit1(U1 - 1, 1, stack=False)

            for c in range(NCH):
                act.wait_ge(o1_turn, c + 1)
                if c >= 2:
                    act.wait_ge(o1_mm, c - 1)
                copy(pt[:, c % 2, :], ps_wide[:, c % 2, :]).then_inc(o1_T, 1)

            ln_act(3)
            for c in range(NCH):
                ln_evacuate(3, c, ps_pair[:, c % 2, :])
            act.wait_ge(sel_in, 16 * 8 * B)
            for c in range(NCH):
                for k in range(2):
                    act.wait_ge(f_mm, 2 * c + k + 1)
                    if c >= 2:
                        act.wait_ge(y_mm, c - 1)
                    nc.scalar.activation(pt[:, 2 * (c % 2) + k, :], ps_wide[:, k, :], ACT.Gelu,
                                         bias=b1[:, c // 2, k:k + 1]).then_inc(gelu_done, 1)

        @block.tensor
        def _(pe):
            mm = nc.tensor.matmul

            def ln_turns(k, c):
                pe.wait_ge(ln_xn, k * NT + (c + 1) * TC)
                if k or c >= 2:
                    pe.wait_ge(ln_xT, k * NCH + c - 1 if c >= 2 else k * NCH)
                for t in range(TC):
                    ins = nc.tensor.transpose(ps_pair[:, c % 2, t * P:(t + 1) * P], xn[:, c * TC + t, :], ident[:])
                ins.then_inc(ln_turn, 1)

            pe.wait_ge(w0_in, 16 * W0_LOADS)
            for h in range(H0):
                g, r = h // 4, h % 4
                ins = mm(ps_wide[0:65, g, r * NZ:(r + 1) * NZ], uk[:, h, :], uq[:, h, :], start=True, stop=True)
                if r == 3:
                    ins.then_inc(prep_mm, 1)
            for h in range(H0):
                g, r = h // 4, h % 4
                ins = mm(ps_wide[32 * r:32 * r + 32, 2, g * D:(g + 1) * D], uv[:, h, 0:DC], wo[:, h, :],
                         start=True, stop=True)
            ins.then_inc(prep_mm, 1)
            pe.wait_ge(fixed, N_FIXED)
            for h in range(H0):
                mm(ps_wide[0:1, 3, 0:D], uv[:, h, DC:DC + 1], wo[:, h, :], start=(h == 0), stop=False)
            mm(ps_wide[0:1, 3, 0:D], ones[0:1, 0:1], bo[:], start=False, stop=True).then_inc(prep_mm, 1)

            for c in range(NCH):
                cols = slice(c * CH, (c + 1) * CH)
                ln_turns(0, c)
                pe.wait_ge(ln_xT, c + 1)
                if c:
                    pe.wait_ge(cq_lo, c)
                mm(ps_ctx[0:3 * DC, :], wdq[:], xnT[:, cols], start=True, stop=True).then_inc(cq_mm, 1)
                if c:
                    pe.wait_ge(kv_done, c)
                mm(ps_misc[0:DC + DR, :], wkv[:], xnT[:, cols], start=True, stop=True).then_inc(kv_mm, 1)
                if c == 0:
                    pe.wait_ge(prep_done, 6)
                for t in range(c * TC, (c + 1) * TC):
                    o = ps_wide[:, 0, t * DC:(t + 1) * DC]
                    mm(o, xnT[:, t * P:(t + 1) * P], wkv[:, 0:DC], start=True, stop=False)
                    ins = mm(o, ones[0:1, :], bkv_row[:], start=False, stop=True)
            ins.then_inc(ckv_mm, 1)

            def make_z(u, h, c):
                bank = TURN0_BANKS[c]
                if h == 0:
                    pe.wait_ge(zcur_ok, u * HP + HP)
                    pe.wait_ge(m_rows, max(u * 4 + (c - 1), 0) if isinstance(u, int) else u * 4 + (c - 1))
                else:
                    pe.wait_ge(z_lo, u * 4 + (c + 1))
                mm(ps[0:NZ, bank, :], zcur[:, h, :], kvr[:, bass.ds((u // UH) * S + c * CH, CH)],
                   start=True, stop=True).then_inc(z_mm, 1)

            def scores_max(u, pp, s, first):
                h, j, c = MX0[s]
                if s == 0:
                    pe.wait_ge(z_lo, u * 4 + 4)
                    pe.wait_ge(cq_copied, u * HP + HP)
                if not (first and s < 3):
                    pe.wait_ge(max_done, u * len(MX0) + ((s - 2) if s >= 3 else min(s - 1, 0)))
                mm(ps[:, MAX0_BANKS[s % 3], :], query_stack[pp][0:NZ, h, j * P:(j + 1) * P],
                   key_stack[pp][0:NZ, h, c * CH:(c + 1) * CH], start=True, stop=True).then_inc(s_mm, 1)

            def turn_max(u, h, hf, first):
                if h == 0 and hf == 0:
                    pe.wait_ge(m_split, u * 2 + 2)
                elif h == 0:
                    if not first:
                        pe.wait_ge(ctx_out, u * 4 - 2)
                else:
                    pe.wait_ge(m_rows, u * 4 + (hf + 1))
                for t in range(TC):
                    ins = nc.tensor.transpose(ps[0:NZM, TURN0_BANKS[hf], t * P:(t + 1) * P].bitcast(F32R),
                                              mstage[:, h, hf * TC + t, :], identr[:])
                ins.then_inc(m_turn, 1)

            def scores(u, pp, h, t, first):
                c, kt = t // TS, t % TS
                if t == 0 and h == 0:
                    pe.wait_ge(m_rows, u * 4 + 4)
                if not (first and t == 0):
                    pe.wait_ge(exp_done, u * (HP * K0) + (HP * (t - 1) + h + 1))
                mm(ps[:, ST0_BANKS[h], :], key_stack[pp][0:NZM, h, kt * P:(kt + 1) * P],
                   query_stack[pp][0:NZM, h, c * CH:(c + 1) * CH], start=True, stop=True).then_inc(st_mm, 1)

            def values(u, pp, t, first):
                c, kt = t // TS, t % TS
                if t == 0:
                    pe.wait_ge(ckv_copied, u + 1)
                if kt == 0 and not (first and c == 0):
                    pe.wait_ge(ctx_T, u * 2 + c)
                pe.wait_ge(exp_done, u * (HP * K0) + (HP * t + HP))
                for h in range(HP):
                    ins = mm(ps[64 * h:64 * h + DC + 1, CTX_BANK, :], ckv_cur[pp][:, kt, :],
                             pt[:, (HP * t + h) % 8, :], start=(kt == 0), stop=(kt == TS - 1))
                ins.then_inc(pv_mm, 1)

            def turn_context(u, c, first):
                pe.wait_ge(ctx_T, u * 2 + (c + 1))
                if not (first and c == 0):
                    pe.wait_ge(ctx_out, u * 4 + 2 * c)
                for t in range(TC):
                    ins = nc.tensor.transpose(ps[:, TURN0_BANKS[1], t * P:(t + 1) * P],
                                              cT[:, c, t * P:(t + 1) * P], ident[:])
                ins.then_inc(ctx_turn, 1)

            def unit0(u, pp, first=False, s=True, z=True):
                n = 0
                for t in range(K0):
                    for h in range(HP):
                        scores(u, pp, h, t, first)
                        if s and n < len(MX0):
                            scores_max(u + 1, 1 - pp, n, False)
                            n += 1
                    if t:
                        values(u, pp, t - 1, first)
                    if s and n < len(MX0):
                        scores_max(u + 1, 1 - pp, n, False)
                        n += 1
                    if t == 2 and not first:
                        turn_context(u - 1, 1, False)
                    if t == TS + 2:
                        turn_context(u, 0, first)
                    if s and t >= K0 - 4:
                        turn_max(u + 1, (t - K0 + 4) // 2, t % 2, False)
                if z:
                    make_z(u + 2, 0, 0)
                    make_z(u + 2, 0, 1)
                values(u, pp, K0 - 1, first)
                if z:
                    make_z(u + 2, 1, 0)
                    make_z(u + 2, 1, 1)

            pe.wait_ge(consts, N_CONST)
            pe.wait_ge(identr_ok, 1)
            pe.wait_ge(cq_lo, NCH)
            pe.wait_ge(kv_done, NCH)
            pe.wait_ge(ckv_done, 1)
            for h in range(HP):
                for c in range(2):
                    make_z(0, h, c)
            for n in range(len(MX0)):
                scores_max(0, 0, n, True)
            for h in range(HP):
                for hf in range(2):
                    turn_max(0, h, hf, True)
            for h in range(HP):
                for c in range(2):
                    make_z(1, h, c)
            unit0(0, 0, first=True)
            unit0(1, 1)
            with pe.Fori(1, U0 // 2 - 1) as i:
                unit0(i * 2, 0)
                unit0(i * 2 + 1, 1)
            unit0(U0 - 2, 0, z=False)
            unit0(U0 - 1, 1, s=False, z=False)
            turn_context(U0 - 1, 1, False)

            ctxn = big[:].rearrange("p a t b n -> p (a t b n)").rearrange("p (t b n) -> p t b n", t=TS, b=B)

            def o_turns(c):
                if c == 0:
                    pe.wait_ge(ctx_out, 4 * U0)
                if c >= 2:
                    pe.wait_ge(o_T, c - 1)
                for g in range(2):
                    for t in range(TC):
                        b, i = (c * TC + t) // TS, (c * TC + t) % TS
                        ins = nc.tensor.transpose(ps_wide[:, 2 * (c % 2) + g, t * P:(t + 1) * P],
                                                  ctxn[:, i, b, g * P:(g + 1) * P], ident[:])
                    ins.then_inc(o_turn, 1)

            def o_mms(c):
                pe.wait_ge(o_T, c + 1)
                if c >= 2:
                    pe.wait_ge(o_add, c - 1)
                for t in range(TC):
                    o = ps_pair[:, c % 2, t * P:(t + 1) * P]
                    for g in range(2):
                        mm(o, pt[:, 4 * (c % 2) + g, t * P:(t + 1) * P], vo[:, g, :], start=(g == 0), stop=False)
                    ins = mm(o, ones[0:1, :], vo_bias[:], start=False, stop=True)
                ins.then_inc(o_mm, 1)

            for c in range(NCH + 1):
                if c < NCH:
                    o_turns(c)
                if c:
                    o_mms(c - 1)

            pe.wait_ge(o_add, NCH)
            for c in range(NCH):
                ln_turns(1, c)
            for c in range(NCH):
                pe.wait_ge(ln_xT, NCH + c + 1)
                for t in range(c * TC, (c + 1) * TC):
                    ins = mm(ps_ctx[:, t * E0:(t + 1) * E0], xnT[:, t * P:(t + 1) * P], gw[:], start=True, stop=True)
            ins.then_inc(gate_mm, 1)
            pe.wait_ge(wm_in, 16)

            def gate_up(ch, e):
                for f in range(3):
                    v, m = 3 * e + f, FM[f]
                    pe.wait_ge(h_done, ch * (3 * NE) + max(v - 1, 0))
                    rhs = xnT[:, bass.ds(ch * CH, CH)]
                    for bank, w0, done in ((v % 2, 0, eg_mm), (2 + v % 2, F0, eu_mm)):
                        mm(ps_wide[0:m, bank, :], wm[:, e, w0 + f * P:w0 + f * P + m], rhs,
                           start=True, stop=True).then_inc(done, 1)

            def down(ch, e):
                pe.wait_ge(h_done, ch * (3 * NE) + (3 * e + 3))
                pe.wait_ge(moe_add, ch * (TC * NE) + TC * max(e - 1, 0))
                for t in range(TC):
                    for f in range(3):
                        m = FM[f]
                        ins = mm(ps_pair[:, e % 2, t * P:(t + 1) * P], pt[0:m, 3 * (e % 2) + f, t * P:(t + 1) * P],
                                 wm[0:m, e, 2 * F0 + f * D:2 * F0 + (f + 1) * D], start=(f == 0), stop=(f == 2))
                ins.then_inc(ed_mm, 1)

            def experts(ch):
                gate_up(ch, 0)
                for e in range(NE):
                    if e + 1 < NE:
                        gate_up(ch, e + 1)
                    down(ch, e)

            experts(0)
            with pe.Fori(1, NCH) as ch:
                experts(ch)

            pe.wait_ge(moe_add, NCH * TC * NE)
            pe.wait_ge(w1_in, 16 * W1_LOADS)
            for c in range(NCH):
                ln_turns(2, c)
                pe.wait_ge(ln_xT, 2 * NCH + c + 1)
                for t in range(c * TC, (c + 1) * TC):
                    if t >= 4:
                        pe.wait_ge(v_out, t - 3)
                    mm(ps_wide[:, t % 4, 0:3 * D], xnT[:, t * P:(t + 1) * P], wqkv[:],
                       start=True, stop=True).then_inc(qkv_mm, 1)

            def turn_stack(u, pp, n):
                hf, src = n // 2, (kstage, qstage)[n % 2][pp]
                if n == 0:
                    pe.wait_ge(staged, u * 8 + 8)
                    pe.wait_ge(m1_rows, u * 2)
                else:
                    pe.wait_ge((k_stacked, q_stacked)[(n - 1) % 2], u * 2 + ((n - 1) // 2 + 1))
                for t in range(TC):
                    ins = nc.tensor.transpose(ps[:, TURN1_BANK, t * P:(t + 1) * P].bitcast(F32R),
                                              src[:, hf * TC + t].rearrange("p h w -> p (h w)"), identr[:])
                ins.then_inc(stack_turn, 1)

            def scores_max1(u, pp, s, first):
                r, i, c = MX1[s]
                if s == 0:
                    pe.wait_ge(k_stacked, u * 2 + 2)
                    pe.wait_ge(q_stacked, u * 2 + 2)
                if not (first and s < 2):
                    pe.wait_ge(max1_done, u * len(MX1) + (s - 1))
                rows = slice(RS * r, RS * r + 3 * DH)
                w = min((i + 1) * P, (c + 1) * CH) - c * CH
                diag = c == i // TC
                bank = MAX1_BANKS[s % 2]
                ins = mm(ps[:, bank, 0:w], query_stack[pp][rows, 0, i * P:(i + 1) * P],
                         key_stack[pp][rows, 0, c * CH:c * CH + w], start=True, stop=not diag)
                if diag:
                    ins = mm(ps[:, bank, w - P:w], identb[:], mask_qk[:], start=False, stop=True)
                ins.then_inc(s1_mm, 1)

            def turn_max1(u, pp, hf, first):
                if hf:
                    pe.wait_ge(m1_rows, u * 2 + 1)
                else:
                    pe.wait_ge(m1_split, u * 2 + 2)
                    if not first:
                        pe.wait_ge(ctx1_out, u * 4 - 2)
                for t in range(TC):
                    ins = nc.tensor.transpose(ps[:, TURN1_BANK, t * P:(t + 1) * P].bitcast(F32R),
                                              qstage[pp][:, hf * TC + t].rearrange("p h w -> p (h w)"), identr[:])
                ins.then_inc(m1_turn, 1)

            def scores1(u, pp, r, t, first):
                j, c = ST1[t]
                q0 = max(j * P, c * CH)
                w = (c + 1) * CH - q0
                if t == 0 and r == 0:
                    pe.wait_ge(m1_rows, u * 2 + 2)
                if r % 2 == 0 and not (first and t == 0):
                    pe.wait_ge(exp1_done, u * (2 * K1) + (2 * (t - 1) + r // 2 + 1))
                rows = slice(RS * r, RS * r + 3 * DH + 2)
                diag = j * P >= c * CH
                bank = ST1_BANKS[r]
                ins = mm(ps[:, bank, 0:w], key_stack[pp][rows, 0, j * P:(j + 1) * P],
                         query_stack[pp][rows, 0, q0:q0 + w], start=True, stop=not diag)
                if diag:
                    ins = mm(ps[:, bank, 0:P], identb[:], mask_kq[:], start=False, stop=True)
                ins.then_inc(st1_mm, 1)

            def values1(u, pp, t, first):
                j, c = ST1[t]
                q0 = max(j * P, c * CH)
                w = (c + 1) * CH - q0
                if t == 0:
                    pe.wait_ge(v_copied, u + 1)
                if j == 0 and not (first and c == 0):
                    pe.wait_ge(ctx1_T, u * 2 + c)
                pe.wait_ge(exp1_done, u * (2 * K1) + (2 * t + 2))
                for r in range(HG):
                    ins = mm(ps[RS * r:RS * r + DH + 1, CTX_BANK, q0 - c * CH:CH], v_cur[pp][:, j, r, :],
                             pt[:, 4 * (t % 2) + r, 0:w], start=(j == 0), stop=(j == (c + 1) * TC - 1))
                ins.then_inc(pv1_mm, 1)

            def turned_before(u, c):
                if isinstance(u, int):
                    return min(2 * (u + 2 + c), 2 * U1)
                return u * 2 + (2 * c + 4)

            def turn_context1(u, c, first):
                pe.wait_ge(ctx1_T, u * 2 + (c + 1))
                if not (first and c == 0):
                    pe.wait_ge(ctx1_out, u * 4 + 2 * c)
                pe.wait_ge(q_stacked, turned_before(u, c))
                for t in range(TC):
                    ins = nc.tensor.transpose(ps[:, TURN1_BANK, t * P:(t + 1) * P],
                                              cT[:, c, t * P:(t + 1) * P], ident[:])
                ins.then_inc(ctx1_turn, 1)

            def unit1(u, pp, first=False, s=True, t=True):
                n = 0
                for k in range(K1):
                    for r in range(HG):
                        scores1(u, pp, r, k, first)
                        if s and n < len(MX1):
                            scores_max1(u + 1, 1 - pp, n, False)
                            n += 1
                    if k:
                        values1(u, pp, k - 1, first)
                    if s and n < len(MX1):
                        scores_max1(u + 1, 1 - pp, n, False)
                        n += 1
                    if k == 1 and not first:
                        turn_context1(u - 1, 1, False)
                    if k == TC + 2:
                        turn_context1(u, 0, first)
                    if s and k == K1 - 1:
                        turn_max1(u + 1, 1 - pp, 0, False)
                values1(u, pp, K1 - 1, first)
                if s:
                    turn_max1(u + 1, 1 - pp, 1, False)
                if t:
                    for n in range(4):
                        turn_stack(u + 2, pp, n)

            for n in range(4):
                turn_stack(0, 0, n)
            for n in range(len(MX1)):
                scores_max1(0, 0, n, True)
            turn_max1(0, 0, 0, True)
            turn_max1(0, 0, 1, True)
            for n in range(4):
                turn_stack(1, 1, n)
            unit1(0, 0, first=True)
            unit1(1, 1)
            with pe.Fori(1, U1 // 2 - 1) as i:
                unit1(i * 2, 0)
                unit1(i * 2 + 1, 1)
            unit1(U1 - 2, 0, t=False)
            unit1(U1 - 1, 1, s=False, t=False)
            turn_context1(U1 - 1, 1, False)

            def o1_turns(c):
                if c == 0:
                    pe.wait_ge(ctx1_out, 4 * U1)
                if c >= 2:
                    pe.wait_ge(o1_T, c - 1)
                for t in range(TC):
                    b, i = (c * TC + t) // TS, (c * TC + t) % TS
                    ins = nc.tensor.transpose(ps_wide[:, c % 2, t * P:(t + 1) * P], ao[:, i, b, :], ident[:])
                ins.then_inc(o1_turn, 1)

            def o1_mms(c):
                pe.wait_ge(o1_T, c + 1)
                if c >= 2:
                    pe.wait_ge(o1_add, c - 1)
                for t in range(TC):
                    ins = mm(ps_pair[:, c % 2, t * P:(t + 1) * P], pt[:, c % 2, t * P:(t + 1) * P], wout[:],
                             start=True, stop=True)
                ins.then_inc(o1_mm, 1)

            for c in range(NCH + 1):
                if c < NCH:
                    o1_turns(c)
                if c:
                    o1_mms(c - 1)

            pe.wait_ge(o1_add, NCH)
            for c in range(NCH):
                ln_turns(3, c)
            for b in range(B):
                pe.wait_ge(ln_xT, 3 * NCH + b * (NCH // B) + 1)
                o = ps_ctx[0:1, b * E1:(b + 1) * E1]
                mm(o, xnT[:, b * S:b * S + 1], wr[:], start=True, stop=False)
                ins = mm(o, ones[0:1, 0:1], br[:], start=False, stop=True)
            ins.then_inc(rt_mm, 1)
            pe.wait_ge(ln_xT, 4 * NCH)
            pe.wait_ge(sel_in, 16 * 8 * B)

            def f_mms(c):
                for k in range(2):
                    if c:
                        pe.wait_ge(gelu_done, 2 * c - 1 + k)
                    mm(ps_wide[:, k, :], w1[:, c // 2, k, :], xnT[:, c * CH:(c + 1) * CH],
                       start=True, stop=True).then_inc(f_mm, 1)

            def y_mms(c):
                pe.wait_ge(gelu_done, 2 * c + 2)
                if c >= 2:
                    pe.wait_ge(y_add, c - 1)
                for t in range(TC):
                    o = ps_pair[:, c % 2, t * P:(t + 1) * P]
                    for k in range(2):
                        mm(o, pt[:, 2 * (c % 2) + k, t * P:(t + 1) * P], w2[:, c // 2, k, :], start=(k == 0), stop=False)
                    ins = mm(o, ones[0:2, :], b2[:, c // 2, :], start=False, stop=True)
                ins.then_inc(y_mm, 1)

            for c in range(NCH + 1):
                if c < NCH:
                    f_mms(c)
                if c:
                    y_mms(c - 1)

        @block.vector
        def _(dve):
            v = nc.vector

            def layer_norm(k, ready):
                for t in range(NT):
                    ready(t)
                    v.bn_stats(stats[:, t, :], x[:, t, :]).then_inc(ln_stats, 1)
                for t in range(NT):
                    dve.wait_ge(ln_stats, k * NT + t + 1)
                    v.bn_aggr(mv[:, t, :], stats[:, t, :]).then_inc(ln_aggr, 1)
                dve.wait_ge(ln_aggr, (k + 1) * NT)
                v.tensor_scalar(lnv[:, 0, :], mv[:, :, 1], EPS, None, ALU.add).then_inc(ln_var, 1)
                dve.wait_ge(ln_root, k + 1)
                s = 5 * k
                v.reciprocal(lnv[:, 2, :], lnv[:, 1, :]).then_inc(ln_step, 1)
                dve.wait_ge(ln_step, s + 1)
                v.tensor_tensor(lnv[:, 3, :], lnv[:, 2, :], lnv[:, 2, :], ALU.mult).then_inc(ln_step, 1)
                dve.wait_ge(ln_step, s + 2)
                v.tensor_tensor(lnv[:, 1, :], lnv[:, 3, :], lnv[:, 0, :], ALU.mult).then_inc(ln_step, 1)
                dve.wait_ge(ln_step, s + 3)
                v.tensor_scalar(lnv[:, 3, :], lnv[:, 1, :], -0.5, 1.5, ALU.mult, ALU.add).then_inc(ln_step, 1)
                dve.wait_ge(ln_step, s + 4)
                v.tensor_tensor(lnv[:, 4, :], lnv[:, 2, :], lnv[:, 3, :], ALU.mult).then_inc(ln_step, 1)
                dve.wait_ge(ln_step, s + 5)
                for t in range(NT):
                    v.tensor_scalar(xn[:, t, :], x[:, t, :], mv[:, t, 0:1], lnv[:, 4, t:t + 1],
                                    ALU.subtract, ALU.mult).then_inc(ln_xn, 1)

            v.memset(ones[:], 1.0).then_inc(fixed, 1)
            v.memset(ps[:, CTX_BANK, :], 0.0).then_inc(fixed, 1)
            for i in range(2):
                v.memset(key_stack[i][96:NZM].bitcast(F32), 1.0).then_inc(fixed, 1)
                v.memset(query_stack[i][96:NZ].bitcast(F32), 1.0).then_inc(fixed, 1)
            v.memset(kvr[64:65, :], 1.0).then_inc(fixed, 1)
            v.memset(mstage[:, :, :, 0:3 * DC].bitcast(F32), 0.0).then_inc(fixed, 1)
            v.memset(mstage[:, :, :, 3 * DC:NZ].bitcast(F32), 1.0).then_inc(fixed, 1)

            layer_norm(0, lambda t: dve.wait_ge(x_in[t // TC], 16))
            dve.wait_ge(w0_in, 16 * W0_LOADS)
            for c in range(NCH):
                cols = slice(c * CH, (c + 1) * CH)
                dve.wait_ge(cq_hi, c + 1)
                v.scalar_tensor_tensor(out=cq[DC:2 * DC, cols], in0=ps_ctx[DC:2 * DC, :], scalar=bdq[DC:2 * DC, 0:1],
                                       in1=cq[DC:2 * DC, cols].bitcast(F32), op0=ALU.add,
                                       op1=ALU.subtract).then_inc(cq_lo, 1)
            dve.wait_ge(ckv_mm, 1)
            v.tensor_copy(ckv[:, :, :, 0:DC],
                          ps_wide[:, 0, :].rearrange("p (b t n) -> p t b n", b=B, n=DC)).then_inc(ckv_done, 1)

            def z_lo_part(u, pp, h, c):
                cols = slice(c * CH, (c + 1) * CH)
                dve.wait_ge(z_hi, u * 4 + (2 * h + c + 1))
                rows = slice(2 * DC, 3 * DC + 1)
                v.tensor_tensor(key_stack[pp][rows, h, cols], ps[rows, TURN0_BANKS[c], :],
                                key_stack[pp][rows, h, cols].bitcast(F32), ALU.subtract).then_inc(z_lo, 1)

            def copy_cq(u, pp, first):
                if not first:
                    dve.wait_ge(st_mm, u * (HP * K0) - HP * K0)
                for h in range(HP):
                    v.tensor_copy(query_stack[pp][0:3 * DC, h, :],
                                  cq[0:3 * DC, bass.ds((u // UH) * S, S)]).then_inc(cq_copied, 1)

            def maximum(u, pp, s):
                h, j, c = MX0[s]
                dve.wait_ge(s_mm, u * len(MX0) + (s + 1))
                v.tensor_reduce(mx_part[pp][:, s:s + 1], ps[:, MAX0_BANKS[s % 3], :], AX_X, ALU.max).then_inc(max_done, 1)

            def split_max(u, pp, first):
                dve.wait_ge(max_done, u * len(MX0) + len(MX0))
                n = HP * TS
                v.tensor_tensor(mx[pp][:, 0:n], mx_part[pp][:, 0:2 * n:2], mx_part[pp][:, 1:2 * n:2],
                                ALU.max).then_inc(mx_ok, 1)
                dve.wait_ge(mx_ok, u + 1)
                m = mx[pp][:, 0:n].rearrange("p (h t) -> p h t", h=HP)
                if not first:
                    dve.wait_ge(m_turn, u * 4)
                v.tensor_scalar(mstage[:, :, :, NZ], m, -1.0, None, ALU.mult).then_inc(m_split, 1)
                dve.wait_ge(m_split, u * 2 + 1)
                v.scalar_tensor_tensor(out=mstage[:, :, :, NZ + 1], in0=m, scalar=-1.0,
                                       in1=mstage[:, :, :, NZ].bitcast(F32), op0=ALU.mult,
                                       op1=ALU.subtract).then_inc(m_split, 1)

            def max_rows(u, pp, h, hf):
                dve.wait_ge(m_turn, u * 4 + (2 * h + hf + 1))
                v.tensor_copy(query_stack[pp][96:NZM, h, hf * CH:(hf + 1) * CH],
                              ps[96:NZM, TURN0_BANKS[hf], :]).then_inc(m_rows, 1)

            ctxn = big[:].rearrange("p a t b n -> p (a t b n)").rearrange("p (t n) -> p t n", t=TS)

            def contexts_out(u, c):
                dve.wait_ge(ctx_turn, u * 2 + (c + 1))
                a = ps[:, TURN0_BANKS[1], :].rearrange("p (t h n) -> p t h n", t=TC, h=HP)
                r = rden[:, 0:TC * HP].rearrange("p (t h) -> p t h", h=HP)
                v.reciprocal(r, a[:, :, :, DC]).then_inc(ctx_out, 1)
                dve.wait_ge(ctx_out, u * 4 + (2 * c + 1))
                dst = ctxn[:, c * TC:(c + 1) * TC, bass.ds(u * (HP * DC), HP * DC)].rearrange("p t (h n) -> p t h n", h=HP)
                v.tensor_tensor(dst, a[:, :, :, 0:DC], r.unsqueeze(3).broadcast_to([P, TC, HP, DC]),
                                ALU.mult).then_inc(ctx_out, 1)

            def unit0(u, pp, first=False, s=True, z=True):
                for n in range(len(MX0)):
                    if n == 8 and not first:
                        contexts_out(u - 1, 1)
                    if s:
                        maximum(u + 1, 1 - pp, n)
                if s:
                    split_max(u + 1, 1 - pp, False)
                contexts_out(u, 0)
                if s:
                    for h in range(HP):
                        for hf in range(2):
                            max_rows(u + 1, 1 - pp, h, hf)
                if z:
                    z_lo_part(u + 2, pp, 0, 0)
                    z_lo_part(u + 2, pp, 0, 1)
                    copy_cq(u + 2, pp, False)
                    z_lo_part(u + 2, pp, 1, 0)
                    z_lo_part(u + 2, pp, 1, 1)

            for u in range(2):
                copy_cq(u, u, True)
            for h in range(HP):
                for c in range(2):
                    z_lo_part(0, 0, h, c)
            for n in range(len(MX0)):
                maximum(0, 0, n)
            split_max(0, 0, True)
            for h in range(HP):
                for hf in range(2):
                    max_rows(0, 0, h, hf)
            for h in range(HP):
                for c in range(2):
                    z_lo_part(1, 1, h, c)
            unit0(0, 0, first=True)
            unit0(1, 1)
            with dve.Fori(1, U0 // 2 - 1) as i:
                unit0(i * 2, 0)
                unit0(i * 2 + 1, 1)
            unit0(U0 - 2, 0, z=False)
            unit0(U0 - 1, 1, s=False, z=False)
            contexts_out(U0 - 1, 1)

            for c in range(NCH):
                dve.wait_ge(o_mm, c + 1)
                xc = x[:, c * TC:(c + 1) * TC, :].rearrange("p t n -> p (t n)")
                v.tensor_tensor(xc, ps_pair[:, c % 2, :], xc, ALU.add).then_inc(o_add, 1)
            layer_norm(1, lambda t: dve.wait_ge(o_add, t // TC + 1))
            gs = Steps(gate_step)
            dve.wait_ge(gate_mm, 1)
            logits = ps_ctx[:, 0:NT * E0].rearrange("p (t e) -> p t e", e=E0)
            top = g1[:, 0, :]

            def over_e(a):
                return a.unsqueeze(2).broadcast_to([P, NT, E0])

            v.tensor_reduce(top, logits, AX_X, ALU.max).then_inc(comb_ok, 1)
            dve.wait_ge(comb_ok, 1)
            gs.mark(v.tensor_tensor(g8[:, 0], logits, over_e(top), ALU.subtract))
            dve.wait_ge(gate_exp, 1)
            n = gs.mark(v.tensor_reduce(g1[:, 1, :], g8[:, 1], AX_X, ALU.add))
            dve.wait_ge(gate_step, n)
            n = gs.mark(v.reciprocal(g1[:, 2, :], g1[:, 1, :]))
            dve.wait_ge(gate_step, n)
            n = gs.mark(v.tensor_tensor(g8[:, 2], g8[:, 1], over_e(g1[:, 2, :]), ALU.mult))
            dve.wait_ge(gate_step, n)
            p_e = g8[:, 2].unsqueeze(3).broadcast_to([P, NT, E0, E0])
            p_j = g8[:, 2].unsqueeze(2).broadcast_to([P, NT, E0, E0])
            gs.mark(v.tensor_tensor(g64[:, 0], p_j, p_e, ALU.is_gt))
            n = gs.mark(v.tensor_tensor(g64[:, 1], p_j, p_e, ALU.is_equal))
            dve.wait_ge(gate_step, n)
            n = gs.mark(v.tensor_tensor(g64[:, 1], g64[:, 1], tri[:].unsqueeze(1).broadcast_to([P, NT, E0, E0]),
                                        ALU.mult))
            dve.wait_ge(gate_step, n)
            n = gs.mark(v.tensor_tensor(g64[:, 0], g64[:, 0], g64[:, 1], ALU.add))
            dve.wait_ge(gate_step, n)
            n = gs.mark(v.tensor_reduce(g8[:, 3], g64[:, 0], AX_X, ALU.add))
            dve.wait_ge(gate_step, n)
            n = gs.mark(v.scalar_tensor_tensor(out=g8[:, 0], in0=g8[:, 3], scalar=1.5, in1=g8[:, 2],
                                               op0=ALU.is_lt, op1=ALU.mult))
            dve.wait_ge(gate_step, n)
            n = gs.mark(v.tensor_reduce(g1[:, 1, :], g8[:, 0], AX_X, ALU.add))
            dve.wait_ge(gate_step, n)
            n = gs.mark(v.tensor_scalar(g1[:, 2, :], g1[:, 1, :], 1e-20, None, ALU.add))
            dve.wait_ge(gate_step, n)
            n = gs.mark(v.reciprocal(g1[:, 3, :], g1[:, 2, :]))
            dve.wait_ge(gate_step, n)
            dve.wait_ge(consts, N_CONST)
            v.tensor_tensor(comb[:, :, 0:E0], g8[:, 0], over_e(g1[:, 3, :]), ALU.mult).then_inc(comb_ok, 1)
            dve.wait_ge(comb_ok, 2)

            def hidden(ch, e):
                for f in range(3):
                    n, m = 3 * e + f, FM[f]
                    dve.wait_ge(silu_done, ch * (3 * NE) + (n + 1))
                    dve.wait_ge(eu_mm, ch * (3 * NE) + (n + 1))
                    if f == 0:
                        dve.wait_ge(ed_mm, ch * NE + max(e - 1, 0))
                    v.tensor_tensor(pt[0:m, 3 * (e % 2) + f, :], ps_wide[0:m, 2 + n % 2, :], pt[0:m, 6 + n % 2, :],
                                    ALU.mult).then_inc(h_done, 1)

            def accumulate(ch, e):
                dve.wait_ge(ed_mm, ch * NE + (e + 1))
                for t in range(TC):
                    dve.wait_ge(moe_add, ch * (TC * NE) + max(TC * (e - 1) + t + 1, 0))
                    xt = x[:, bass.ds(ch * TC + t, 1), :].rearrange("p o n -> p (o n)")
                    w = comb[:, bass.ds(ch * TC + t, 1), e:e + 1].rearrange("p o n -> p (o n)")
                    v.scalar_tensor_tensor(out=xt, in0=ps_pair[:, e % 2, t * P:(t + 1) * P], scalar=w, in1=xt,
                                           op0=ALU.mult, op1=ALU.add).then_inc(moe_add, 1)

            def experts(ch):
                hidden(ch, 0)
                for e in range(NE):
                    if e + 1 < NE:
                        hidden(ch, e + 1)
                    accumulate(ch, e)

            experts(0)
            with dve.Fori(1, NCH) as ch:
                experts(ch)

            dve.wait_ge(moe_add, NCH * TC * NE)
            layer_norm(2, lambda t: None)
            dve.wait_ge(w1_in, 16 * W1_LOADS)
            for c in range(NCH):
                b, i0 = c * TC // TS, c * TC % TS
                dve.wait_ge(qk_out, (c + 1) * TC)
                qk = [big[:, a, i0:i0 + TC, b, :].rearrange("p t (h w) -> p t h w", w=DH) for a in range(2)]
                ta = [pt[:, a, :].rearrange("p (t h w) -> p t h w", t=TC, w=DH) for a in range(2)]
                tb = [pt[:, 2 + a, :].rearrange("p (t h w) -> p t h w", t=TC, w=DH) for a in range(2)]
                h = DH // 2

                def over_heads(tab, lo, hi):
                    return tab[:, i0:i0 + TC, lo:hi].unsqueeze(2).broadcast_to([P, TC, H1, hi - lo])

                if c:
                    dve.wait_ge(rope_step, 2 * c)
                for a in range(2):
                    v.tensor_tensor(ta[a], qk[a], over_heads(cos, 0, DH), ALU.mult).then_inc(rope_mul, 1)
                    v.tensor_tensor(tb[a][:, :, :, 0:h], qk[a][:, :, :, h:DH], over_heads(sin, 0, h), ALU.mult).then_inc(rope_mul, 1)
                    v.tensor_tensor(tb[a][:, :, :, h:DH], qk[a][:, :, :, 0:h], over_heads(sin, h, DH), ALU.mult).then_inc(rope_mul, 1)
                dve.wait_ge(rope_mul, 6 * (c + 1))
                for a in range(2):
                    v.tensor_tensor(qk[a], ta[a], tb[a], ALU.add).then_inc(rope_step, 1)

            def q_stack(u, pp, hf):
                dve.wait_ge(stack_turn, u * 4 + (2 * hf + 2))
                v.tensor_copy(query_stack[pp][:, 0, hf * CH:(hf + 1) * CH], ps[:, TURN1_BANK, :]).then_inc(q_stacked, 1)

            def maximum1(u, pp, s):
                r, i, c = MX1[s]
                w = min((i + 1) * P, (c + 1) * CH) - c * CH
                n = TS * r + (i if i < TC else 2 * (i - TC) + c)
                dst = (mx if i < TC else mx_part)[pp][:, n:n + 1]
                dve.wait_ge(s1_mm, u * len(MX1) + (s + 1))
                v.tensor_reduce(dst, ps[:, MAX1_BANKS[s % 2], 0:w], AX_X, ALU.max).then_inc(max1_done, 1)

            def split_max1(u, pp):
                dve.wait_ge(max1_done, u * len(MX1) + len(MX1))
                part = mx_part[pp][:].rearrange("p (r t c) -> p r t c", r=HG, c=2)
                v.tensor_tensor(mx[pp][:].rearrange("p (r t) -> p r t", r=HG)[:, :, TC:TS], part[:, :, :, 0],
                                part[:, :, :, 1], ALU.max).then_inc(mx1_ok, 1)
                dve.wait_ge(mx1_ok, u + 1)
                m = mx[pp][:].rearrange("p (r t) -> p t r", r=HG)
                hi, lo = (qstage[pp][:, :, :, 3 * DH + n] for n in range(2))
                v.tensor_scalar(hi, m, -1.0, None, ALU.mult).then_inc(m1_split, 1)
                dve.wait_ge(m1_split, u * 2 + 1)
                v.scalar_tensor_tensor(out=lo, in0=m, scalar=-1.0, in1=hi.bitcast(F32), op0=ALU.mult,
                                       op1=ALU.subtract).then_inc(m1_split, 1)

            def max_rows1(u, pp, hf):
                dve.wait_ge(m1_turn, u * 2 + (hf + 1))
                v.tensor_copy(query_stack[pp][:, 0, hf * CH:(hf + 1) * CH], ps[:, TURN1_BANK, :]).then_inc(m1_rows, 1)

            def contexts_out1(u, c):
                dve.wait_ge(ctx1_turn, u * 2 + (c + 1))
                a = ps[:, TURN1_BANK, :].rearrange("p (t r n) -> p t r n", t=TC, r=HG)
                r = rden[:].rearrange("p (t r) -> p t r", r=HG)
                v.reciprocal(r, a[:, :, :, DH]).then_inc(ctx1_out, 1)
                dve.wait_ge(ctx1_out, u * 4 + (2 * c + 1))
                dst = ao.rearrange("p t b n -> p t (b n)")[:, c * TC:(c + 1) * TC, bass.ds(u * (HG * DH), HG * DH)] \
                    .rearrange("p t (r w) -> p t r w", w=DH)
                v.tensor_tensor(dst, a[:, :, :, 0:DH], r.unsqueeze(3).broadcast_to([P, TC, HG, DH]),
                                ALU.mult).then_inc(ctx1_out, 1)

            def unit1(u, pp, first=False, s=True, t=True):
                for n in range(len(MX1)):
                    if n == 9 and not first:
                        contexts_out1(u - 1, 1)
                    if s:
                        maximum1(u + 1, 1 - pp, n)
                if s:
                    split_max1(u + 1, 1 - pp)
                contexts_out1(u, 0)
                if s:
                    for hf in range(2):
                        max_rows1(u + 1, 1 - pp, hf)
                if t:
                    for hf in range(2):
                        q_stack(u + 2, pp, hf)

            for hf in range(2):
                q_stack(0, 0, hf)
            for n in range(len(MX1)):
                maximum1(0, 0, n)
            split_max1(0, 0)
            for hf in range(2):
                max_rows1(0, 0, hf)
            for hf in range(2):
                q_stack(1, 1, hf)
            unit1(0, 0, first=True)
            unit1(1, 1)
            with dve.Fori(1, U1 // 2 - 1) as i:
                unit1(i * 2, 0)
                unit1(i * 2 + 1, 1)
            unit1(U1 - 2, 0, t=False)
            unit1(U1 - 1, 1, s=False, t=False)
            contexts_out1(U1 - 1, 1)

            for c in range(NCH):
                dve.wait_ge(o1_mm, c + 1)
                xc = x[:, c * TC:(c + 1) * TC, :].rearrange("p t n -> p (t n)")
                v.tensor_tensor(xc, ps_pair[:, c % 2, :], xc, ALU.add).then_inc(o1_add, 1)
            layer_norm(3, lambda t: dve.wait_ge(o1_add, t // TC + 1))

            rs = Steps(rt_step)
            dve.wait_ge(rt_mm, 1)
            n = rs.mark(v.tensor_copy(rt[:, 0], ps_ctx[0:1, 0:B * E1].rearrange("p (b e) -> p b e", b=B)))
            dve.wait_ge(rt_step, n)
            s_e = rt[:, 0].unsqueeze(3).broadcast_to([1, B, E1, E1])
            s_j = rt[:, 0].unsqueeze(2).broadcast_to([1, B, E1, E1])
            rs.mark(v.tensor_tensor(rt64[:, 0], s_j, s_e, ALU.is_gt))
            n = rs.mark(v.tensor_tensor(rt64[:, 1], s_j, s_e, ALU.is_equal))
            dve.wait_ge(rt_step, n)
            n = rs.mark(v.tensor_tensor(rt64[:, 1], rt64[:, 1], tri[0:1].unsqueeze(1).broadcast_to([1, B, E1, E1]),
                                        ALU.mult))
            dve.wait_ge(rt_step, n)
            n = rs.mark(v.tensor_tensor(rt64[:, 0], rt64[:, 0], rt64[:, 1], ALU.add))
            dve.wait_ge(rt_step, n)
            n = rs.mark(v.tensor_reduce(rt[:, 1], rt64[:, 0], AX_X, ALU.add))
            dve.wait_ge(rt_step, n)
            for k in range(2):
                n = rs.mark(v.scalar_tensor_tensor(out=rt[:, 2 + k], in0=rt[:, 1], scalar=float(k),
                                                   in1=ecount[:].unsqueeze(1).broadcast_to([1, B, E1]),
                                                   op0=ALU.is_equal, op1=ALU.mult))
            dve.wait_ge(rt_step, n)
            for k in range(2):
                n = rs.mark(v.tensor_reduce(idx_f[:, :, k], rt[:, 2 + k], AX_X, ALU.add))
            dve.wait_ge(rt_step, n)
            v.tensor_copy(idx_i[:], idx_f[:]).then_inc(idx_ok, 1)

            for c in range(NCH):
                dve.wait_ge(y_mm, c + 1)
                xc = x[:, c * TC:(c + 1) * TC, :].rearrange("p t n -> p (t n)")
                v.scalar_tensor_tensor(out=xc, in0=ps_pair[:, c % 2, :], scalar=0.5, in1=xc,
                                       op0=ALU.mult, op1=ALU.add).then_inc(y_add, 1)


def lay_out(i):
    a = {k: np.asarray(v) for k, v in i.items()}
    f = np.float32

    def heads(w, b, n):
        return (w.reshape(w.shape[0], H0, n).transpose(2, 1, 0), b.reshape(1, H0, n).transpose(2, 1, 0))

    uq, ubq = heads(a["L0_attn_W_UQ"], a["L0_attn_b_UQ"], DK)
    qr, qrb = heads(a["L0_attn_W_QR"], a["L0_attn_b_QR"], DR)
    uk, ukb = heads(a["L0_attn_W_UK"], a["L0_attn_b_UK"], DK)
    uv, uvb = heads(a["L0_attn_W_UV"], a["L0_attn_b_UV"], DK)
    up = np.concatenate([a["L0_ffn_expert_gate"], a["L0_ffn_shared_gate"][None]], 0)
    uu = np.concatenate([a["L0_ffn_expert_up"], a["L0_ffn_shared_up"][None]], 0)
    dn = np.concatenate([a["L0_ffn_expert_down"], a["L0_ffn_shared_down"][None]], 0).transpose(0, 2, 1)
    dnp = np.zeros((NE, 3 * P, D), f)
    dnp[:, :F0] = dn
    dnp = dnp.reshape(NE, 3, P, D).transpose(2, 0, 1, 3).reshape(P, NE, 3 * D)
    wm = np.concatenate([up.transpose(2, 0, 1), uu.transpose(2, 0, 1), dnp], 2)

    inv = (f(1.0) / f(10000.0) ** (np.arange(0, DH, 2, dtype=f) / f(DH))).astype(f)
    fr = np.arange(S, dtype=f)[:, None] * inv[None, :]
    c, s = np.cos(fr).astype(f), np.sin(fr).astype(f)
    cos = np.concatenate([c, c], 1).reshape(TS, P, DH).transpose(1, 0, 2)
    sin = np.concatenate([-s, s], 1).reshape(TS, P, DH).transpose(1, 0, 2)
    bf = mybir.dt.np(BF16)
    later = np.triu(np.full((P, P), NEG, f), 1)
    tri = np.broadcast_to(np.tril(np.ones((E0, E0), f), -1), (P, E0, E0))
    out = {
        "x": a["L0_attn_h_t"].reshape(T, D),
        "uk": np.concatenate([uk, np.zeros((DK, H0, 64 - DC), f), ukb], 2),
        "uq": np.concatenate([uq, uq, uq, ubq, ubq], 2),
        "qr": np.concatenate([qr, qr, qr, qrb, qrb], 2),
        "uv": np.concatenate([uv, uvb], 2),
        "wo": a["L0_attn_W_O"].reshape(H0, DK, D).transpose(1, 0, 2),
        "bo": a["L0_attn_b_O"][None],
        "wdq": np.concatenate([a["L0_attn_W_DQ"]] * 3, 1),
        "bdq": np.concatenate([a["L0_attn_b_DQ"]] * 3)[:, None],
        "wkv": np.concatenate([a["L0_attn_W_DKV"], a["L0_attn_W_KR"]], 1),
        "bkv": np.concatenate([a["L0_attn_b_DKV"], a["L0_attn_b_KR"]])[:, None],
        "bkv_row": a["L0_attn_b_DKV"][None],
        "ident": np.eye(P, dtype=f), "identb": np.eye(P).astype(bf),
        "mask_qk": later.astype(bf), "mask_kq": later.T.astype(bf),
        "gw": a["L0_ffn_gate_w"].T, "tri": tri, "wm": wm,
        "wqkv": a["L1_attn_w_qkv"], "wout": a["L1_attn_w_out"], "cos": cos, "sin": sin,
        "wr": a["L1_ffn_Wr"], "br": a["L1_ffn_br"][None], "ecount": np.arange(E1, dtype=f)[None],
        "W1": a["L1_ffn_W1"], "b1": a["L1_ffn_b1"], "W2": a["L1_ffn_W2"], "b2": a["L1_ffn_b2"],
    }
    return {k: np.ascontiguousarray(v) for k, v in out.items()}


def kernel(**inputs):
    import concourse.bacc as bacc
    from concourse.bass_utils import run_bass_kernel_spmd

    arrays = {f"in_{k}": v for k, v in lay_out(inputs).items()}
    nc = bacc.Bacc("TRN2", target_bir_lowering=False, num_devices=1)
    d = {k[3:]: nc.dram_tensor(k, v.shape, mybir.dt.from_np(v.dtype), kind="ExternalInput").ap()
         for k, v in arrays.items()}
    out = nc.dram_tensor("out_0", (T, D), F32, kind="ExternalOutput").ap()
    build(nc, d, out)
    r = run_bass_kernel_spmd(nc, [arrays], core_ids=[0])
    return r.results[0]["out_0"].reshape(B, S, D)
```

```python
from contextlib import ExitStack

import numpy as np

import concourse.bass as bass
from concourse import mybir

ALU = mybir.AluOpType
ACT = mybir.ActivationFunctionType
AX_X = mybir.AxisListType.X
F32 = mybir.dt.float32
F32R = mybir.dt.float32r
BF16 = mybir.dt.bfloat16
I32 = mybir.dt.int32

P = 128
D = 128
B, S = 2, 1024
T = B * S
NT = T // P
TS = S // P
CH = 512
NCH = T // CH
TC = CH // P
EPS = 1e-5

H0, DK, DC, DR = 8, 128, 32, 32
NZ = 3 * DC + 2
NZM = NZ + 2
HP = 2
U0 = B * H0 // HP
UH = H0 // HP
K0 = (S // CH) * TS
SCALE0 = 1.0 / float(DK + DR) ** 0.5

E0, F0 = 8, 352
NE = E0 + 1
FM = [128, 128, 96]
WCOLS = 2 * F0 + 3 * D

H1, DH = 16, 8
HG = 4
U1 = B * (H1 // HG)
RS = 32
SCALE1 = float(DH) ** -0.5
E1 = 8
NEG = -3.0e38

ST1 = []
for c in range(S // CH):
    j0 = c * TC
    ST1 += [(c, ((j, 0, CH),)) for j in range(j0 + 1)]
    ST1 += [(c, ((j0 + 1, 0, CH - P), (j0 + 3, CH - P, P))), (c, ((j0 + 2, 0, CH - 2 * P),))]
K1 = len(ST1)
K1_FIRST = [c for c, _ in ST1].index(1)
MX0 = [(h, j, c) for c in range(S // CH) for j in range(TS) for h in range(HP)]
MX0_STEP = 3
Z0_SECOND, CTX0_BEFORE, CTX0_FIRST, TURN0_MAX, Z0_FIRST = (0, 1), 2, 10, (11, 11, 12, 13), (14, 15)

MX1 = []
for i0, c in ((0, 0), (TC, 0), (TC, 1)):
    if c * TC == i0:
        parts = [((i0, 0, P), (i0 + 2, P, 3 * P)), ((i0 + 1, 0, 2 * P),), ((i0 + 3, 0, CH),)]
    else:
        parts = [((i, 0, CH),) for i in range(i0, i0 + TC)]
    MX1 += [(r, c, p) for p in parts for r in range(HG)]
MX1_Q_HALF = [m[2][0][0] >= TC for m in MX1].index(True)
MX1_K_HALF = [m[1] for m in MX1].index(1)
MX1_END = [sum(len(m[2]) for m in MX1[:s + 1]) for s in range(len(MX1))]
NMX1 = MX1_END[-1]
STACK1_SECOND, CTX1_BEFORE, CTX1_FIRST, STACK1_FIRST, TURN1_MAX = (0, 1), 2, 5, (6, 7), (8, 9)
MX1_STEP = 5


class Steps:

    def __init__(self, sem):
        self.sem, self.n = sem, 0

    def mark(self, ins):
        ins.then_inc(self.sem, 1)
        self.n += 1
        return self.n


def build(nc, d, out):
    with ExitStack() as ctx:
        def sb(name, shape, dt=F32):
            return ctx.enter_context(nc.sbuf_tensor(name, shape, dt))

        def sem(name):
            return ctx.enter_context(nc.semaphore(name))

        ps = ctx.enter_context(nc.psum_tensor("ps", [P, 8, CH], F32))
        ps_wide, ps_pair, ps_ctx, ps_misc = ps[:, 0:4, :], ps[:, 4:6, :], ps[:, 6, :], ps[:, 7, :]
        MAX0_BANKS, TURN0_BANKS, ST0_BANKS, CTX_BANK = (0, 1, 7), (2, 3), (4, 5), 6
        MAX1_BANKS, ST1_BANKS, TURN1_BANK = (0, 1), (2, 3, 4, 5), 7

        x = sb("x", [P, NT, D])
        xn = sb("xn", [P, NT, D])
        xnT = sb("xnT", [P, T])
        stats = sb("stats", [P, NT, 6])
        mv = sb("mv", [P, NT, 2])
        lnv = sb("lnv", [P, 5, NT])
        ident = sb("ident", [P, P])
        identr = sb("identr", [P, P], F32R)
        identb = sb("identb", [P, P], BF16)
        mask_qk = sb("mask_qk", [P, P], BF16)
        mask_kq = sb("mask_kq", [P, P], BF16)
        ones = sb("ones", [P, P])

        wdq = sb("wdq", [P, 3 * DC])
        bdq = sb("bdq", [3 * DC, 1])
        wkv = sb("wkv", [P, DC + DR])
        bkv = sb("bkv", [DC + DR, 1])
        bkv_row = sb("bkv_row", [1, DC])
        early = sb("early", [P, H0 * (65 + NZ + DC + 1 + D)])
        e0, e1, e2 = H0 * 65, H0 * (65 + NZ), H0 * (65 + NZ + DC + 1)
        uk = early[:, 0:e0].rearrange("p (h n) -> p h n", h=H0)
        uq = early[:, e0:e1].rearrange("p (h n) -> p h n", h=H0)
        uv = early[:, e1:e2].rearrange("p (h n) -> p h n", h=H0)
        wo = early[:, e2:].rearrange("p (h n) -> p h n", h=H0)
        v1 = early[:, 0:TS * B * H1 * (DH + 1)].rearrange("p (t b h w) -> p t b h w", t=TS, b=B, h=H1)
        zmap = sb("zmap", [65, H0, NZ])
        zcur = sb("zcur", [65, HP, NZ])
        bo = sb("bo", [1, D])
        vo = sb("vo", [P, 2, D])
        vo_bias = sb("vo_bias", [1, D])
        cq = sb("cq", [P, T], F32R)
        half = sb("half", [P, T])
        kvr = half[0:65, :]
        ao = half[:].rearrange("p (t b n) -> p t b n", t=TS, b=B)
        ckv = sb("ckv", [P, TS, B, DC + 1])
        ckv_cur = [sb(f"ckv_cur{i}", [P, TS, DC + 1]) for i in range(2)]
        stacks = sb("stacks", [P, 4 * HP * S], F32R)
        key_stack, query_stack = ([stacks[:, (2 * k + i) * HP * S:(2 * k + i + 1) * HP * S]
                                   .rearrange("p (h n) -> p h n", h=HP) for i in range(2)] for k in range(2))
        key_stack1 = [stacks[:, i * HG * S:(i + 1) * HG * S].rearrange("p (r n) -> p r n", r=HG) for i in range(2)]
        query_stack1 = [cq[:, i * S:(i + 1) * S] for i in range(2)]
        cT = sb("cT", [P, 2, CH])
        mstage = sb("mstage", [P, HP, TS, NZM], F32R)
        mx = [sb(f"mx{i}", [P, HG * TS]) for i in range(2)]
        mx_part = [sb(f"mx_part{i}", [P, HG * TS]) for i in range(2)]
        pt = sb("pt", [P, 8, CH])
        rden = sb("rden", [P, HG * TC])
        big = sb("big", [P, 2, TS, B, D])

        gw = sb("gw", [P, E0])
        wm = sb("wm", [P, NE, WCOLS])
        tri = sb("tri", [P, E0, E0])
        comb = sb("comb", [P, NT, NE])
        g8 = sb("g8", [P, 4, NT, E0])
        g64 = pt[:, 0:4, :].rearrange("p a n -> p (a n)").rearrange("p (k t e j) -> p k t e j", k=2, t=NT, e=E0)
        g1 = sb("g1", [P, 4, NT])

        wqkv = sb("wqkv", [P, 3 * D])
        wout = sb("wout", [P, D])
        cos = sb("cos", [P, TS, DH])
        sin = sb("sin", [P, TS, DH])
        v_cur = [sb(f"v_cur{i}", [P, TS, HG, DH + 1]) for i in range(2)]
        kstage = [sb(f"kstage{i}", [P, TS, HG, RS], F32R) for i in range(2)]
        qstage = [sb(f"qstage{i}", [P, TS, HG, RS], F32R) for i in range(2)]
        rawqk = xn[:, 0:4, :].rearrange("p a n -> p (a n)").rearrange("p (k t n) -> p k t n", k=2, t=TS)


        zero = sb("zero", [P, 1])

        wr = sb("wr", [P, E1])
        br = sb("br", [1, E1])
        rt = sb("rt", [1, 6, B, E1])
        rt64 = sb("rt64", [1, 2, B, E1, E1])
        ecount = sb("ecount", [1, E1])
        idx_f = sb("idx_f", [1, B, 2])
        idx_i = sb("idx_i", [1, B, 2], I32)
        w1 = sb("w1", [P, B, 2, D])
        b1 = sb("b1", [P, B, 2])
        w2 = sb("w2", [P, B, 2, D])
        b2 = sb("b2", [2, B, D])

        x_in = [sem(f"x_in{i}") for i in range(NCH)]
        w0_in, wm_in, w1_in, sel_in, out_done = map(sem, ("w0_in", "wm_in", "w1_in", "sel_in", "out_done"))
        consts = sem("consts")
        identr_ok, fixed = sem("identr_ok"), sem("fixed")
        ln_stats, ln_aggr, ln_var, ln_root, ln_step, ln_xn, ln_turn, ln_xT = map(
            sem, ("ln_stats", "ln_aggr", "ln_var", "ln_root", "ln_step", "ln_xn", "ln_turn", "ln_xT"))
        prep_mm, prep_done = sem("prep_mm"), sem("prep_done")
        cq_mm, cq_hi, cq_lo, kv_mm, kv_done, ckv_mm, ckv_done = map(
            sem, ("cq_mm", "cq_hi", "cq_lo", "kv_mm", "kv_done", "ckv_mm", "ckv_done"))
        zcur_ok, cq_copied, ckv_copied, ctx_T = map(sem, ("zcur_ok", "cq_copied", "ckv_copied", "ctx_T"))
        ctx_turn, v_copied, ctx1_T, ctx1_turn = map(sem, ("ctx_turn", "v_copied", "ctx1_T", "ctx1_turn"))
        v_ones = sem("v_ones")
        z_mm, z_hi, z_lo, mx_ok, mx1_ok = map(sem, ("z_mm", "z_hi", "z_lo", "mx_ok", "mx1_ok"))
        s_mm, max_done, m_split, m_turn, m_rows = map(sem, ("s_mm", "max_done", "m_split", "m_turn", "m_rows"))
        st_mm, exp_done, pv_mm, ctx_out = map(sem, ("st_mm", "exp_done", "pv_mm", "ctx_out"))
        o_turn, o_T, o_mm, o_add = map(sem, ("o_turn", "o_T", "o_mm", "o_add"))
        gate_mm, gate_step, gate_exp, comb_ok = map(sem, ("gate_mm", "gate_step", "gate_exp", "comb_ok"))
        eg_mm, eu_mm, silu_done, h_done, ed_mm, moe_add = map(
            sem, ("eg_mm", "eu_mm", "silu_done", "h_done", "ed_mm", "moe_add"))
        qkv_mm, qk_out, v_out, rope_mul, rope_step = map(sem, ("qkv_mm", "qk_out", "v_out", "rope_mul", "rope_step"))
        staged, stack_turn, stacked, keys_zero = map(sem, ("staged", "stack_turn", "stacked", "keys_zero"))
        s1_mm, max1_done, m1_split, m1_turn, m1_rows = map(
            sem, ("s1_mm", "max1_done", "m1_split", "m1_turn", "m1_rows"))
        st1_mm, exp1_done, pv1_mm, ctx1_out = map(sem, ("st1_mm", "exp1_done", "pv1_mm", "ctx1_out"))
        o1_turn, o1_T, o1_mm, o1_add = map(sem, ("o1_turn", "o1_T", "o1_mm", "o1_add"))
        rt_mm, rt_step, idx_ok = sem("rt_mm"), sem("rt_step"), sem("idx_ok")
        f_mm, gelu_done, y_mm, y_add = map(sem, ("f_mm", "gelu_done", "y_mm", "y_add"))

        N_CONST = 7
        N_FIXED = 9
        W0_LOADS, W1_LOADS = 16, 8

        block = ctx.enter_context(nc.Block())

        @block.sync
        def _(sp):
            xd = d["x"].rearrange("(c t p) m -> c p t m", p=P, t=TC)
            for c in range(NCH):
                sp.dma_start(x[:, c * TC:(c + 1) * TC, :], xd[c]).then_inc(x_in[c], 16)
            loads = [(uk, "uk"), (uq, "uq"), (uv, "uv"), (wo, "wo"), (bo, "bo"), (wdq, "wdq"), (bdq, "bdq"),
                     (wkv, "wkv"), (bkv, "bkv"), (bkv_row, "bkv_row"), (ident, "ident"), (identb, "identb"),
                     (gw, "gw"), (tri, "tri"), (mask_qk, "mask_qk")]
            for t, n in loads:
                sp.dma_start(t[:], d[n]).then_inc(w0_in, 16)
            sp.dma_start(zmap[DC:DC + DR, :, :], d["qr"]).then_inc(w0_in, 16)
            assert len(loads) + 1 == W0_LOADS
            sp.dma_start(wm[:], d["wm"]).then_inc(wm_in, 16)
            loads = [(mask_kq, "mask_kq"), (wqkv, "wqkv"), (wout, "wout"), (cos, "cos"), (sin, "sin"),
                     (wr, "wr"), (br, "br"), (ecount, "ecount")]
            for t, n in loads:
                sp.dma_start(t[:], d[n]).then_inc(w1_in, 16)
            assert len(loads) == W1_LOADS
            sp.wait_ge(idx_ok, 1)
            for b in range(B):
                for k in range(2):
                    e = sp.value_load(idx_i[0:1, b, k:k + 1], min_val=0, max_val=E1 - 1)
                    sp.dma_start(w1[:, b, k, :], d["W1"][bass.ds(e, 1)].rearrange("e p n -> (e p) n")).then_inc(sel_in, 16)
                    sp.dma_start(w2[:, b, k, :], d["W2"][bass.ds(e, 1)].rearrange("e p n -> (e p) n")).then_inc(sel_in, 16)
                    sp.dma_start(b1[:, b, k:k + 1], d["b1"][bass.ds(e, 1)].rearrange("e (p u) -> (e p) u", u=1)).then_inc(sel_in, 16)
                    sp.dma_start(b2[k:k + 1, b, :], d["b2"][bass.ds(e, 1)]).then_inc(sel_in, 16)
            od = out.rearrange("(c t p) m -> c p t m", p=P, t=TC)
            for c in range(NCH):
                sp.wait_ge(y_add, c + 1)
                sp.dma_start(od[c], x[:, c * TC:(c + 1) * TC, :]).then_inc(out_done, 16)
            sp.wait_ge(out_done, 16 * NCH)

        @block.gpsimd
        def _(pool):
            nc.gpsimd.memset(zero[:], 0.0).then_inc(consts, 1)
            nc.gpsimd.memset(ckv[:, :, :, DC:DC + 1], 1.0).then_inc(consts, 1)
            nc.gpsimd.memset(comb[:, :, E0:NE], 1.0).then_inc(consts, 1)
            for i in range(2):
                nc.gpsimd.memset(kstage[i][:].bitcast(F32), 0.0).then_inc(consts, 1)
                nc.gpsimd.memset(qstage[i][:].bitcast(F32), 0.0).then_inc(consts, 1)

            def unit0(u, pp, wait):
                pool.wait_ge(z_mm, u * 4)
                for h in range(HP):
                    nc.gpsimd.tensor_copy(zcur[:, h, :], zmap[:, bass.ds((u % UH) * HP + h, 1), :]
                                          .rearrange("p o n -> p (o n)")).then_inc(zcur_ok, 1)
                if wait:
                    pool.wait_ge(pv_mm, u * K0 - K0)
                nc.gpsimd.tensor_copy(ckv_cur[pp][:], ckv[:].rearrange("p t b n -> p t (b n)")
                                      [:, :, bass.ds((u // UH) * (DC + 1), DC + 1)]).then_inc(ckv_copied, 1)

            pool.wait_ge(prep_done, 5)
            pool.wait_ge(ckv_done, 1)
            pool.wait_ge(consts, N_CONST)
            for u in range(2):
                unit0(u, u, False)
            with pool.Fori(1, U0 // 2) as i:
                for pp in range(2):
                    unit0(i * 2 + pp, pp, True)
            pool.wait_ge(prep_mm, 4)
            nc.gpsimd.memset(v1[:, :, :, :, DH:DH + 1], 1.0).then_inc(v_ones, 1)

            none = zero[:].unsqueeze(2).unsqueeze(3).broadcast_to([P, TS, HG, DH])

            def stage(u, pp, wait):
                if wait:
                    pool.wait_ge(m1_turn, u * 2 - 2)
                for n, (dst, src, cols) in enumerate(((kstage[pp], 1, (0, 8, 16)), (qstage[pp], 0, (0, 16, 8)))):
                    val = big[:, src].rearrange("p t b n -> p t (b n)")[:, :, bass.ds(u * (HG * DH), HG * DH)]
                    raw = rawqk[:, n].rearrange("p t (h w) -> p t h w", w=DH)
                    pool.wait_ge(staged, u * 8 + 4 * n)
                    nc.gpsimd.tensor_copy(rawqk[:, n], val).then_inc(staged, 1)
                    hi_a, hi_b, lo = (dst[:, :, :, c:c + DH] for c in cols)
                    pool.wait_ge(staged, u * 8 + 4 * n + 1)
                    nc.gpsimd.tensor_tensor(hi_a, raw, none, ALU.add).then_inc(staged, 1)
                    if n == 1:
                        nc.gpsimd.memset(dst[:, :, :, 3 * DH:3 * DH + 2].bitcast(F32), 0.0)
                    nc.gpsimd.tensor_tensor(hi_b, raw, none, ALU.add).then_inc(staged, 1)
                    pool.wait_ge(staged, u * 8 + 4 * n + 2)
                    nc.gpsimd.tensor_tensor(lo, raw, hi_a.bitcast(F32), ALU.subtract).then_inc(staged, 1)
                if wait:
                    pool.wait_ge(pv1_mm, u * K1 - K1)
                nc.gpsimd.tensor_copy(v_cur[pp][:].rearrange("p t h w -> p t (h w)"),
                                      v1.rearrange("p t b h w -> p t (b h w)")
                                      [:, :, bass.ds(u * (HG * (DH + 1)), HG * (DH + 1))]).then_inc(v_copied, 1)

            pool.wait_ge(consts, N_CONST)
            for i in range(2):
                nc.gpsimd.memset(kstage[i][:, :, :, 3 * DH:3 * DH + 2].bitcast(F32), 1.0).then_inc(consts, 1)
            pool.wait_ge(consts, N_CONST + 2)
            pool.wait_ge(pv_mm, U0 * K0)
            for i in range(2):
                nc.gpsimd.memset(key_stack1[i].bitcast(F32), 0.0).then_inc(keys_zero, 1)
            pool.wait_ge(rope_step, 2 * NCH)
            pool.wait_ge(v_out, NT)
            pool.wait_ge(v_ones, 1)
            for u in range(2):
                stage(u, u, False)
            with pool.Fori(1, U1 // 2) as i:
                for pp in range(2):
                    stage(i * 2 + pp, pp, True)

        @block.scalar
        def _(act):
            def copy(dst, src):
                return nc.scalar.activation(dst, src, ACT.Copy)

            def ln_act(k):
                act.wait_ge(ln_var, k + 1)
                nc.scalar.activation(lnv[:, 1, :], lnv[:, 0, :], ACT.Sqrt).then_inc(ln_root, 1)

            def ln_evacuate(k, c, bank):
                act.wait_ge(ln_turn, k * NCH + c + 1)
                copy(xnT[:, c * CH:(c + 1) * CH], bank).then_inc(ln_xT, 1)

            act.wait_ge(w0_in, 16 * W0_LOADS)
            copy(identr[:], ident[:]).then_inc(identr_ok, 1)
            for g in range(2):
                act.wait_ge(prep_mm, g + 1)
                v = ps_wide[:, g, 0:4 * NZ].rearrange("p (h n) -> p h n", n=NZ)
                copy(zmap[0:DC, 4 * g:4 * g + 4, :], v[0:DC]).then_inc(prep_done, 1)
                copy(zmap[64:65, 4 * g:4 * g + 4, :], v[64:65]).then_inc(prep_done, 1)
            act.wait_ge(prep_mm, 3)
            copy(vo[:], ps_wide[:, 2, 0:2 * D].rearrange("p (g n) -> p g n", g=2)).then_inc(prep_done, 1)
            act.wait_ge(prep_mm, 4)
            copy(vo_bias[:], ps_wide[0:1, 3, 0:D]).then_inc(prep_done, 1)

            ln_act(0)
            for c in range(NCH):
                ln_evacuate(0, c, ps_pair[:, c % 2, :])
                cols = slice(c * CH, (c + 1) * CH)
                act.wait_ge(cq_mm, c + 1)
                nc.scalar.activation(cq[0:3 * DC, cols], ps_ctx[0:3 * DC, :], ACT.Identity,
                                     bias=bdq[:, 0:1]).then_inc(cq_hi, 1)
                act.wait_ge(kv_mm, c + 1)
                nc.scalar.activation(kvr[0:DC + DR, cols], ps_misc[0:DC + DR, :], ACT.Identity,
                                     bias=bkv[:, 0:1]).then_inc(kv_done, 1)

            def z_hi_copy(u, pp, k):
                h, c = k % HP, k // HP
                act.wait_ge(z_mm, u * 4 + (k + 1))
                copy(key_stack[pp][0:NZ, h, c * CH:(c + 1) * CH], ps[0:NZ, TURN0_BANKS[k % 2], :]).then_inc(z_hi, 1)

            def exps0(u, t, first):
                for h in range(HP):
                    act.wait_ge(st_mm, u * (HP * K0) + (HP * t + h + 1))
                    if not (first and t < 4):
                        act.wait_ge(pv_mm, u * K0 + (t - 3))
                    nc.scalar.activation(pt[:, (HP * t + h) % 8, :], ps[:, ST0_BANKS[h], :], ACT.Exp,
                                         scale=SCALE0).then_inc(exp_done, 1)

            def context_T(u, c, first):
                act.wait_ge(pv_mm, u * K0 + (c + 1) * TS)
                if not first:
                    act.wait_ge(ctx_turn, u * 2 + (c - 1))
                copy(cT[:, c, :], ps[:, CTX_BANK, :]).then_inc(ctx_T, 1)

            def unit0(u, pp, first=False, s=True, z=True):
                for t in range(K0):
                    exps0(u, t, first)
                    if s and t in Z0_SECOND:
                        z_hi_copy(u + 1, 1 - pp, 2 + Z0_SECOND.index(t))
                    if t == TS:
                        context_T(u, 0, first)
                    if z and t in Z0_FIRST:
                        z_hi_copy(u + 2, pp, Z0_FIRST.index(t))
                context_T(u, 1, first)

            act.wait_ge(fixed, N_FIXED)
            for k in range(4):
                z_hi_copy(0, 0, k)
            for k in range(2):
                z_hi_copy(1, 1, k)
            unit0(0, 0, first=True)
            unit0(1, 1)
            with act.Fori(1, U0 // 2 - 1) as i:
                unit0(i * 2, 0)
                unit0(i * 2 + 1, 1)
            unit0(U0 - 2, 0, z=False)
            unit0(U0 - 1, 1, s=False, z=False)

            for c in range(NCH):
                act.wait_ge(o_turn, 2 * c + 2)
                if c >= 2:
                    act.wait_ge(o_mm, c - 1)
                copy(pt[:, 4 * (c % 2):4 * (c % 2) + 2, :], ps_wide[:, 2 * (c % 2):2 * (c % 2) + 2, :]).then_inc(o_T, 1)

            ln_act(1)
            for c in range(NCH):
                ln_evacuate(1, c, ps_pair[:, c % 2, :])

            act.wait_ge(gate_step, 1)
            nc.scalar.activation(g8[:, 1], g8[:, 0], ACT.Exp).then_inc(gate_exp, 1)

            def silus(ch):
                for v in range(3 * NE):
                    act.wait_ge(eg_mm, ch * (3 * NE) + (v + 1))
                    m = FM[v % 3]
                    if v >= 2:
                        act.wait_ge(h_done, ch * (3 * NE) + (v - 1))
                    else:
                        act.wait_ge(h_done, ch * (3 * NE))
                    nc.scalar.activation(pt[0:m, 6 + v % 2, :], ps_wide[0:m, v % 2, :], ACT.Silu).then_inc(silu_done, 1)

            silus(0)
            with act.Fori(1, NCH) as ch:
                silus(ch)

            ln_act(2)
            for c in range(NCH):
                ln_evacuate(2, c, ps_pair[:, c % 2, :])
                for t in range(c * TC, (c + 1) * TC):
                    b, i = t // TS, t % TS
                    act.wait_ge(qkv_mm, t + 1)
                    bank = ps_wide[:, t % 4, :]
                    copy(big[:, :, i, b, :], bank[:, 0:2 * D].rearrange("p (k n) -> p k n", k=2)).then_inc(qk_out, 1)
                    copy(v1[:, i, b, :, 0:DH],
                         bank[:, 2 * D:3 * D].rearrange("p (h w) -> p h w", w=DH)).then_inc(v_out, 1)

            def stack(u, pp, n):
                act.wait_ge(stack_turn, u * 4 + (n + 1))
                cols = slice(n // 2 * CH, (n // 2 + 1) * CH)
                if n % 2 == 0:
                    copy(query_stack1[pp][:, cols], ps[:, TURN1_BANK, :]).then_inc(stacked, 1)
                    return
                for r in range(HG):
                    rows = slice(RS * r, RS * (r + 1))
                    ins = copy(key_stack1[pp][rows, r, cols], ps[rows, TURN1_BANK, :])
                ins.then_inc(stacked, 1)

            def max_rows1(u, pp, hf):
                act.wait_ge(m1_turn, u * 2 + (hf + 1))
                copy(query_stack1[pp][:, hf * CH:(hf + 1) * CH], ps[:, TURN1_BANK, :]).then_inc(m1_rows, 1)

            def exps1(u, t, first):
                w = sum(m for _, _, m in ST1[t][1])
                for g in range(2):
                    act.wait_ge(st1_mm, u * (2 * K1) + (2 * t + g + 1))
                    if not (first and t < 2):
                        act.wait_ge(pv1_mm, u * K1 + (t - 1))
                    nc.scalar.activation(pt[:, 4 * (t % 2) + 2 * g:4 * (t % 2) + 2 * g + 2, 0:w],
                                         ps[:, ST1_BANKS[2 * g]:ST1_BANKS[2 * g] + 2, 0:w], ACT.Exp,
                                         scale=SCALE1).then_inc(exp1_done, 1)

            def context1_T(u, c, first):
                act.wait_ge(pv1_mm, u * K1 + (K1_FIRST if c == 0 else K1))
                if not first:
                    act.wait_ge(ctx1_turn, u * 2 + (c - 1))
                copy(cT[:, c, :], ps[:, CTX_BANK, :]).then_inc(ctx1_T, 1)

            def unit1(u, pp, first=False, s=True, t=True):
                for k in range(K1):
                    exps1(u, k, first)
                    if k == K1_FIRST:
                        context1_T(u, 0, first)
                    if s and k in STACK1_SECOND:
                        stack(u + 1, 1 - pp, 2 + STACK1_SECOND.index(k))
                    if t and k in STACK1_FIRST:
                        stack(u + 2, pp, STACK1_FIRST.index(k))
                    if s and k in TURN1_MAX:
                        max_rows1(u + 1, 1 - pp, TURN1_MAX.index(k))
                context1_T(u, 1, first)

            act.wait_ge(keys_zero, 2)
            for n in range(4):
                stack(0, 0, n)
            for hf in range(2):
                max_rows1(0, 0, hf)
            for n in range(2):
                stack(1, 1, n)
            unit1(0, 0, first=True)
            unit1(1, 1)
            with act.Fori(1, U1 // 2 - 1) as i:
                unit1(i * 2, 0)
                unit1(i * 2 + 1, 1)
            unit1(U1 - 2, 0, t=False)
            unit1(U1 - 1, 1, s=False, t=False)

            for c in range(NCH):
                act.wait_ge(o1_turn, c + 1)
                if c >= 2:
                    act.wait_ge(o1_mm, c - 1)
                copy(pt[:, c % 2, :], ps_wide[:, c % 2, :]).then_inc(o1_T, 1)

            ln_act(3)
            for c in range(NCH):
                ln_evacuate(3, c, ps_pair[:, c % 2, :])
            act.wait_ge(sel_in, 16 * 8 * B)
            for c in range(NCH):
                for k in range(2):
                    act.wait_ge(f_mm, 2 * c + k + 1)
                    if c >= 2:
                        act.wait_ge(y_mm, c - 1)
                    nc.scalar.activation(pt[:, 2 * (c % 2) + k, :], ps_wide[:, k, :], ACT.Gelu,
                                         bias=b1[:, c // 2, k:k + 1]).then_inc(gelu_done, 1)

        @block.tensor
        def _(pe):
            mm = nc.tensor.matmul

            def ln_turns(k, c):
                pe.wait_ge(ln_xn, k * NT + (c + 1) * TC)
                if k or c >= 2:
                    pe.wait_ge(ln_xT, k * NCH + c - 1 if c >= 2 else k * NCH)
                for t in range(TC):
                    ins = nc.tensor.transpose(ps_pair[:, c % 2, t * P:(t + 1) * P], xn[:, c * TC + t, :], ident[:])
                ins.then_inc(ln_turn, 1)

            pe.wait_ge(w0_in, 16 * W0_LOADS)
            for h in range(H0):
                g, r = h // 4, h % 4
                ins = mm(ps_wide[0:65, g, r * NZ:(r + 1) * NZ], uk[:, h, :], uq[:, h, :], start=True, stop=True)
                if r == 3:
                    ins.then_inc(prep_mm, 1)
            for h in range(H0):
                g, r = h // 4, h % 4
                ins = mm(ps_wide[32 * r:32 * r + 32, 2, g * D:(g + 1) * D], uv[:, h, 0:DC], wo[:, h, :],
                         start=True, stop=True)
            ins.then_inc(prep_mm, 1)
            pe.wait_ge(fixed, N_FIXED)
            for h in range(H0):
                mm(ps_wide[0:1, 3, 0:D], uv[:, h, DC:DC + 1], wo[:, h, :], start=(h == 0), stop=False)
            mm(ps_wide[0:1, 3, 0:D], ones[0:1, 0:1], bo[:], start=False, stop=True).then_inc(prep_mm, 1)

            for c in range(NCH):
                cols = slice(c * CH, (c + 1) * CH)
                ln_turns(0, c)
                pe.wait_ge(ln_xT, c + 1)
                if c:
                    pe.wait_ge(cq_lo, c)
                mm(ps_ctx[0:3 * DC, :], wdq[:], xnT[:, cols], start=True, stop=True).then_inc(cq_mm, 1)
                if c:
                    pe.wait_ge(kv_done, c)
                mm(ps_misc[0:DC + DR, :], wkv[:], xnT[:, cols], start=True, stop=True).then_inc(kv_mm, 1)
                if c == 0:
                    pe.wait_ge(prep_done, 6)
                for t in range(c * TC, (c + 1) * TC):
                    o = ps_wide[:, 0, t * DC:(t + 1) * DC]
                    mm(o, xnT[:, t * P:(t + 1) * P], wkv[:, 0:DC], start=True, stop=False)
                    ins = mm(o, ones[0:1, :], bkv_row[:], start=False, stop=True)
            ins.then_inc(ckv_mm, 1)

            def make_z(u, k, before):
                h, c = k % HP, k // HP
                if k == 0:
                    pe.wait_ge(zcur_ok, u * HP + HP)
                if before:
                    pe.wait_ge(*before)
                mm(ps[0:NZ, TURN0_BANKS[k % 2], :], zcur[:, h, :], kvr[:, bass.ds((u // UH) * S + c * CH, CH)],
                   start=True, stop=True).then_inc(z_mm, 1)

            def scores_max(u, pp, s, first):
                h, j, c = MX0[s]
                if s == 0:
                    pe.wait_ge(z_lo, u * 4 + 2)
                    pe.wait_ge(cq_copied, u * 2 + 1)
                if s == HP * TC:
                    pe.wait_ge(cq_copied, u * 2 + 2)
                if s == HP * TS:
                    pe.wait_ge(z_lo, u * 4 + 4)
                if not (first and s < 3):
                    pe.wait_ge(max_done, u * len(MX0) + ((s - 2) if s >= 3 else min(s - 1, 0)))
                mm(ps[:, MAX0_BANKS[s % 3], :], query_stack[pp][0:NZ, h, j * P:(j + 1) * P],
                   key_stack[pp][0:NZ, h, c * CH:(c + 1) * CH], start=True, stop=True).then_inc(s_mm, 1)

            def turn_max(u, k, before):
                h, hf = k // 2, k % 2
                if k == 0:
                    pe.wait_ge(m_split, u * 2 + 2)
                if before:
                    pe.wait_ge(*before)
                for t in range(TC):
                    ins = nc.tensor.transpose(ps[0:NZM, TURN0_BANKS[hf], t * P:(t + 1) * P].bitcast(F32R),
                                              mstage[:, h, hf * TC + t, :], identr[:])
                ins.then_inc(m_turn, 1)

            def scores(u, pp, h, t, first):
                c, kt = t // TS, t % TS
                if t == 0 and h == 0:
                    pe.wait_ge(m_rows, u * 4 + 4)
                if not (first and t == 0):
                    pe.wait_ge(exp_done, u * (HP * K0) + (HP * (t - 1) + h + 1))
                mm(ps[:, ST0_BANKS[h], :], key_stack[pp][0:NZM, h, kt * P:(kt + 1) * P],
                   query_stack[pp][0:NZM, h, c * CH:(c + 1) * CH], start=True, stop=True).then_inc(st_mm, 1)

            def values(u, pp, t, first):
                c, kt = t // TS, t % TS
                if t == 0:
                    pe.wait_ge(ckv_copied, u + 1)
                if kt == 0 and not (first and c == 0):
                    pe.wait_ge(ctx_T, u * 2 + c)
                pe.wait_ge(exp_done, u * (HP * K0) + (HP * t + HP))
                for h in range(HP):
                    ins = mm(ps[64 * h:64 * h + DC + 1, CTX_BANK, :], ckv_cur[pp][:, kt, :],
                             pt[:, (HP * t + h) % 8, :], start=(kt == 0), stop=(kt == TS - 1))
                ins.then_inc(pv_mm, 1)

            def turn_context(u, c, before):
                pe.wait_ge(ctx_T, u * 2 + (c + 1))
                if before:
                    pe.wait_ge(*before)
                for t in range(TC):
                    ins = nc.tensor.transpose(ps[:, TURN0_BANKS[1 - c], t * P:(t + 1) * P],
                                              cT[:, c, t * P:(t + 1) * P], ident[:])
                ins.then_inc(ctx_turn, 1)

            def unit0(u, pp, first=False, s=True, z=True):
                def piece(t, n):
                    if s and MX0_STEP * t + n < len(MX0):
                        scores_max(u + 1, 1 - pp, MX0_STEP * t + n, False)

                for t in range(K0):
                    for h in range(HP):
                        scores(u, pp, h, t, first)
                        piece(t, h)
                    if t:
                        values(u, pp, t - 1, first)
                    piece(t, 2)
                    if s and t in Z0_SECOND:
                        k = 2 + Z0_SECOND.index(t)
                        make_z(u + 1, k, (z_lo, u * 4 + (k + 3)))
                    if t == CTX0_BEFORE and not first:
                        turn_context(u - 1, 1, (z_lo, u * 4 + 7) if s else None)
                    if t == CTX0_FIRST:
                        turn_context(u, 0, (z_lo, u * 4 + 8) if s else None)
                    for k in range(4):
                        if s and t == TURN0_MAX[k]:
                            turn_max(u + 1, k, (m_rows, u * 4 + (k + 3)) if k >= 2 else (ctx_out, u * 4 + 2) if k
                                     else None if first else (ctx_out, u * 4))
                    if z and t in Z0_FIRST:
                        k = Z0_FIRST.index(t)
                        make_z(u + 2, k, (m_rows, u * 4 + (k + 7)))
                values(u, pp, K0 - 1, first)

            pe.wait_ge(consts, N_CONST)
            pe.wait_ge(identr_ok, 1)
            pe.wait_ge(cq_lo, NCH)
            pe.wait_ge(kv_done, NCH)
            pe.wait_ge(ckv_done, 1)
            for k in range(4):
                make_z(0, k, (z_lo, k - 1) if k >= 2 else None)
            for n in range(len(MX0)):
                scores_max(0, 0, n, True)
            for k in range(4):
                turn_max(0, k, (m_rows, k - 1) if k >= 2 else None)
            for k in range(2):
                make_z(1, k, (m_rows, k + 3))
            unit0(0, 0, first=True)
            unit0(1, 1)
            with pe.Fori(1, U0 // 2 - 1) as i:
                unit0(i * 2, 0)
                unit0(i * 2 + 1, 1)
            unit0(U0 - 2, 0, z=False)
            unit0(U0 - 1, 1, s=False, z=False)
            turn_context(U0 - 1, 1, (ctx_out, 4 * U0 - 2))

            ctxn = big[:].rearrange("p a t b n -> p (a t b n)").rearrange("p (t b n) -> p t b n", t=TS, b=B)

            def o_turns(c):
                if c == 0:
                    pe.wait_ge(ctx_out, 4 * U0)
                if c >= 2:
                    pe.wait_ge(o_T, c - 1)
                for g in range(2):
                    for t in range(TC):
                        b, i = (c * TC + t) // TS, (c * TC + t) % TS
                        ins = nc.tensor.transpose(ps_wide[:, 2 * (c % 2) + g, t * P:(t + 1) * P],
                                                  ctxn[:, i, b, g * P:(g + 1) * P], ident[:])
                    ins.then_inc(o_turn, 1)

            def o_mms(c):
                pe.wait_ge(o_T, c + 1)
                if c >= 2:
                    pe.wait_ge(o_add, c - 1)
                for t in range(TC):
                    o = ps_pair[:, c % 2, t * P:(t + 1) * P]
                    for g in range(2):
                        mm(o, pt[:, 4 * (c % 2) + g, t * P:(t + 1) * P], vo[:, g, :], start=(g == 0), stop=False)
                    ins = mm(o, ones[0:1, :], vo_bias[:], start=False, stop=True)
                ins.then_inc(o_mm, 1)

            for c in range(NCH + 1):
                if c < NCH:
                    o_turns(c)
                if c:
                    o_mms(c - 1)

            pe.wait_ge(o_add, NCH)
            for c in range(NCH):
                ln_turns(1, c)
            for c in range(NCH):
                pe.wait_ge(ln_xT, NCH + c + 1)
                for t in range(c * TC, (c + 1) * TC):
                    ins = mm(ps_ctx[:, t * E0:(t + 1) * E0], xnT[:, t * P:(t + 1) * P], gw[:], start=True, stop=True)
            ins.then_inc(gate_mm, 1)
            pe.wait_ge(wm_in, 16)

            def gate_up(ch, e):
                for f in range(3):
                    v, m = 3 * e + f, FM[f]
                    pe.wait_ge(h_done, ch * (3 * NE) + max(v - 1, 0))
                    rhs = xnT[:, bass.ds(ch * CH, CH)]
                    for bank, w0, done in ((v % 2, 0, eg_mm), (2 + v % 2, F0, eu_mm)):
                        mm(ps_wide[0:m, bank, :], wm[:, e, w0 + f * P:w0 + f * P + m], rhs,
                           start=True, stop=True).then_inc(done, 1)

            def down(ch, e):
                pe.wait_ge(h_done, ch * (3 * NE) + (3 * e + 3))
                pe.wait_ge(moe_add, ch * (TC * NE) + TC * max(e - 1, 0))
                for t in range(TC):
                    for f in range(3):
                        m = FM[f]
                        ins = mm(ps_pair[:, e % 2, t * P:(t + 1) * P], pt[0:m, 3 * (e % 2) + f, t * P:(t + 1) * P],
                                 wm[0:m, e, 2 * F0 + f * D:2 * F0 + (f + 1) * D], start=(f == 0), stop=(f == 2))
                ins.then_inc(ed_mm, 1)

            def experts(ch):
                gate_up(ch, 0)
                for e in range(NE):
                    if e + 1 < NE:
                        gate_up(ch, e + 1)
                    down(ch, e)

            experts(0)
            with pe.Fori(1, NCH) as ch:
                experts(ch)

            pe.wait_ge(moe_add, NCH * TC * NE)
            pe.wait_ge(w1_in, 16 * W1_LOADS)
            for c in range(NCH):
                ln_turns(2, c)
                pe.wait_ge(ln_xT, 2 * NCH + c + 1)
                for t in range(c * TC, (c + 1) * TC):
                    if t >= 4:
                        pe.wait_ge(v_out, t - 3)
                    mm(ps_wide[:, t % 4, 0:3 * D], xnT[:, t * P:(t + 1) * P], wqkv[:],
                       start=True, stop=True).then_inc(qkv_mm, 1)

            def turn_stack(u, pp, n, before):
                hf, src = n // 2, (qstage, kstage)[n % 2][pp]
                if n == 0:
                    pe.wait_ge(staged, u * 8 + 8)
                pe.wait_ge(*before)
                for t in range(TC):
                    ins = nc.tensor.transpose(ps[:, TURN1_BANK, t * P:(t + 1) * P].bitcast(F32R),
                                              src[:, hf * TC + t].rearrange("p h w -> p (h w)"), identr[:])
                ins.then_inc(stack_turn, 1)

            def scores_max1(u, pp, s, first):
                r, c, parts = MX1[s]
                if s == 0:
                    pe.wait_ge(stacked, u * 4 + 2)
                if s == MX1_Q_HALF:
                    pe.wait_ge(stacked, u * 4 + 3)
                if s == MX1_K_HALF:
                    pe.wait_ge(stacked, u * 4 + 4)
                if not (first and s < 2):
                    pe.wait_ge(max1_done, u * NMX1 + (MX1_END[s - 2] if s >= 2 else s - 1))
                bank = ps[:, MAX1_BANKS[s % 2], :]
                ins = None
                for i, o, w in parts:
                    diag = c == i // TC
                    ins = mm(bank[:, o:o + w], query_stack1[pp][:, i * P:(i + 1) * P],
                             key_stack1[pp][:, r, c * CH:c * CH + w], start=(o == 0), stop=not diag)
                if diag:
                    for i, o, w in parts:
                        ins = mm(bank[:, o + w - P:o + w], identb[:], mask_qk[:], start=False,
                                 stop=(o == parts[-1][1]))
                ins.then_inc(s1_mm, 1)

            def turn_max1(u, pp, hf, before):
                if hf == 0:
                    pe.wait_ge(m1_split, u * 2 + 2)
                pe.wait_ge(*before)
                for t in range(TC):
                    ins = nc.tensor.transpose(ps[:, TURN1_BANK, t * P:(t + 1) * P].bitcast(F32R),
                                              qstage[pp][:, hf * TC + t].rearrange("p h w -> p (h w)"), identr[:])
                ins.then_inc(m1_turn, 1)

            def scores1(u, pp, r, t, first):
                c, parts = ST1[t]
                if t == 0 and r == 0:
                    pe.wait_ge(m1_rows, u * 2 + 2)
                if r % 2 == 0 and not (first and t == 0):
                    pe.wait_ge(exp1_done, u * (2 * K1) + (2 * (t - 1) + r // 2 + 1))
                for j, o, w in parts:
                    diag = j >= c * TC
                    q0 = (c + 1) * CH - w
                    ins = mm(ps[:, ST1_BANKS[r], o:o + w], key_stack1[pp][:, r, j * P:(j + 1) * P],
                             query_stack1[pp][:, q0:q0 + w], start=(o == 0), stop=not diag)
                if not diag and r % 2:
                    ins.then_inc(st1_mm, 1)

            def masks1(t):
                c, parts = ST1[t]
                if parts[0][0] < c * TC:
                    return
                for r in range(HG):
                    for j, o, w in parts:
                        ins = mm(ps[:, ST1_BANKS[r], o:o + P], identb[:], mask_kq[:], start=False,
                                 stop=(o == parts[-1][1]))
                    if r % 2:
                        ins.then_inc(st1_mm, 1)

            def values1(u, pp, t, first):
                c, parts = ST1[t]
                if t == 0:
                    pe.wait_ge(v_copied, u + 1)
                if parts[0][0] == 0 and not (first and c == 0):
                    pe.wait_ge(ctx1_T, u * 2 + c)
                pe.wait_ge(exp1_done, u * (2 * K1) + (2 * t + 2))
                for j, o, w in parts:
                    for r in range(HG):
                        ins = mm(ps[RS * r:RS * r + DH + 1, CTX_BANK, CH - w:CH], v_cur[pp][:, j, r, :],
                                 pt[:, 4 * (t % 2) + r, o:o + w], start=(j == 0), stop=(j == c * TC + 2))
                ins.then_inc(pv1_mm, 1)

            def turn_context1(u, c, before):
                pe.wait_ge(ctx1_T, u * 2 + (c + 1))
                pe.wait_ge(*before)
                for t in range(TC):
                    ins = nc.tensor.transpose(ps[:, TURN1_BANK, t * P:(t + 1) * P],
                                              cT[:, c, t * P:(t + 1) * P], ident[:])
                ins.then_inc(ctx1_turn, 1)

            def unit1(u, pp, first=False, s=True, t=True):
                def piece(k, n):
                    if s and MX1_STEP * k + n < len(MX1):
                        scores_max1(u + 1, 1 - pp, MX1_STEP * k + n, False)

                for k in range(K1):
                    scores1(u, pp, 0, k, first)
                    scores1(u, pp, 1, k, first)
                    piece(k, 0)
                    scores1(u, pp, 2, k, first)
                    scores1(u, pp, 3, k, first)
                    piece(k, 1)
                    masks1(k)
                    piece(k, 2)
                    if k:
                        values1(u, pp, k - 1, first)
                    piece(k, 3)
                    piece(k, 4)
                    if s and k in STACK1_SECOND:
                        n = 2 + STACK1_SECOND.index(k)
                        turn_stack(u + 1, 1 - pp, n, (stacked, u * 4 + (n + 4)))
                    if k == CTX1_BEFORE and not first:
                        turn_context1(u - 1, 1, (stacked, u * 4 + 8) if s else (m1_rows, u * 2 + 2))
                    if k == CTX1_FIRST:
                        turn_context1(u, 0, (stacked, u * 4 + 8) if first else (ctx1_out, u * 4))
                    if t and k in STACK1_FIRST:
                        n = STACK1_FIRST.index(k)
                        turn_stack(u + 2, pp, n, (stacked, u * 4 + 9) if n else (ctx1_out, u * 4 + 2))
                    if s and k in TURN1_MAX:
                        hf = TURN1_MAX.index(k)
                        turn_max1(u + 1, 1 - pp, hf, (m1_rows, u * 2 + 3) if hf else
                                  (stacked, u * 4 + 10) if t else (ctx1_out, u * 4 + 2))
                values1(u, pp, K1 - 1, first)

            for n in range(4):
                turn_stack(0, 0, n, (stacked, n))
            for n in range(len(MX1)):
                scores_max1(0, 0, n, True)
            turn_max1(0, 0, 0, (stacked, 4))
            turn_max1(0, 0, 1, (m1_rows, 1))
            turn_stack(1, 1, 0, (m1_rows, 2))
            turn_stack(1, 1, 1, (stacked, 5))
            unit1(0, 0, first=True)
            unit1(1, 1)
            with pe.Fori(1, U1 // 2 - 1) as i:
                unit1(i * 2, 0)
                unit1(i * 2 + 1, 1)
            unit1(U1 - 2, 0, t=False)
            unit1(U1 - 1, 1, s=False, t=False)
            turn_context1(U1 - 1, 1, (ctx1_out, 4 * U1 - 2))

            def o1_turns(c):
                if c == 0:
                    pe.wait_ge(ctx1_out, 4 * U1)
                if c >= 2:
                    pe.wait_ge(o1_T, c - 1)
                for t in range(TC):
                    b, i = (c * TC + t) // TS, (c * TC + t) % TS
                    ins = nc.tensor.transpose(ps_wide[:, c % 2, t * P:(t + 1) * P], ao[:, i, b, :], ident[:])
                ins.then_inc(o1_turn, 1)

            def o1_mms(c):
                pe.wait_ge(o1_T, c + 1)
                if c >= 2:
                    pe.wait_ge(o1_add, c - 1)
                for t in range(TC):
                    ins = mm(ps_pair[:, c % 2, t * P:(t + 1) * P], pt[:, c % 2, t * P:(t + 1) * P], wout[:],
                             start=True, stop=True)
                ins.then_inc(o1_mm, 1)

            for c in range(NCH + 1):
                if c < NCH:
                    o1_turns(c)
                if c:
                    o1_mms(c - 1)

            pe.wait_ge(o1_add, NCH)
            for c in range(NCH):
                ln_turns(3, c)
            for b in range(B):
                pe.wait_ge(ln_xT, 3 * NCH + b * (NCH // B) + 1)
                o = ps_ctx[0:1, b * E1:(b + 1) * E1]
                mm(o, xnT[:, b * S:b * S + 1], wr[:], start=True, stop=False)
                ins = mm(o, ones[0:1, 0:1], br[:], start=False, stop=True)
            ins.then_inc(rt_mm, 1)
            pe.wait_ge(ln_xT, 4 * NCH)
            pe.wait_ge(sel_in, 16 * 8 * B)

            def f_mms(c):
                for k in range(2):
                    if c:
                        pe.wait_ge(gelu_done, 2 * c - 1 + k)
                    mm(ps_wide[:, k, :], w1[:, c // 2, k, :], xnT[:, c * CH:(c + 1) * CH],
                       start=True, stop=True).then_inc(f_mm, 1)

            def y_mms(c):
                pe.wait_ge(gelu_done, 2 * c + 2)
                if c >= 2:
                    pe.wait_ge(y_add, c - 1)
                for t in range(TC):
                    o = ps_pair[:, c % 2, t * P:(t + 1) * P]
                    for k in range(2):
                        mm(o, pt[:, 2 * (c % 2) + k, t * P:(t + 1) * P], w2[:, c // 2, k, :], start=(k == 0), stop=False)
                    ins = mm(o, ones[0:2, :], b2[:, c // 2, :], start=False, stop=True)
                ins.then_inc(y_mm, 1)

            for c in range(NCH + 1):
                if c < NCH:
                    f_mms(c)
                if c:
                    y_mms(c - 1)

        @block.vector
        def _(dve):
            v = nc.vector

            def layer_norm(k, ready):
                for t in range(NT):
                    ready(t)
                    v.bn_stats(stats[:, t, :], x[:, t, :]).then_inc(ln_stats, 1)
                for t in range(NT):
                    dve.wait_ge(ln_stats, k * NT + t + 1)
                    v.bn_aggr(mv[:, t, :], stats[:, t, :]).then_inc(ln_aggr, 1)
                dve.wait_ge(ln_aggr, (k + 1) * NT)
                v.tensor_scalar(lnv[:, 0, :], mv[:, :, 1], EPS, None, ALU.add).then_inc(ln_var, 1)
                dve.wait_ge(ln_root, k + 1)
                s = 5 * k
                v.reciprocal(lnv[:, 2, :], lnv[:, 1, :]).then_inc(ln_step, 1)
                dve.wait_ge(ln_step, s + 1)
                v.tensor_tensor(lnv[:, 3, :], lnv[:, 2, :], lnv[:, 2, :], ALU.mult).then_inc(ln_step, 1)
                dve.wait_ge(ln_step, s + 2)
                v.tensor_tensor(lnv[:, 1, :], lnv[:, 3, :], lnv[:, 0, :], ALU.mult).then_inc(ln_step, 1)
                dve.wait_ge(ln_step, s + 3)
                v.tensor_scalar(lnv[:, 3, :], lnv[:, 1, :], -0.5, 1.5, ALU.mult, ALU.add).then_inc(ln_step, 1)
                dve.wait_ge(ln_step, s + 4)
                v.tensor_tensor(lnv[:, 4, :], lnv[:, 2, :], lnv[:, 3, :], ALU.mult).then_inc(ln_step, 1)
                dve.wait_ge(ln_step, s + 5)
                for t in range(NT):
                    v.tensor_scalar(xn[:, t, :], x[:, t, :], mv[:, t, 0:1], lnv[:, 4, t:t + 1],
                                    ALU.subtract, ALU.mult).then_inc(ln_xn, 1)

            v.memset(ones[:], 1.0).then_inc(fixed, 1)
            v.memset(ps[:, CTX_BANK, :], 0.0).then_inc(fixed, 1)
            for i in range(2):
                v.memset(key_stack[i][96:NZM].bitcast(F32), 1.0).then_inc(fixed, 1)
                v.memset(query_stack[i][96:NZ].bitcast(F32), 1.0).then_inc(fixed, 1)
            v.memset(kvr[64:65, :], 1.0).then_inc(fixed, 1)
            v.memset(mstage[:, :, :, 0:3 * DC].bitcast(F32), 0.0).then_inc(fixed, 1)
            v.memset(mstage[:, :, :, 3 * DC:NZ].bitcast(F32), 1.0).then_inc(fixed, 1)

            layer_norm(0, lambda t: dve.wait_ge(x_in[t // TC], 16))
            dve.wait_ge(w0_in, 16 * W0_LOADS)
            for c in range(NCH):
                cols = slice(c * CH, (c + 1) * CH)
                dve.wait_ge(cq_hi, c + 1)
                v.scalar_tensor_tensor(out=cq[DC:2 * DC, cols], in0=ps_ctx[DC:2 * DC, :], scalar=bdq[DC:2 * DC, 0:1],
                                       in1=cq[DC:2 * DC, cols].bitcast(F32), op0=ALU.add,
                                       op1=ALU.subtract).then_inc(cq_lo, 1)
            dve.wait_ge(ckv_mm, 1)
            v.tensor_copy(ckv[:, :, :, 0:DC],
                          ps_wide[:, 0, :].rearrange("p (b t n) -> p t b n", b=B, n=DC)).then_inc(ckv_done, 1)

            def z_lo_part(u, pp, k):
                h, c = k % HP, k // HP
                cols = slice(c * CH, (c + 1) * CH)
                dve.wait_ge(z_hi, u * 4 + (k + 1))
                rows = slice(2 * DC, 3 * DC + 1)
                v.tensor_tensor(key_stack[pp][rows, h, cols], ps[rows, TURN0_BANKS[k % 2], :],
                                key_stack[pp][rows, h, cols].bitcast(F32), ALU.subtract).then_inc(z_lo, 1)

            def copy_cq(u, pp, hf, wait):
                if wait:
                    dve.wait_ge(st_mm, u * (HP * K0) + (HP * TS * (hf + 1) - 2 * HP * K0))
                src = cq[0:3 * DC, bass.ds((u // UH) * S + hf * CH, CH)]
                v.tensor_copy(query_stack[pp][0:3 * DC, :, hf * CH:(hf + 1) * CH],
                              src.unsqueeze(1).broadcast_to([3 * DC, HP, CH])).then_inc(cq_copied, 1)

            def maximum(u, pp, s):
                h, j, c = MX0[s]
                dve.wait_ge(s_mm, u * len(MX0) + (s + 1))
                v.tensor_reduce(mx_part[pp][:, s:s + 1], ps[:, MAX0_BANKS[s % 3], :], AX_X, ALU.max).then_inc(max_done, 1)

            def split_max(u, pp, first):
                dve.wait_ge(max_done, u * len(MX0) + len(MX0))
                n = HP * TS
                v.tensor_tensor(mx[pp][:, 0:n], mx_part[pp][:, 0:n], mx_part[pp][:, n:2 * n],
                                ALU.max).then_inc(mx_ok, 1)
                dve.wait_ge(mx_ok, u + 1)
                m = mx[pp][:, 0:n].rearrange("p (t h) -> p h t", h=HP)
                if not first:
                    dve.wait_ge(m_turn, u * 4)
                v.tensor_scalar(mstage[:, :, :, NZ], m, -1.0, None, ALU.mult).then_inc(m_split, 1)
                dve.wait_ge(m_split, u * 2 + 1)
                v.scalar_tensor_tensor(out=mstage[:, :, :, NZ + 1], in0=m, scalar=-1.0,
                                       in1=mstage[:, :, :, NZ].bitcast(F32), op0=ALU.mult,
                                       op1=ALU.subtract).then_inc(m_split, 1)

            def max_rows(u, pp, h, hf):
                dve.wait_ge(m_turn, u * 4 + (2 * h + hf + 1))
                v.tensor_copy(query_stack[pp][96:NZM, h, hf * CH:(hf + 1) * CH],
                              ps[96:NZM, TURN0_BANKS[hf], :]).then_inc(m_rows, 1)

            ctxn = big[:].rearrange("p a t b n -> p (a t b n)").rearrange("p (t n) -> p t n", t=TS)

            def contexts_out(u, c, first=False):
                dve.wait_ge(ctx_turn, u * 2 + (c + 1))
                a = ps[:, TURN0_BANKS[1 - c], :].rearrange("p (t h n) -> p t h n", t=TC, h=HP)
                r = rden[:, 0:TC * HP].rearrange("p (t h) -> p t h", h=HP)
                if not first:
                    dve.wait_ge(ctx_out, u * 4 + 2 * c)
                v.reciprocal(r, a[:, :, :, DC]).then_inc(ctx_out, 1)
                dve.wait_ge(ctx_out, u * 4 + (2 * c + 1))
                dst = ctxn[:, c * TC:(c + 1) * TC, bass.ds(u * (HP * DC), HP * DC)].rearrange("p t (h n) -> p t h n", h=HP)
                v.tensor_tensor(dst, a[:, :, :, 0:DC], r.unsqueeze(3).broadcast_to([P, TC, HP, DC]),
                                ALU.mult).then_inc(ctx_out, 1)

            def unit0(u, pp, first=False, s=True, z=True):
                for n in range(len(MX0)):
                    if s and n == 1:
                        copy_cq(u + 1, 1 - pp, 1, not first)
                    for k in range(2):
                        if s and n == MX0_STEP * (Z0_SECOND[k] + 1):
                            z_lo_part(u + 1, 1 - pp, 2 + k)
                    if n == MX0_STEP * (CTX0_BEFORE + 1) and not first:
                        contexts_out(u - 1, 1)
                    if s:
                        maximum(u + 1, 1 - pp, n)
                if s:
                    split_max(u + 1, 1 - pp, False)
                contexts_out(u, 0, first)
                if s:
                    for h in range(HP):
                        for hf in range(2):
                            max_rows(u + 1, 1 - pp, h, hf)
                if z:
                    copy_cq(u + 2, pp, 0, True)
                    for k in range(2):
                        z_lo_part(u + 2, pp, k)

            copy_cq(0, 0, 0, False)
            copy_cq(0, 0, 1, False)
            copy_cq(1, 1, 0, False)
            for k in range(4):
                z_lo_part(0, 0, k)
            for n in range(len(MX0)):
                maximum(0, 0, n)
            split_max(0, 0, True)
            for h in range(HP):
                for hf in range(2):
                    max_rows(0, 0, h, hf)
            for k in range(2):
                z_lo_part(1, 1, k)
            unit0(0, 0, first=True)
            unit0(1, 1)
            with dve.Fori(1, U0 // 2 - 1) as i:
                unit0(i * 2, 0)
                unit0(i * 2 + 1, 1)
            unit0(U0 - 2, 0, z=False)
            unit0(U0 - 1, 1, s=False, z=False)
            contexts_out(U0 - 1, 1)

            for c in range(NCH):
                dve.wait_ge(o_mm, c + 1)
                xc = x[:, c * TC:(c + 1) * TC, :].rearrange("p t n -> p (t n)")
                v.tensor_tensor(xc, ps_pair[:, c % 2, :], xc, ALU.add).then_inc(o_add, 1)
            layer_norm(1, lambda t: dve.wait_ge(o_add, t // TC + 1))
            gs = Steps(gate_step)
            dve.wait_ge(gate_mm, 1)
            logits = ps_ctx[:, 0:NT * E0].rearrange("p (t e) -> p t e", e=E0)
            top = g1[:, 0, :]

            def over_e(a):
                return a.unsqueeze(2).broadcast_to([P, NT, E0])

            v.tensor_reduce(top, logits, AX_X, ALU.max).then_inc(comb_ok, 1)
            dve.wait_ge(comb_ok, 1)
            gs.mark(v.tensor_tensor(g8[:, 0], logits, over_e(top), ALU.subtract))
            dve.wait_ge(gate_exp, 1)
            n = gs.mark(v.tensor_reduce(g1[:, 1, :], g8[:, 1], AX_X, ALU.add))
            dve.wait_ge(gate_step, n)
            n = gs.mark(v.reciprocal(g1[:, 2, :], g1[:, 1, :]))
            dve.wait_ge(gate_step, n)
            n = gs.mark(v.tensor_tensor(g8[:, 2], g8[:, 1], over_e(g1[:, 2, :]), ALU.mult))
            dve.wait_ge(gate_step, n)
            p_e = g8[:, 2].unsqueeze(3).broadcast_to([P, NT, E0, E0])
            p_j = g8[:, 2].unsqueeze(2).broadcast_to([P, NT, E0, E0])
            gs.mark(v.tensor_tensor(g64[:, 0], p_j, p_e, ALU.is_gt))
            n = gs.mark(v.tensor_tensor(g64[:, 1], p_j, p_e, ALU.is_equal))
            dve.wait_ge(gate_step, n)
            n = gs.mark(v.tensor_tensor(g64[:, 1], g64[:, 1], tri[:].unsqueeze(1).broadcast_to([P, NT, E0, E0]),
                                        ALU.mult))
            dve.wait_ge(gate_step, n)
            n = gs.mark(v.tensor_tensor(g64[:, 0], g64[:, 0], g64[:, 1], ALU.add))
            dve.wait_ge(gate_step, n)
            n = gs.mark(v.tensor_reduce(g8[:, 3], g64[:, 0], AX_X, ALU.add))
            dve.wait_ge(gate_step, n)
            n = gs.mark(v.scalar_tensor_tensor(out=g8[:, 0], in0=g8[:, 3], scalar=1.5, in1=g8[:, 2],
                                               op0=ALU.is_lt, op1=ALU.mult))
            dve.wait_ge(gate_step, n)
            n = gs.mark(v.tensor_reduce(g1[:, 1, :], g8[:, 0], AX_X, ALU.add))
            dve.wait_ge(gate_step, n)
            n = gs.mark(v.tensor_scalar(g1[:, 2, :], g1[:, 1, :], 1e-20, None, ALU.add))
            dve.wait_ge(gate_step, n)
            n = gs.mark(v.reciprocal(g1[:, 3, :], g1[:, 2, :]))
            dve.wait_ge(gate_step, n)
            dve.wait_ge(consts, N_CONST)
            v.tensor_tensor(comb[:, :, 0:E0], g8[:, 0], over_e(g1[:, 3, :]), ALU.mult).then_inc(comb_ok, 1)
            dve.wait_ge(comb_ok, 2)

            def hidden(ch, e):
                for f in range(3):
                    n, m = 3 * e + f, FM[f]
                    dve.wait_ge(silu_done, ch * (3 * NE) + (n + 1))
                    dve.wait_ge(eu_mm, ch * (3 * NE) + (n + 1))
                    if f == 0:
                        dve.wait_ge(ed_mm, ch * NE + max(e - 1, 0))
                    v.tensor_tensor(pt[0:m, 3 * (e % 2) + f, :], ps_wide[0:m, 2 + n % 2, :], pt[0:m, 6 + n % 2, :],
                                    ALU.mult).then_inc(h_done, 1)

            def accumulate(ch, e):
                dve.wait_ge(ed_mm, ch * NE + (e + 1))
                for t in range(TC):
                    dve.wait_ge(moe_add, ch * (TC * NE) + max(TC * (e - 1) + t + 1, 0))
                    xt = x[:, bass.ds(ch * TC + t, 1), :].rearrange("p o n -> p (o n)")
                    w = comb[:, bass.ds(ch * TC + t, 1), e:e + 1].rearrange("p o n -> p (o n)")
                    v.scalar_tensor_tensor(out=xt, in0=ps_pair[:, e % 2, t * P:(t + 1) * P], scalar=w, in1=xt,
                                           op0=ALU.mult, op1=ALU.add).then_inc(moe_add, 1)

            def experts(ch):
                hidden(ch, 0)
                for e in range(NE):
                    if e + 1 < NE:
                        hidden(ch, e + 1)
                    accumulate(ch, e)

            experts(0)
            with dve.Fori(1, NCH) as ch:
                experts(ch)

            dve.wait_ge(moe_add, NCH * TC * NE)
            layer_norm(2, lambda t: None)
            dve.wait_ge(w1_in, 16 * W1_LOADS)
            for c in range(NCH):
                b, i0 = c * TC // TS, c * TC % TS
                dve.wait_ge(qk_out, (c + 1) * TC)
                qk = [big[:, a, i0:i0 + TC, b, :].rearrange("p t (h w) -> p t h w", w=DH) for a in range(2)]
                ta = [pt[:, a, :].rearrange("p (t h w) -> p t h w", t=TC, w=DH) for a in range(2)]
                tb = [pt[:, 2 + a, :].rearrange("p (t h w) -> p t h w", t=TC, w=DH) for a in range(2)]
                h = DH // 2

                def over_heads(tab, lo, hi):
                    return tab[:, i0:i0 + TC, lo:hi].unsqueeze(2).broadcast_to([P, TC, H1, hi - lo])

                if c:
                    dve.wait_ge(rope_step, 2 * c)
                for a in range(2):
                    v.tensor_tensor(ta[a], qk[a], over_heads(cos, 0, DH), ALU.mult).then_inc(rope_mul, 1)
                    v.tensor_tensor(tb[a][:, :, :, 0:h], qk[a][:, :, :, h:DH], over_heads(sin, 0, h), ALU.mult).then_inc(rope_mul, 1)
                    v.tensor_tensor(tb[a][:, :, :, h:DH], qk[a][:, :, :, 0:h], over_heads(sin, h, DH), ALU.mult).then_inc(rope_mul, 1)
                dve.wait_ge(rope_mul, 6 * (c + 1))
                for a in range(2):
                    v.tensor_tensor(qk[a], ta[a], tb[a], ALU.add).then_inc(rope_step, 1)

            def maximum1(u, pp, s):
                r, c, parts = MX1[s]
                dve.wait_ge(s1_mm, u * len(MX1) + (s + 1))
                for i, o, w in parts:
                    n = TS * r + (i if i < TC else 2 * (i - TC) + c)
                    dst = (mx if i < TC else mx_part)[pp][:, n:n + 1]
                    v.tensor_reduce(dst, ps[:, MAX1_BANKS[s % 2], o:o + w], AX_X, ALU.max).then_inc(max1_done, 1)

            def split_max1(u, pp):
                dve.wait_ge(max1_done, u * NMX1 + NMX1)
                part = mx_part[pp][:].rearrange("p (r t c) -> p r t c", r=HG, c=2)
                v.tensor_tensor(mx[pp][:].rearrange("p (r t) -> p r t", r=HG)[:, :, TC:TS], part[:, :, :, 0],
                                part[:, :, :, 1], ALU.max).then_inc(mx1_ok, 1)
                dve.wait_ge(mx1_ok, u + 1)
                m = mx[pp][:].rearrange("p (r t) -> p t r", r=HG)
                hi, lo = (qstage[pp][:, :, :, 3 * DH + n] for n in range(2))
                v.tensor_scalar(hi, m, -1.0, None, ALU.mult).then_inc(m1_split, 1)
                dve.wait_ge(m1_split, u * 2 + 1)
                v.scalar_tensor_tensor(out=lo, in0=m, scalar=-1.0, in1=hi.bitcast(F32), op0=ALU.mult,
                                       op1=ALU.subtract).then_inc(m1_split, 1)

            def contexts_out1(u, c):
                dve.wait_ge(ctx1_turn, u * 2 + (c + 1))
                a = ps[:, TURN1_BANK, :].rearrange("p (t r n) -> p t r n", t=TC, r=HG)
                r = rden[:].rearrange("p (t r) -> p t r", r=HG)
                v.reciprocal(r, a[:, :, :, DH]).then_inc(ctx1_out, 1)
                dve.wait_ge(ctx1_out, u * 4 + (2 * c + 1))
                dst = ao.rearrange("p t b n -> p t (b n)")[:, c * TC:(c + 1) * TC, bass.ds(u * (HG * DH), HG * DH)] \
                    .rearrange("p t (r w) -> p t r w", w=DH)
                v.tensor_tensor(dst, a[:, :, :, 0:DH], r.unsqueeze(3).broadcast_to([P, TC, HG, DH]),
                                ALU.mult).then_inc(ctx1_out, 1)

            def unit1(u, pp, first=False, s=True):
                for n in range(len(MX1)):
                    if n == MX1_STEP * (CTX1_BEFORE + 1) and not first:
                        contexts_out1(u - 1, 1)
                    if n == MX1_STEP * (CTX1_FIRST + 1):
                        contexts_out1(u, 0)
                    if s:
                        maximum1(u + 1, 1 - pp, n)
                if s:
                    split_max1(u + 1, 1 - pp)

            for n in range(len(MX1)):
                maximum1(0, 0, n)
            split_max1(0, 0)
            unit1(0, 0, first=True)
            unit1(1, 1)
            with dve.Fori(1, U1 // 2 - 1) as i:
                unit1(i * 2, 0)
                unit1(i * 2 + 1, 1)
            unit1(U1 - 2, 0)
            unit1(U1 - 1, 1, s=False)
            contexts_out1(U1 - 1, 1)

            for c in range(NCH):
                dve.wait_ge(o1_mm, c + 1)
                xc = x[:, c * TC:(c + 1) * TC, :].rearrange("p t n -> p (t n)")
                v.tensor_tensor(xc, ps_pair[:, c % 2, :], xc, ALU.add).then_inc(o1_add, 1)
            layer_norm(3, lambda t: dve.wait_ge(o1_add, t // TC + 1))

            rs = Steps(rt_step)
            dve.wait_ge(rt_mm, 1)
            n = rs.mark(v.tensor_copy(rt[:, 0], ps_ctx[0:1, 0:B * E1].rearrange("p (b e) -> p b e", b=B)))
            dve.wait_ge(rt_step, n)
            s_e = rt[:, 0].unsqueeze(3).broadcast_to([1, B, E1, E1])
            s_j = rt[:, 0].unsqueeze(2).broadcast_to([1, B, E1, E1])
            rs.mark(v.tensor_tensor(rt64[:, 0], s_j, s_e, ALU.is_gt))
            n = rs.mark(v.tensor_tensor(rt64[:, 1], s_j, s_e, ALU.is_equal))
            dve.wait_ge(rt_step, n)
            n = rs.mark(v.tensor_tensor(rt64[:, 1], rt64[:, 1], tri[0:1].unsqueeze(1).broadcast_to([1, B, E1, E1]),
                                        ALU.mult))
            dve.wait_ge(rt_step, n)
            n = rs.mark(v.tensor_tensor(rt64[:, 0], rt64[:, 0], rt64[:, 1], ALU.add))
            dve.wait_ge(rt_step, n)
            n = rs.mark(v.tensor_reduce(rt[:, 1], rt64[:, 0], AX_X, ALU.add))
            dve.wait_ge(rt_step, n)
            for k in range(2):
                n = rs.mark(v.scalar_tensor_tensor(out=rt[:, 2 + k], in0=rt[:, 1], scalar=float(k),
                                                   in1=ecount[:].unsqueeze(1).broadcast_to([1, B, E1]),
                                                   op0=ALU.is_equal, op1=ALU.mult))
            dve.wait_ge(rt_step, n)
            for k in range(2):
                n = rs.mark(v.tensor_reduce(idx_f[:, :, k], rt[:, 2 + k], AX_X, ALU.add))
            dve.wait_ge(rt_step, n)
            v.tensor_copy(idx_i[:], idx_f[:]).then_inc(idx_ok, 1)

            for c in range(NCH):
                dve.wait_ge(y_mm, c + 1)
                xc = x[:, c * TC:(c + 1) * TC, :].rearrange("p t n -> p (t n)")
                v.scalar_tensor_tensor(out=xc, in0=ps_pair[:, c % 2, :], scalar=0.5, in1=xc,
                                       op0=ALU.mult, op1=ALU.add).then_inc(y_add, 1)


def lay_out(i):
    a = {k: np.asarray(v) for k, v in i.items()}
    f = np.float32

    def heads(w, b, n):
        return (w.reshape(w.shape[0], H0, n).transpose(2, 1, 0), b.reshape(1, H0, n).transpose(2, 1, 0))

    uq, ubq = heads(a["L0_attn_W_UQ"], a["L0_attn_b_UQ"], DK)
    qr, qrb = heads(a["L0_attn_W_QR"], a["L0_attn_b_QR"], DR)
    uk, ukb = heads(a["L0_attn_W_UK"], a["L0_attn_b_UK"], DK)
    uv, uvb = heads(a["L0_attn_W_UV"], a["L0_attn_b_UV"], DK)
    up = np.concatenate([a["L0_ffn_expert_gate"], a["L0_ffn_shared_gate"][None]], 0)
    uu = np.concatenate([a["L0_ffn_expert_up"], a["L0_ffn_shared_up"][None]], 0)
    dn = np.concatenate([a["L0_ffn_expert_down"], a["L0_ffn_shared_down"][None]], 0).transpose(0, 2, 1)
    dnp = np.zeros((NE, 3 * P, D), f)
    dnp[:, :F0] = dn
    dnp = dnp.reshape(NE, 3, P, D).transpose(2, 0, 1, 3).reshape(P, NE, 3 * D)
    wm = np.concatenate([up.transpose(2, 0, 1), uu.transpose(2, 0, 1), dnp], 2)

    inv = (f(1.0) / f(10000.0) ** (np.arange(0, DH, 2, dtype=f) / f(DH))).astype(f)
    fr = np.arange(S, dtype=f)[:, None] * inv[None, :]
    c, s = np.cos(fr).astype(f), np.sin(fr).astype(f)
    cos = np.concatenate([c, c], 1).reshape(TS, P, DH).transpose(1, 0, 2)
    sin = np.concatenate([-s, s], 1).reshape(TS, P, DH).transpose(1, 0, 2)
    bf = mybir.dt.np(BF16)
    later = np.triu(np.full((P, P), NEG, f), 1)
    tri = np.broadcast_to(np.tril(np.ones((E0, E0), f), -1), (P, E0, E0))
    out = {
        "x": a["L0_attn_h_t"].reshape(T, D),
        "uk": np.concatenate([uk, np.zeros((DK, H0, 64 - DC), f), ukb], 2),
        "uq": np.concatenate([uq, uq, uq, ubq, ubq], 2),
        "qr": np.concatenate([qr, qr, qr, qrb, qrb], 2),
        "uv": np.concatenate([uv, uvb], 2),
        "wo": a["L0_attn_W_O"].reshape(H0, DK, D).transpose(1, 0, 2),
        "bo": a["L0_attn_b_O"][None],
        "wdq": np.concatenate([a["L0_attn_W_DQ"]] * 3, 1),
        "bdq": np.concatenate([a["L0_attn_b_DQ"]] * 3)[:, None],
        "wkv": np.concatenate([a["L0_attn_W_DKV"], a["L0_attn_W_KR"]], 1),
        "bkv": np.concatenate([a["L0_attn_b_DKV"], a["L0_attn_b_KR"]])[:, None],
        "bkv_row": a["L0_attn_b_DKV"][None],
        "ident": np.eye(P, dtype=f), "identb": np.eye(P).astype(bf),
        "mask_qk": later.astype(bf), "mask_kq": later.T.astype(bf),
        "gw": a["L0_ffn_gate_w"].T, "tri": tri, "wm": wm,
        "wqkv": a["L1_attn_w_qkv"], "wout": a["L1_attn_w_out"], "cos": cos, "sin": sin,
        "wr": a["L1_ffn_Wr"], "br": a["L1_ffn_br"][None], "ecount": np.arange(E1, dtype=f)[None],
        "W1": a["L1_ffn_W1"], "b1": a["L1_ffn_b1"], "W2": a["L1_ffn_W2"], "b2": a["L1_ffn_b2"],
    }
    return {k: np.ascontiguousarray(v) for k, v in out.items()}


def kernel(**inputs):
    import concourse.bacc as bacc
    from concourse.bass_utils import run_bass_kernel_spmd

    arrays = {f"in_{k}": v for k, v in lay_out(inputs).items()}
    nc = bacc.Bacc("TRN2", target_bir_lowering=False, num_devices=1)
    d = {k[3:]: nc.dram_tensor(k, v.shape, mybir.dt.from_np(v.dtype), kind="ExternalInput").ap()
         for k, v in arrays.items()}
    out = nc.dram_tensor("out_0", (T, D), F32, kind="ExternalOutput").ap()
    build(nc, d, out)
    r = run_bass_kernel_spmd(nc, [arrays], core_ids=[0])
    return r.results[0]["out_0"].reshape(B, S, D)
```

```python
from contextlib import ExitStack

import numpy as np

import concourse.bass as bass
from concourse import mybir

ALU = mybir.AluOpType
ACT = mybir.ActivationFunctionType
AX_X = mybir.AxisListType.X
F32 = mybir.dt.float32
F32R = mybir.dt.float32r
BF16 = mybir.dt.bfloat16
I32 = mybir.dt.int32

P = 128
D = 128
B, S = 2, 1024
T = B * S
NT = T // P
TS = S // P
CH = 512
NCH = T // CH
TC = CH // P
EPS = 1e-5

H0, DK, DC, DR = 8, 128, 32, 32
NZ = 3 * DC + 2
NZM = NZ + 2
HP = 2
U0 = B * H0 // HP
UH = H0 // HP
K0 = (S // CH) * TS
SCALE0 = 1.0 / float(DK + DR) ** 0.5

E0, F0 = 8, 352
NE = E0 + 1
FM = [128, 128, 96]
WCOLS = 2 * F0 + 3 * D

H1, DH = 16, 8
HG = 4
U1 = B * (H1 // HG)
RS = 32
SCALE1 = float(DH) ** -0.5
E1 = 8
NEG = -3.0e38

ST1 = []
for c in range(S // CH):
    j0 = c * TC
    ST1 += [(c, ((j, 0, CH),)) for j in range(j0 + 1)]
    ST1 += [(c, ((j0 + 1, 0, CH - P), (j0 + 3, CH - P, P))), (c, ((j0 + 2, 0, CH - 2 * P),))]
K1 = len(ST1)
K1_FIRST = [c for c, _ in ST1].index(1)
MX0 = [(h, j, c) for c in range(S // CH) for j in range(TS) for h in range(HP)]
MX0_STEP = 3
Z0_SECOND, CTX0_BEFORE, CTX0_FIRST, TURN0_MAX, Z0_FIRST = (0, 1), 2, 10, (11, 11, 12, 13), (14, 15)

MX1 = []
for i0, c in ((0, 0), (TC, 0), (TC, 1)):
    if c * TC == i0:
        parts = [((i0, 0, P), (i0 + 2, P, 3 * P)), ((i0 + 1, 0, 2 * P),), ((i0 + 3, 0, CH),)]
    else:
        parts = [((i, 0, CH),) for i in range(i0, i0 + TC)]
    MX1 += [(r, c, p) for p in parts for r in range(HG)]
MX1_Q_HALF = [m[2][0][0] >= TC for m in MX1].index(True)
MX1_K_HALF = [m[1] for m in MX1].index(1)
MX1_END = [sum(len(m[2]) for m in MX1[:s + 1]) for s in range(len(MX1))]
NMX1 = MX1_END[-1]
STACK1_SECOND, CTX1_BEFORE, CTX1_FIRST, STACK1_FIRST, TURN1_MAX = (0, 1), 2, 5, (6, 7), (8, 9)
MX1_STEP = (5, 5, 5, 5, 5, 5, 5, 5, 0, 0)
MX1_UPTO = [sum(MX1_STEP[:k + 1]) for k in range(len(MX1_STEP))]


FRONT_STATS, FRONT_RSTD, FRONT_XN, FRONT_TURN, FRONT_QKV, FRONT_ROPE = 0, 1, 2, 3, (4, 4, 5, 5), (6, 7)
FIRST_QKV = 2, 6
LAST_NORM_ORDER = (0, 2, 1, 3)
NEWTON = 3
N_NORM = 2 * TC + 5 + 3 * NEWTON


class Steps:

    def __init__(self, sem):
        self.sem, self.n = sem, 0

    def mark(self, ins):
        ins.then_inc(self.sem, 1)
        self.n += 1
        return self.n


def build(nc, d, out):
    with ExitStack() as ctx:
        def sb(name, shape, dt=F32):
            return ctx.enter_context(nc.sbuf_tensor(name, shape, dt))

        def sem(name):
            return ctx.enter_context(nc.semaphore(name))

        ps = ctx.enter_context(nc.psum_tensor("ps", [P, 8, CH], F32))
        ps_wide, ps_pair, ps_ctx, ps_misc = ps[:, 0:4, :], ps[:, 4:6, :], ps[:, 6, :], ps[:, 7, :]
        MAX0_BANKS, TURN0_BANKS, ST0_BANKS, CTX_BANK = (0, 1, 7), (2, 3), (4, 5), 6
        MAX1_BANKS, ST1_BANKS, TURN1_BANK = (0, 1), (2, 3, 4, 5), 7
        MAX0_BANKS_FIRST, MAX1_BANKS_FIRST = MAX0_BANKS + ST0_BANKS, MAX1_BANKS + ST1_BANKS

        x = sb("x", [P, NT, D])
        xn = sb("xn", [P, NT, D])
        xnT = sb("xnT", [P, T])
        stats = sb("stats", [P, NT, 6])
        mv = sb("mv", [P, NT, 2])
        lnv = sb("lnv", [P, 5, NT])
        ident = sb("ident", [P, P])
        identr = sb("identr", [P, P], F32R)
        identb = sb("identb", [P, P], BF16)
        mask_qk = sb("mask_qk", [P, P], BF16)
        mask_kq = sb("mask_kq", [P, P], BF16)
        ones = sb("ones", [P, P])

        wdq = sb("wdq", [P, 3 * DC])
        bdq = sb("bdq", [3 * DC, 1])
        wkv = sb("wkv", [P, DC + DR])
        bkv = sb("bkv", [DC + DR, 1])
        bkv_row = sb("bkv_row", [1, DC])
        early = sb("early", [P, H0 * (65 + NZ + DC + 1 + D)])
        e0, e1, e2 = H0 * 65, H0 * (65 + NZ), H0 * (65 + NZ + DC + 1)
        uk = early[:, 0:e0].rearrange("p (h n) -> p h n", h=H0)
        uq = early[:, e0:e1].rearrange("p (h n) -> p h n", h=H0)
        uv = early[:, e1:e2].rearrange("p (h n) -> p h n", h=H0)
        wo = early[:, e2:].rearrange("p (h n) -> p h n", h=H0)
        v1 = early[:, 0:TS * B * H1 * (DH + 1)].rearrange("p (t b h w) -> p t b h w", t=TS, b=B, h=H1)
        zmap = sb("zmap", [65, H0, NZ])
        zcur = sb("zcur", [65, HP, NZ])
        bo = sb("bo", [1, D])
        vo = sb("vo", [P, 2, D])
        vo_bias = sb("vo_bias", [1, D])
        a0, a1 = 4 * HP * S, 4 * HP * S + T
        rounded = sb("rounded", [P, a1 + HP * TS * NZM], F32R)
        cq = rounded[:, a0:a1]
        half = sb("half", [P, T])
        kvr = half[0:65, :]
        ao = half[:].rearrange("p (t b n) -> p t b n", t=TS, b=B)
        ckv = sb("ckv", [P, TS, B, DC + 1])
        ckv_cur = [sb(f"ckv_cur{i}", [P, TS, DC + 1]) for i in range(2)]
        stacks = rounded[:, 0:a0]
        key_stack, query_stack = ([stacks[:, (2 * k + i) * HP * S:(2 * k + i + 1) * HP * S]
                                   .rearrange("p (h n) -> p h n", h=HP) for i in range(2)] for k in range(2))
        key_stack1 = [stacks[:, i * HG * S:(i + 1) * HG * S].rearrange("p (r n) -> p r n", r=HG) for i in range(2)]
        query_stack1 = [cq[:, i * S:(i + 1) * S] for i in range(2)]
        cT = sb("cT", [P, 2, CH])
        mstage = rounded[:, a1:].rearrange("p (h t n) -> p h t n", h=HP, t=TS)
        w_hi, w_lo = (rounded[:, k * E0 * 2 * F0:(k + 1) * E0 * 2 * F0].rearrange("p (e n) -> p e n", e=E0)
                      for k in range(2))
        x_hi = rounded[:, 2 * E0 * 2 * F0:2 * E0 * 2 * F0 + CH]
        x_lo = sb("x_lo", [P, CH], F32R)
        mx = [sb(f"mx{i}", [P, HG * TS]) for i in range(2)]
        mx_part = [sb(f"mx_part{i}", [P, HG * TS]) for i in range(2)]
        pt = sb("pt", [P, 8, CH])
        rden = sb("rden", [P, HG * TC])
        big = sb("big", [P, 2, TS, B, D])

        gw = sb("gw", [P, E0])
        wm = sb("wm", [P, NE, WCOLS])
        tri = sb("tri", [P, E0, E0])
        comb = sb("comb", [P, NT, NE])
        g8 = sb("g8", [P, 4, NT, E0])
        g64 = big[:, 0].rearrange("p t b n -> p (t b n)").rearrange("p (k t e j) -> p k t e j", k=2, t=NT, e=E0)
        g1 = sb("g1", [P, 4, NT])

        wqkv = sb("wqkv", [P, 3 * D])
        wout = sb("wout", [P, D])
        cos = sb("cos", [P, TS, DH])
        sin = sb("sin", [P, TS, DH])
        v_cur = [sb(f"v_cur{i}", [P, TS, HG, DH + 1]) for i in range(2)]
        kstage = [sb(f"kstage{i}", [P, TS, HG, RS], F32R) for i in range(2)]
        qstage = [sb(f"qstage{i}", [P, TS, HG, RS], F32R) for i in range(2)]
        rawqk = xn[:, TC:TC + 4, :].rearrange("p a n -> p (a n)").rearrange("p (k t n) -> p k t n", k=2, t=TS)


        zero = sb("zero", [P, 1])
        gelu_first = sb("gelu_first", [1, 1])
        norm = sb("norm", [P, 4, TC])
        norm_bits = sb("norm_bits", [P, TC], I32)

        wr = sb("wr", [P, E1])
        br = sb("br", [1, E1])
        rt = sb("rt", [1, 6, B, E1])
        rt64 = sb("rt64", [1, 2, B, E1, E1])
        ecount = sb("ecount", [1, E1])
        idx_f = sb("idx_f", [1, B, 2])
        idx_i = sb("idx_i", [1, B, 2], I32)
        space = wm[:].rearrange("p e n -> p (e n)")
        c0, c1, c2 = E1 * (2 * D + 1), E1 * (3 * D + 1), E1 * (3 * D + 1) + B * 2 * D
        experts1 = space[:, 0:c0].rearrange("p (e n) -> p e n", e=E1)
        b2_all = space[0:1, c0:c1].rearrange("p (e n) -> p e n", e=E1)
        b2 = space[0:1, c1:c2].rearrange("p (b k n) -> p b k n", b=B, k=2)
        chosen = space[:, c2:c2 + B * 2 * (2 * D + 1)].rearrange("p (b k n) -> p b k n", b=B, k=2)

        b2_sum = sb("b2_sum", [1, B, D])

        x_in = [sem(f"x_in{i}") for i in range(NCH)]
        w0_in, wm_in, w1_in, exp1_in, out_done = map(sem, ("w0_in", "wm_in", "w1_in", "exp1_in", "out_done"))
        consts = sem("consts")
        identr_ok, ones_ok, fixed = sem("identr_ok"), sem("ones_ok"), sem("fixed")
        ln_stats, ln_aggr, ln_var, ln_root, ln_step, ln_xn, ln_turn, ln_xT = map(
            sem, ("ln_stats", "ln_aggr", "ln_var", "ln_root", "ln_step", "ln_xn", "ln_turn", "ln_xT"))
        prep_mm, prep_done = sem("prep_mm"), sem("prep_done")
        cq_mm, cq_hi, cq_lo, kv_mm, kv_done, ckv_mm, ckv_done = map(
            sem, ("cq_mm", "cq_hi", "cq_lo", "kv_mm", "kv_done", "ckv_mm", "ckv_done"))
        zcur_ok, cq_copied, ckv_copied, ctx_T = map(sem, ("zcur_ok", "cq_copied", "ckv_copied", "ctx_T"))
        ctx_turn, v_copied, ctx1_T, ctx1_turn = map(sem, ("ctx_turn", "v_copied", "ctx1_T", "ctx1_turn"))
        v_ones = sem("v_ones")
        z_mm, z_hi, z_lo, mx_ok, mx1_ok = map(sem, ("z_mm", "z_hi", "z_lo", "mx_ok", "mx1_ok"))
        s_mm, max_done, m_split, m_turn, m_rows = map(sem, ("s_mm", "max_done", "m_split", "m_turn", "m_rows"))
        st_mm, exp_done, pv_mm, ctx_out = map(sem, ("st_mm", "exp_done", "pv_mm", "ctx_out"))
        o_turn, o_T, o_mm, o_add = map(sem, ("o_turn", "o_T", "o_mm", "o_add"))
        gate_mm, gate_step, gate_exp, comb_ok = map(sem, ("gate_mm", "gate_step", "gate_exp", "comb_ok"))
        eg_mm, eu_mm, silu_done, h_done, ed_mm, moe_add = map(
            sem, ("eg_mm", "eu_mm", "silu_done", "h_done", "ed_mm", "moe_add"))
        w_hi_ok, w_lo_ok, x_hi_ok, x_lo_ok = map(sem, ("w_hi_ok", "w_lo_ok", "x_hi_ok", "x_lo_ok"))
        norm_step, norm_xn, norm_turn, norm_xT = map(sem, ("norm_step", "norm_xn", "norm_turn", "norm_xT"))
        qkv_mm, qk_out, v_out, rope_mul, rope_step = map(sem, ("qkv_mm", "qk_out", "v_out", "rope_mul", "rope_step"))
        staged, stack_turn, stacked, keys_zero = map(sem, ("staged", "stack_turn", "stacked", "keys_zero"))
        s1_mm, max1_done, m1_split, m1_turn, m1_rows = map(
            sem, ("s1_mm", "max1_done", "m1_split", "m1_turn", "m1_rows"))
        st1_mm, exp1_done, pv1_mm, ctx1_out = map(sem, ("st1_mm", "exp1_done", "pv1_mm", "ctx1_out"))
        o1_turn, o1_T, o1_mm, o1_add = map(sem, ("o1_turn", "o1_T", "o1_mm", "o1_add"))
        rt_mm, rt_step, idx_ok, chosen_ok, b2_ok = map(sem, ("rt_mm", "rt_step", "idx_ok", "chosen_ok", "b2_ok"))
        f_mm, gelu_done, y_mm, y_add = map(sem, ("f_mm", "gelu_done", "y_mm", "y_add"))

        N_CONST = 7
        N_FIXED = 8
        W0_LOADS, W1_LOADS = 16, 8

        block = ctx.enter_context(nc.Block())

        @block.sync
        def _(sp):
            xd = d["x"].rearrange("(c t p) m -> c p t m", p=P, t=TC)
            for c in range(NCH):
                sp.dma_start(x[:, c * TC:(c + 1) * TC, :], xd[c]).then_inc(x_in[c], 16)
            loads = [(uk, "uk"), (uq, "uq"), (uv, "uv"), (wo, "wo"), (bo, "bo"), (wdq, "wdq"), (bdq, "bdq"),
                     (wkv, "wkv"), (bkv, "bkv"), (bkv_row, "bkv_row"), (ident, "ident"), (identb, "identb"),
                     (gw, "gw"), (tri, "tri"), (mask_qk, "mask_qk")]
            for t, n in loads:
                sp.dma_start(t[:], d[n]).then_inc(w0_in, 16)
            sp.dma_start(zmap[DC:DC + DR, :, :], d["qr"]).then_inc(w0_in, 16)
            assert len(loads) + 1 == W0_LOADS
            sp.dma_start(wm[:], d["wm"]).then_inc(wm_in, 16)
            loads = [(mask_kq, "mask_kq"), (wqkv, "wqkv"), (wout, "wout"), (cos, "cos"), (sin, "sin"),
                     (wr, "wr"), (br, "br"), (ecount, "ecount")]
            for t, n in loads:
                sp.dma_start(t[:], d[n]).then_inc(w1_in, 16)
            assert len(loads) == W1_LOADS
            sp.wait_ge(ed_mm, NCH * NE)
            sp.dma_start(experts1, d["experts1"]).then_inc(exp1_in, 16)
            sp.dma_start(b2_all, d["b2"]).then_inc(exp1_in, 16)
            od = out.rearrange("(c t p) m -> c p t m", p=P, t=TC)
            for c in range(NCH):
                sp.wait_ge(y_add, c + 1)
                sp.dma_start(od[c], x[:, c * TC:(c + 1) * TC, :]).then_inc(out_done, 16)
            sp.wait_ge(out_done, 16 * NCH)

        @block.gpsimd
        def _(pool):
            nc.gpsimd.memset(zero[:], 0.0).then_inc(consts, 1)
            nc.gpsimd.memset(ckv[:, :, :, DC:DC + 1], 1.0).then_inc(consts, 1)
            nc.gpsimd.memset(comb[:, :, E0:NE], 1.0).then_inc(consts, 1)
            for i in range(2):
                nc.gpsimd.memset(kstage[i][:].bitcast(F32), 0.0).then_inc(consts, 1)
                nc.gpsimd.memset(qstage[i][:].bitcast(F32), 0.0).then_inc(consts, 1)

            def unit0(u, pp, wait):
                pool.wait_ge(z_mm, u * 4)
                for h in range(HP):
                    nc.gpsimd.tensor_copy(zcur[:, h, :], zmap[:, bass.ds((u % UH) * HP + h, 1), :]
                                          .rearrange("p o n -> p (o n)")).then_inc(zcur_ok, 1)
                if wait:
                    pool.wait_ge(pv_mm, u * K0 - K0)
                nc.gpsimd.tensor_copy(ckv_cur[pp][:], ckv[:].rearrange("p t b n -> p t (b n)")
                                      [:, :, bass.ds((u // UH) * (DC + 1), DC + 1)]).then_inc(ckv_copied, 1)

            pool.wait_ge(prep_done, 5)
            pool.wait_ge(ckv_done, 1)
            pool.wait_ge(consts, N_CONST)
            for u in range(2):
                unit0(u, u, False)
            with pool.Fori(1, U0 // 2) as i:
                for pp in range(2):
                    unit0(i * 2 + pp, pp, True)
            pool.wait_ge(prep_mm, 4)
            nc.gpsimd.memset(v1[:, :, :, :, DH:DH + 1], 1.0).then_inc(v_ones, 1)

            pool.wait_ge(wm_in, 16)
            pool.wait_ge(pv_mm, U0 * K0)
            for e in range(E0):
                pool.wait_ge(w_hi_ok, e + 1)
                nc.gpsimd.tensor_tensor(w_lo[:, e, :], wm[:, e, 0:2 * F0], w_hi[:, e, :].bitcast(F32),
                                        ALU.subtract).then_inc(w_lo_ok, 1)

            none = zero[:].unsqueeze(2).unsqueeze(3).broadcast_to([P, TS, HG, DH])

            def stage(u, pp, wait):
                if wait:
                    pool.wait_ge(m1_turn, u * 2 - 2)
                for n, (dst, src, cols) in enumerate(((kstage[pp], 1, (0, 8, 16)), (qstage[pp], 0, (0, 16, 8)))):
                    val = big[:, src].rearrange("p t b n -> p t (b n)")[:, :, bass.ds(u * (HG * DH), HG * DH)]
                    raw = rawqk[:, n].rearrange("p t (h w) -> p t h w", w=DH)
                    pool.wait_ge(staged, u * 8 + 4 * n)
                    nc.gpsimd.tensor_copy(rawqk[:, n], val).then_inc(staged, 1)
                    hi_a, hi_b, lo = (dst[:, :, :, c:c + DH] for c in cols)
                    pool.wait_ge(staged, u * 8 + 4 * n + 1)
                    nc.gpsimd.tensor_tensor(hi_a, raw, none, ALU.add).then_inc(staged, 1)
                    if n == 1:
                        nc.gpsimd.memset(dst[:, :, :, 3 * DH:3 * DH + 2].bitcast(F32), 0.0)
                    nc.gpsimd.tensor_tensor(hi_b, raw, none, ALU.add).then_inc(staged, 1)
                    pool.wait_ge(staged, u * 8 + 4 * n + 2)
                    nc.gpsimd.tensor_tensor(lo, raw, hi_a.bitcast(F32), ALU.subtract).then_inc(staged, 1)
                if wait:
                    pool.wait_ge(pv1_mm, u * K1 - K1)
                nc.gpsimd.tensor_copy(v_cur[pp][:].rearrange("p t h w -> p t (h w)"),
                                      v1.rearrange("p t b h w -> p t (b h w)")
                                      [:, :, bass.ds(u * (HG * (DH + 1)), HG * (DH + 1))]).then_inc(v_copied, 1)

            pool.wait_ge(consts, N_CONST)
            for i in range(2):
                nc.gpsimd.memset(kstage[i][:, :, :, 3 * DH:3 * DH + 2].bitcast(F32), 1.0).then_inc(consts, 1)
            pool.wait_ge(consts, N_CONST + 2)
            pool.wait_ge(rope_step, 2 * (NCH // B))
            pool.wait_ge(v_out, TS)
            pool.wait_ge(v_ones, 1)
            for u in range(2):
                stage(u, u, False)
            pool.wait_ge(eu_mm, 3 * (NCH * NE - 1))
            for i in range(2):
                nc.gpsimd.memset(key_stack1[i].bitcast(F32), 0.0).then_inc(keys_zero, 1)
            pool.wait_ge(rope_step, 2 * NCH)
            pool.wait_ge(v_out, NT)
            with pool.Fori(1, U1 // 2) as i:
                for pp in range(2):
                    stage(i * 2 + pp, pp, True)

        @block.scalar
        def _(act):
            def copy(dst, src):
                return nc.scalar.activation(dst, src, ACT.Copy)

            def ln_act(k):
                act.wait_ge(ln_var, k + 1)
                nc.scalar.activation(lnv[:, 1, :], lnv[:, 0, :], ACT.Sqrt).then_inc(ln_root, 1)

            def ln_evacuate(k, c, bank):
                n = LAST_NORM_ORDER.index(c) if k == 2 else c
                act.wait_ge(ln_turn, k * NCH + n + 1)
                copy(xnT[:, c * CH:(c + 1) * CH], bank).then_inc(ln_xT, 1)

            ln_act(0)
            act.wait_ge(w0_in, 16 * W0_LOADS)
            copy(identr[:], ident[:]).then_inc(identr_ok, 1)
            for g in range(2):
                act.wait_ge(prep_mm, g + 1)
                v = ps_wide[:, g, 0:4 * NZ].rearrange("p (h n) -> p h n", n=NZ)
                copy(zmap[0:DC, 4 * g:4 * g + 4, :], v[0:DC]).then_inc(prep_done, 1)
                copy(zmap[64:65, 4 * g:4 * g + 4, :], v[64:65]).then_inc(prep_done, 1)
            act.wait_ge(prep_mm, 3)
            copy(vo[:], ps_wide[:, 2, 0:2 * D].rearrange("p (g n) -> p g n", g=2)).then_inc(prep_done, 1)
            act.wait_ge(prep_mm, 4)
            copy(vo_bias[:], ps_wide[0:1, 3, 0:D]).then_inc(prep_done, 1)

            for c in range(NCH):
                ln_evacuate(0, c, ps_pair[:, c % 2, :])
                cols = slice(c * CH, (c + 1) * CH)
                act.wait_ge(cq_mm, c + 1)
                nc.scalar.activation(cq[0:3 * DC, cols], ps_ctx[0:3 * DC, :], ACT.Identity,
                                     bias=bdq[:, 0:1]).then_inc(cq_hi, 1)
                act.wait_ge(kv_mm, c + 1)
                nc.scalar.activation(kvr[0:DC + DR, cols], ps_misc[0:DC + DR, :], ACT.Identity,
                                     bias=bkv[:, 0:1]).then_inc(kv_done, 1)

            def z_hi_copy(u, pp, k):
                h, c = k % HP, k // HP
                act.wait_ge(z_mm, u * 4 + (k + 1))
                copy(key_stack[pp][0:NZ, h, c * CH:(c + 1) * CH], ps[0:NZ, TURN0_BANKS[k % 2], :]).then_inc(z_hi, 1)

            def exps0(u, t, first):
                for h in range(HP):
                    act.wait_ge(st_mm, u * (HP * K0) + (HP * t + h + 1))
                    if not (first and t < 4):
                        act.wait_ge(pv_mm, u * K0 + (t - 3))
                    nc.scalar.activation(pt[:, (HP * t + h) % 8, :], ps[:, ST0_BANKS[h], :], ACT.Exp,
                                         scale=SCALE0).then_inc(exp_done, 1)

            def context_T(u, c, first):
                act.wait_ge(pv_mm, u * K0 + (c + 1) * TS)
                if not first:
                    act.wait_ge(ctx_turn, u * 2 + (c - 1))
                copy(cT[:, c, :], ps[:, CTX_BANK, :]).then_inc(ctx_T, 1)

            def unit0(u, pp, first=False, s=True, z=True):
                for t in range(K0):
                    exps0(u, t, first)
                    if s and t in Z0_SECOND:
                        z_hi_copy(u + 1, 1 - pp, 2 + Z0_SECOND.index(t))
                    if t == TS:
                        context_T(u, 0, first)
                    if z and t in Z0_FIRST:
                        z_hi_copy(u + 2, pp, Z0_FIRST.index(t))
                context_T(u, 1, first)

            act.wait_ge(fixed, N_FIXED)
            for k in range(4):
                z_hi_copy(0, 0, k)
            for k in range(2):
                z_hi_copy(1, 1, k)
            unit0(0, 0, first=True)
            unit0(1, 1)
            with act.Fori(1, U0 // 2 - 1) as i:
                unit0(i * 2, 0)
                unit0(i * 2 + 1, 1)
            unit0(U0 - 2, 0, z=False)
            unit0(U0 - 1, 1, s=False, z=False)

            for c in range(NCH):
                act.wait_ge(o_turn, 2 * c + 2)
                if c >= 2:
                    act.wait_ge(o_mm, c - 1)
                copy(pt[:, 4 * (c % 2):4 * (c % 2) + 2, :], ps_wide[:, 2 * (c % 2):2 * (c % 2) + 2, :]).then_inc(o_T, 1)

            act.wait_ge(wm_in, 16)
            act.wait_ge(pv_mm, U0 * K0)
            for e in range(E0):
                copy(w_hi[:, e, :], wm[:, e, 0:2 * F0]).then_inc(w_hi_ok, 1)

            ln_act(1)
            for c in range(NCH):
                ln_evacuate(1, c, ps_pair[:, c % 2, :])
                if c == 0:
                    act.wait_ge(ln_xT, NCH + 1)
                    copy(x_hi, xnT[:, 0:CH]).then_inc(x_hi_ok, 1)

            act.wait_ge(gate_step, 1)
            nc.scalar.activation(g8[:, 1], g8[:, 0], ACT.Exp).then_inc(gate_exp, 1)

            def front_evacuate(c, e):
                if e == FRONT_TURN:
                    act.wait_ge(norm_turn, c + 1)
                    copy(cT[:, 0, :], ps_ctx).then_inc(norm_xT, 1)
                for t in range(TC):
                    if e == FRONT_QKV[t]:
                        i, b = c % 2 * TC + t, c // 2
                        bank = (ps_misc, ps_ctx)[t % 2]
                        act.wait_ge(qkv_mm, c * TC + (t + 1))
                        vals = v1.rearrange("p t b h w -> p t (b h) w")[:, bass.ds(i, 1), bass.ds(b * H1, H1), 0:DH]
                        copy(vals.rearrange("p o h w -> p (o h) w"),
                             bank[:, 2 * D:3 * D].rearrange("p (h w) -> p h w", w=DH)).then_inc(v_out, 1)
                        qk = big[:].rearrange("p k t b n -> p k t (b n)")[:, :, bass.ds(i, 1), bass.ds(b * D, D)]
                        copy(qk.rearrange("p k o n -> p k (o n)"),
                             bank[:, 0:2 * D].rearrange("p (k n) -> p k n", k=2)).then_inc(qk_out, 1)

            def silus(ch, front=True, following=True):
                for v in range(3 * NE):
                    if following and v == 3 * E0:
                        act.wait_ge(eu_mm, ch * (3 * NE) + 3 * E0)
                        copy(x_hi, xnT[:, bass.ds((ch + 1) * CH, CH)]).then_inc(x_hi_ok, 1)
                    if front and v % 3 == 0 and v >= 6:
                        front_evacuate(ch - 1, v // 3 - 2)
                    act.wait_ge(eg_mm, ch * (3 * NE) + (v + 1))
                    m = FM[v % 3]
                    if v >= 2:
                        act.wait_ge(h_done, ch * (3 * NE) + (v - 1))
                    else:
                        act.wait_ge(h_done, ch * (3 * NE))
                    nc.scalar.activation(pt[0:m, 6 + v % 2, :], ps_wide[0:m, v % 2, :], ACT.Silu).then_inc(silu_done, 1)

            silus(0, front=False)
            with act.Fori(1, NCH - 1) as ch:
                silus(ch)
            silus(NCH - 1, following=False)
            def stack(u, pp, n):
                act.wait_ge(stack_turn, u * 4 + (n + 1))
                cols = slice(n // 2 * CH, (n // 2 + 1) * CH)
                if n % 2 == 0:
                    copy(query_stack1[pp][:, cols], ps[:, TURN1_BANK, :]).then_inc(stacked, 1)
                    return
                for r in range(HG):
                    rows = slice(RS * r, RS * (r + 1))
                    ins = copy(key_stack1[pp][rows, r, cols], ps[rows, TURN1_BANK, :])
                ins.then_inc(stacked, 1)

            def max_rows1(u, pp, hf):
                act.wait_ge(m1_turn, u * 2 + (hf + 1))
                copy(query_stack1[pp][:, hf * CH:(hf + 1) * CH], ps[:, TURN1_BANK, :]).then_inc(m1_rows, 1)

            def exps1(u, t, first):
                w = sum(m for _, _, m in ST1[t][1])
                for g in range(2):
                    act.wait_ge(st1_mm, u * (2 * K1) + (2 * t + g + 1))
                    if not (first and t < 2):
                        act.wait_ge(pv1_mm, u * K1 + (t - 1))
                    nc.scalar.activation(pt[:, 4 * (t % 2) + 2 * g:4 * (t % 2) + 2 * g + 2, 0:w],
                                         ps[:, ST1_BANKS[2 * g]:ST1_BANKS[2 * g] + 2, 0:w], ACT.Exp,
                                         scale=SCALE1).then_inc(exp1_done, 1)

            def context1_T(u, c, first):
                act.wait_ge(pv1_mm, u * K1 + (K1_FIRST if c == 0 else K1))
                if not first:
                    act.wait_ge(ctx1_turn, u * 2 + (c - 1))
                copy(cT[:, c, :], ps[:, CTX_BANK, :]).then_inc(ctx1_T, 1)

            def unit1(u, pp, first=False, s=True, t=True):
                for k in range(K1):
                    exps1(u, k, first)
                    if k == K1_FIRST:
                        context1_T(u, 0, first)
                    if s and k in STACK1_SECOND:
                        stack(u + 1, 1 - pp, 2 + STACK1_SECOND.index(k))
                    if t and k in STACK1_FIRST:
                        stack(u + 2, pp, STACK1_FIRST.index(k))
                    if s and k in TURN1_MAX:
                        max_rows1(u + 1, 1 - pp, TURN1_MAX.index(k))
                context1_T(u, 1, first)

            act.wait_ge(keys_zero, 2)
            for n in range(4):
                stack(0, 0, n)
            for e in range(NE):
                front_evacuate(NCH - 1, e)
            for hf in range(2):
                max_rows1(0, 0, hf)
            for n in range(2):
                stack(1, 1, n)
            unit1(0, 0, first=True)
            unit1(1, 1)
            with act.Fori(1, U1 // 2 - 1) as i:
                unit1(i * 2, 0)
                unit1(i * 2 + 1, 1)
            unit1(U1 - 2, 0, t=False)
            unit1(U1 - 1, 1, s=False, t=False)

            for c in range(NCH):
                act.wait_ge(o1_turn, c + 1)
                if c >= 2:
                    act.wait_ge(o1_mm, c - 1)
                copy(pt[:, c % 2, :], ps_wide[:, c % 2, :]).then_inc(o1_T, 1)

            ln_act(2)
            for n, c in enumerate(LAST_NORM_ORDER[0:3]):
                ln_evacuate(2, c, ps_pair[:, n % 2, :])
            act.wait_ge(exp1_in, 32)
            nc.scalar.activation(gelu_first[:], zero[0:1, :], ACT.Gelu)
            act.wait_ge(idx_ok, 1)
            for c in range(NCH):
                if c % (NCH // B) == 0:
                    b = c // (NCH // B)
                    for k in range(2):
                        e = act.value_load(idx_i[0:1, b, k:k + 1], min_val=0, max_val=E1 - 1)
                        copy(chosen[:, b, k, :], experts1[:, bass.ds(e, 1), :].rearrange("p o n -> p (o n)")).then_inc(chosen_ok, 1)
                        copy(b2[:, b, k, :], b2_all[:, bass.ds(e, 1), :].rearrange("p o n -> p (o n)")).then_inc(chosen_ok, 1)
                    act.wait_ge(chosen_ok, 4 * (b + 1))
                    if b == 0:
                        ln_evacuate(2, LAST_NORM_ORDER[3], ps_pair[:, 1, :])
                for k in range(2):
                    act.wait_ge(f_mm, 2 * c + k + 1)
                    if c >= 2:
                        act.wait_ge(y_mm, c - 1)
                    nc.scalar.activation(pt[:, 2 * (c % 2) + k, :], ps_wide[:, k, :], ACT.Gelu,
                                         bias=chosen[:, c // 2, k, 2 * D:2 * D + 1]).then_inc(gelu_done, 1)

        @block.tensor
        def _(pe):
            mm = nc.tensor.matmul

            def ln_turns(k, c):
                n = LAST_NORM_ORDER.index(c) if k == 2 else c
                pe.wait_ge(ln_xn, k * NT + (n + 1) * TC)
                if k or n >= 2:
                    pe.wait_ge(ln_xT, k * NCH + n - 1 if n >= 2 else k * NCH)
                for t in range(TC):
                    ins = nc.tensor.transpose(ps_pair[:, n % 2, t * P:(t + 1) * P], xn[:, c * TC + t, :], ident[:])
                ins.then_inc(ln_turn, 1)

            pe.wait_ge(w0_in, 16 * W0_LOADS)
            for h in range(H0):
                g, r = h // 4, h % 4
                ins = mm(ps_wide[0:65, g, r * NZ:(r + 1) * NZ], uk[:, h, :], uq[:, h, :], start=True, stop=True)
                if r == 3:
                    ins.then_inc(prep_mm, 1)
            for h in range(H0):
                g, r = h // 4, h % 4
                ins = mm(ps_wide[32 * r:32 * r + 32, 2, g * D:(g + 1) * D], uv[:, h, 0:DC], wo[:, h, :],
                         start=True, stop=True)
            ins.then_inc(prep_mm, 1)
            pe.wait_ge(ones_ok, 1)
            for h in range(H0):
                mm(ps_wide[0:1, 3, 0:D], uv[:, h, DC:DC + 1], wo[:, h, :], start=(h == 0), stop=False)
            mm(ps_wide[0:1, 3, 0:D], ones[0:1, 0:1], bo[:], start=False, stop=True).then_inc(prep_mm, 1)

            for c in range(NCH):
                cols = slice(c * CH, (c + 1) * CH)
                if c == 0:
                    ln_turns(0, 0)
                if c + 1 < NCH:
                    ln_turns(0, c + 1)
                pe.wait_ge(ln_xT, c + 1)
                if c:
                    pe.wait_ge(cq_lo, c)
                mm(ps_ctx[0:3 * DC, :], wdq[:], xnT[:, cols], start=True, stop=True).then_inc(cq_mm, 1)
                if c:
                    pe.wait_ge(kv_done, c)
                mm(ps_misc[0:DC + DR, :], wkv[:], xnT[:, cols], start=True, stop=True).then_inc(kv_mm, 1)
                if c == 0:
                    pe.wait_ge(prep_done, 6)
                for t in range(c * TC, (c + 1) * TC):
                    o = ps_wide[:, 0, t * DC:(t + 1) * DC]
                    mm(o, xnT[:, t * P:(t + 1) * P], wkv[:, 0:DC], start=True, stop=False)
                    ins = mm(o, ones[0:1, :], bkv_row[:], start=False, stop=True)
            ins.then_inc(ckv_mm, 1)

            def make_z(u, k, before):
                h, c = k % HP, k // HP
                if k == 0:
                    pe.wait_ge(zcur_ok, u * HP + HP)
                if before:
                    pe.wait_ge(*before)
                mm(ps[0:NZ, TURN0_BANKS[k % 2], :], zcur[:, h, :], kvr[:, bass.ds((u // UH) * S + c * CH, CH)],
                   start=True, stop=True).then_inc(z_mm, 1)

            def scores_max(u, pp, s, first):
                h, j, c = MX0[s]
                if s == 0:
                    pe.wait_ge(z_lo, u * 4 + 2)
                    pe.wait_ge(cq_copied, u * 2 + 1)
                if s == HP * TC:
                    pe.wait_ge(cq_copied, u * 2 + 2)
                if s == HP * TS:
                    pe.wait_ge(z_lo, u * 4 + 4)
                banks = MAX0_BANKS_FIRST if first else MAX0_BANKS
                if s >= len(banks):
                    pe.wait_ge(max_done, u * len(MX0) + (s + 1 - len(banks)))
                elif not first:
                    pe.wait_ge(max_done, u * len(MX0))
                mm(ps[:, banks[s % len(banks)], :], query_stack[pp][0:NZ, h, j * P:(j + 1) * P],
                   key_stack[pp][0:NZ, h, c * CH:(c + 1) * CH], start=True, stop=True).then_inc(s_mm, 1)

            def turn_max(u, k, before):
                h, hf = k // 2, k % 2
                if k == 0:
                    pe.wait_ge(m_split, u * 2 + 2)
                if before:
                    pe.wait_ge(*before)
                for t in range(TC):
                    ins = nc.tensor.transpose(ps[0:NZM, TURN0_BANKS[hf], t * P:(t + 1) * P].bitcast(F32R),
                                              mstage[:, h, hf * TC + t, :], identr[:])
                ins.then_inc(m_turn, 1)

            def scores(u, pp, h, t, first):
                c, kt = t // TS, t % TS
                if t == 0 and h == 0:
                    pe.wait_ge(m_rows, u * 4 + 4)
                if not (first and t == 0):
                    pe.wait_ge(exp_done, u * (HP * K0) + (HP * (t - 1) + h + 1))
                mm(ps[:, ST0_BANKS[h], :], key_stack[pp][0:NZM, h, kt * P:(kt + 1) * P],
                   query_stack[pp][0:NZM, h, c * CH:(c + 1) * CH], start=True, stop=True).then_inc(st_mm, 1)

            def values(u, pp, t, first):
                c, kt = t // TS, t % TS
                if t == 0:
                    pe.wait_ge(ckv_copied, u + 1)
                if kt == 0 and not (first and c == 0):
                    pe.wait_ge(ctx_T, u * 2 + c)
                pe.wait_ge(exp_done, u * (HP * K0) + (HP * t + HP))
                for h in range(HP):
                    ins = mm(ps[64 * h:64 * h + DC + 1, CTX_BANK, :], ckv_cur[pp][:, kt, :],
                             pt[:, (HP * t + h) % 8, :], start=(kt == 0), stop=(kt == TS - 1))
                ins.then_inc(pv_mm, 1)

            def turn_context(u, c, before):
                pe.wait_ge(ctx_T, u * 2 + (c + 1))
                if before:
                    pe.wait_ge(*before)
                for t in range(TC):
                    ins = nc.tensor.transpose(ps[:, TURN0_BANKS[1 - c], t * P:(t + 1) * P],
                                              cT[:, c, t * P:(t + 1) * P], ident[:])
                ins.then_inc(ctx_turn, 1)

            def unit0(u, pp, first=False, s=True, z=True):
                def piece(t, n):
                    if s and MX0_STEP * t + n < len(MX0):
                        scores_max(u + 1, 1 - pp, MX0_STEP * t + n, False)

                for t in range(K0):
                    for h in range(HP):
                        scores(u, pp, h, t, first)
                        piece(t, h)
                    if t:
                        values(u, pp, t - 1, first)
                    piece(t, 2)
                    if s and t in Z0_SECOND:
                        k = 2 + Z0_SECOND.index(t)
                        make_z(u + 1, k, (z_lo, u * 4 + (k + 3)))
                    if t == CTX0_BEFORE and not first:
                        turn_context(u - 1, 1, (z_lo, u * 4 + 7) if s else None)
                    if t == CTX0_FIRST:
                        turn_context(u, 0, (z_lo, u * 4 + 8) if s else None)
                    for k in range(4):
                        if s and t == TURN0_MAX[k]:
                            turn_max(u + 1, k, (m_rows, u * 4 + (k + 3)) if k >= 2 else (ctx_out, u * 4 + 2) if k
                                     else None if first else (ctx_out, u * 4))
                    if z and t in Z0_FIRST:
                        k = Z0_FIRST.index(t)
                        make_z(u + 2, k, (m_rows, u * 4 + (k + 7)))
                values(u, pp, K0 - 1, first)

            pe.wait_ge(consts, N_CONST)
            pe.wait_ge(identr_ok, 1)
            pe.wait_ge(fixed, N_FIXED)
            pe.wait_ge(cq_lo, NCH)
            pe.wait_ge(kv_done, NCH)
            pe.wait_ge(ckv_done, 1)
            for k in range(4):
                make_z(0, k, (z_lo, k - 1) if k >= 2 else None)
            for n in range(len(MX0)):
                scores_max(0, 0, n, True)
            for k in range(4):
                turn_max(0, k, (m_rows, k - 1) if k >= 2 else None)
            for k in range(2):
                make_z(1, k, (m_rows, k + 3))
            unit0(0, 0, first=True)
            unit0(1, 1)
            with pe.Fori(1, U0 // 2 - 1) as i:
                unit0(i * 2, 0)
                unit0(i * 2 + 1, 1)
            unit0(U0 - 2, 0, z=False)
            unit0(U0 - 1, 1, s=False, z=False)
            turn_context(U0 - 1, 1, (ctx_out, 4 * U0 - 2))

            ctxn = big[:].rearrange("p a t b n -> p (a t b n)").rearrange("p (t b n) -> p t b n", t=TS, b=B)

            def o_turns(c):
                if c == 0:
                    pe.wait_ge(ctx_out, 4 * U0)
                if c >= 2:
                    pe.wait_ge(o_T, c - 1)
                for g in range(2):
                    for t in range(TC):
                        b, i = (c * TC + t) // TS, (c * TC + t) % TS
                        ins = nc.tensor.transpose(ps_wide[:, 2 * (c % 2) + g, t * P:(t + 1) * P],
                                                  ctxn[:, i, b, g * P:(g + 1) * P], ident[:])
                    ins.then_inc(o_turn, 1)

            def o_mms(c):
                pe.wait_ge(o_T, c + 1)
                if c >= 2:
                    pe.wait_ge(o_add, c - 1)
                for t in range(TC):
                    o = ps_pair[:, c % 2, t * P:(t + 1) * P]
                    for g in range(2):
                        mm(o, pt[:, 4 * (c % 2) + g, t * P:(t + 1) * P], vo[:, g, :], start=(g == 0), stop=False)
                    ins = mm(o, ones[0:1, :], vo_bias[:], start=False, stop=True)
                ins.then_inc(o_mm, 1)

            for c in range(NCH + 1):
                if c < NCH:
                    o_turns(c)
                if c:
                    o_mms(c - 1)

            pe.wait_ge(o_add, NCH)
            for c in range(NCH):
                ln_turns(1, c)
            for c in range(NCH):
                pe.wait_ge(ln_xT, NCH + c + 1)
                for t in range(c * TC, (c + 1) * TC):
                    ins = mm(ps_ctx[:, t * E0:(t + 1) * E0], xnT[:, t * P:(t + 1) * P], gw[:], start=True, stop=True)
            ins.then_inc(gate_mm, 1)
            pe.wait_ge(wm_in, 16)

            def gate_up(ch, e):
                for f in range(3):
                    v, m = 3 * e + f, FM[f]
                    pe.wait_ge(h_done, ch * (3 * NE) + max(v - 1, 0))
                    if f == 0 and e < E0:
                        if e == 0:
                            pe.wait_ge(x_lo_ok, ch + 1)
                        if isinstance(ch, int) and ch == 0:
                            pe.wait_ge(w_lo_ok, e + 1)
                    for bank, w0, done in ((v % 2, 0, eg_mm), (2 + v % 2, F0, eu_mm)):
                        o, cols = ps_wide[0:m, bank, :], slice(w0 + f * P, w0 + f * P + m)
                        if e == E0:
                            mm(o, wm[:, e, cols], xnT[:, bass.ds(ch * CH, CH)], start=True, stop=True).then_inc(done, 1)
                            continue
                        mm(o, w_lo[:, e, cols], x_hi, start=True, stop=False)
                        mm(o, w_hi[:, e, cols], x_lo[:], start=False, stop=False)
                        mm(o, w_hi[:, e, cols], x_hi, start=False, stop=True).then_inc(done, 1)

            def down(ch, e):
                pe.wait_ge(h_done, ch * (3 * NE) + (3 * e + 3))
                pe.wait_ge(moe_add, ch * (TC * NE) + TC * max(e - 1, 0))
                for t in range(TC):
                    for f in range(3):
                        m = FM[f]
                        ins = mm(ps_pair[:, e % 2, t * P:(t + 1) * P], pt[0:m, 3 * (e % 2) + f, t * P:(t + 1) * P],
                                 wm[0:m, e, 2 * F0 + f * D:2 * F0 + (f + 1) * D], start=(f == 0), stop=(f == 2))
                ins.then_inc(ed_mm, 1)

            def front(c, e):
                if e == FRONT_TURN:
                    pe.wait_ge(norm_xn, c * TC + TC)
                    for t in range(TC):
                        ins = nc.tensor.transpose(ps_ctx[:, t * P:(t + 1) * P], xn[:, t, :], ident[:])
                    ins.then_inc(norm_turn, 1)
                for t in range(TC):
                    if e == FRONT_QKV[t]:
                        if t < 2:
                            pe.wait_ge(norm_xT, c + 1)
                        else:
                            pe.wait_ge(qk_out, c * TC + (t - 1))
                        mm((ps_misc, ps_ctx)[t % 2][:, 0:3 * D], cT[:, 0, t * P:(t + 1) * P], wqkv[:],
                           start=True, stop=True).then_inc(qkv_mm, 1)

            def experts(ch, beside=True):
                gate_up(ch, 0)
                for e in range(NE):
                    if e + 1 < NE:
                        gate_up(ch, e + 1)
                    down(ch, e)
                    if beside:
                        front(ch - 1, e)

            experts(0, beside=False)
            pe.wait_ge(w1_in, 16 * W1_LOADS)
            with pe.Fori(1, NCH - 1) as ch:
                experts(ch)
            experts(NCH - 1)

            def turn_stack(u, pp, n, before):
                hf, src = n // 2, (qstage, kstage)[n % 2][pp]
                if n == 0:
                    pe.wait_ge(staged, u * 8 + 8)
                pe.wait_ge(*before)
                for t in range(TC):
                    ins = nc.tensor.transpose(ps[:, TURN1_BANK, t * P:(t + 1) * P].bitcast(F32R),
                                              src[:, hf * TC + t].rearrange("p h w -> p (h w)"), identr[:])
                ins.then_inc(stack_turn, 1)

            def scores_max1(u, pp, s, first):
                r, c, parts = MX1[s]
                if s == 0:
                    pe.wait_ge(stacked, u * 4 + 2)
                if s == MX1_Q_HALF:
                    pe.wait_ge(stacked, u * 4 + 3)
                if s == MX1_K_HALF:
                    pe.wait_ge(stacked, u * 4 + 4)
                banks = MAX1_BANKS_FIRST if first else MAX1_BANKS
                if s >= len(banks):
                    pe.wait_ge(max1_done, u * NMX1 + MX1_END[s - len(banks)])
                elif not first:
                    pe.wait_ge(max1_done, u * NMX1)
                bank = ps[:, banks[s % len(banks)], :]
                ins = None
                for i, o, w in parts:
                    diag = c == i // TC
                    ins = mm(bank[:, o:o + w], query_stack1[pp][:, i * P:(i + 1) * P],
                             key_stack1[pp][:, r, c * CH:c * CH + w], start=(o == 0), stop=not diag)
                if diag:
                    for i, o, w in parts:
                        ins = mm(bank[:, o + w - P:o + w], identb[:], mask_qk[:], start=False,
                                 stop=(o == parts[-1][1]))
                ins.then_inc(s1_mm, 1)

            def turn_max1(u, pp, hf, before):
                if hf == 0:
                    pe.wait_ge(m1_split, u * 2 + 2)
                pe.wait_ge(*before)
                for t in range(TC):
                    ins = nc.tensor.transpose(ps[:, TURN1_BANK, t * P:(t + 1) * P].bitcast(F32R),
                                              qstage[pp][:, hf * TC + t].rearrange("p h w -> p (h w)"), identr[:])
                ins.then_inc(m1_turn, 1)

            def scores1(u, pp, r, t, first):
                c, parts = ST1[t]
                if t == 0 and r == 0:
                    pe.wait_ge(m1_rows, u * 2 + 2)
                if r % 2 == 0 and not (first and t == 0):
                    pe.wait_ge(exp1_done, u * (2 * K1) + (2 * (t - 1) + r // 2 + 1))
                for j, o, w in parts:
                    diag = j >= c * TC
                    q0 = (c + 1) * CH - w
                    ins = mm(ps[:, ST1_BANKS[r], o:o + w], key_stack1[pp][:, r, j * P:(j + 1) * P],
                             query_stack1[pp][:, q0:q0 + w], start=(o == 0), stop=not diag)
                if not diag and r % 2:
                    ins.then_inc(st1_mm, 1)

            def masks1(t):
                c, parts = ST1[t]
                if parts[0][0] < c * TC:
                    return
                for r in range(HG):
                    for j, o, w in parts:
                        ins = mm(ps[:, ST1_BANKS[r], o:o + P], identb[:], mask_kq[:], start=False,
                                 stop=(o == parts[-1][1]))
                    if r % 2:
                        ins.then_inc(st1_mm, 1)

            def values1(u, pp, t, first):
                c, parts = ST1[t]
                if t == 0:
                    pe.wait_ge(v_copied, u + 1)
                if parts[0][0] == 0 and not (first and c == 0):
                    pe.wait_ge(ctx1_T, u * 2 + c)
                pe.wait_ge(exp1_done, u * (2 * K1) + (2 * t + 2))
                for j, o, w in parts:
                    for r in range(HG):
                        ins = mm(ps[RS * r:RS * r + DH + 1, CTX_BANK, CH - w:CH], v_cur[pp][:, j, r, :],
                                 pt[:, 4 * (t % 2) + r, o:o + w], start=(j == 0), stop=(j == c * TC + 2))
                ins.then_inc(pv1_mm, 1)

            def turn_context1(u, c, before):
                pe.wait_ge(ctx1_T, u * 2 + (c + 1))
                pe.wait_ge(*before)
                for t in range(TC):
                    ins = nc.tensor.transpose(ps[:, TURN1_BANK, t * P:(t + 1) * P],
                                              cT[:, c, t * P:(t + 1) * P], ident[:])
                ins.then_inc(ctx1_turn, 1)

            def unit1(u, pp, first=False, s=True, t=True):
                def piece(k, n):
                    if s and n < MX1_STEP[k]:
                        scores_max1(u + 1, 1 - pp, MX1_UPTO[k] - MX1_STEP[k] + n, False)

                for k in range(K1):
                    scores1(u, pp, 0, k, first)
                    scores1(u, pp, 1, k, first)
                    piece(k, 0)
                    scores1(u, pp, 2, k, first)
                    scores1(u, pp, 3, k, first)
                    piece(k, 1)
                    masks1(k)
                    piece(k, 2)
                    if k:
                        values1(u, pp, k - 1, first)
                    for n in range(3, max(MX1_STEP)):
                        piece(k, n)
                    if s and k in STACK1_SECOND:
                        n = 2 + STACK1_SECOND.index(k)
                        turn_stack(u + 1, 1 - pp, n, (stacked, u * 4 + (n + 4)))
                    if k == CTX1_BEFORE and not first:
                        turn_context1(u - 1, 1, (stacked, u * 4 + 8) if s else (m1_rows, u * 2 + 2))
                    if k == CTX1_FIRST:
                        turn_context1(u, 0, (stacked, u * 4 + 8) if first else (ctx1_out, u * 4))
                    if t and k in STACK1_FIRST:
                        n = STACK1_FIRST.index(k)
                        turn_stack(u + 2, pp, n, (stacked, u * 4 + 9) if n else (ctx1_out, u * 4 + 2))
                    if s and k in TURN1_MAX:
                        hf = TURN1_MAX.index(k)
                        turn_max1(u + 1, 1 - pp, hf, (m1_rows, u * 2 + 3) if hf else
                                  (stacked, u * 4 + 10) if t else (ctx1_out, u * 4 + 2))
                values1(u, pp, K1 - 1, first)

            for n in range(4):
                turn_stack(0, 0, n, (stacked, n))
            pe.wait_ge(stacked, 4)
            front(NCH - 1, FRONT_TURN)
            for n in range(len(MX1)):
                scores_max1(0, 0, n, True)
                if n == FIRST_QKV[0]:
                    front(NCH - 1, FRONT_QKV[0])
                if n == FIRST_QKV[1]:
                    front(NCH - 1, FRONT_QKV[2])
            turn_max1(0, 0, 0, (qk_out, NT))
            turn_max1(0, 0, 1, (m1_rows, 1))
            turn_stack(1, 1, 0, (m1_rows, 2))
            turn_stack(1, 1, 1, (stacked, 5))
            unit1(0, 0, first=True)
            unit1(1, 1)
            with pe.Fori(1, U1 // 2 - 1) as i:
                unit1(i * 2, 0)
                unit1(i * 2 + 1, 1)
            unit1(U1 - 2, 0, t=False)
            unit1(U1 - 1, 1, s=False, t=False)
            turn_context1(U1 - 1, 1, (ctx1_out, 4 * U1 - 2))

            def o1_turns(c):
                if c == 0:
                    pe.wait_ge(ctx1_out, 4 * U1)
                if c >= 2:
                    pe.wait_ge(o1_T, c - 1)
                for t in range(TC):
                    b, i = (c * TC + t) // TS, (c * TC + t) % TS
                    ins = nc.tensor.transpose(ps_wide[:, c % 2, t * P:(t + 1) * P], ao[:, i, b, :], ident[:])
                ins.then_inc(o1_turn, 1)

            def o1_mms(c):
                pe.wait_ge(o1_T, c + 1)
                if c >= 2:
                    pe.wait_ge(o1_add, c - 1)
                for t in range(TC):
                    ins = mm(ps_pair[:, c % 2, t * P:(t + 1) * P], pt[:, c % 2, t * P:(t + 1) * P], wout[:],
                             start=True, stop=True)
                ins.then_inc(o1_mm, 1)

            for c in range(NCH + 1):
                if c < NCH:
                    o1_turns(c)
                if c:
                    o1_mms(c - 1)

            pe.wait_ge(o1_add, NCH)
            for c in LAST_NORM_ORDER[0:3]:
                ln_turns(2, c)
            pe.wait_ge(ln_xT, 2 * NCH + 2)
            for b in range(B):
                o = ps_ctx[0:1, b * E1:(b + 1) * E1]
                mm(o, xnT[:, b * S:b * S + 1], wr[:], start=True, stop=False)
                ins = mm(o, ones[0:1, 0:1], br[:], start=False, stop=True)
            ins.then_inc(rt_mm, 1)
            ln_turns(2, LAST_NORM_ORDER[3])
            pe.wait_ge(ln_xT, 3 * NCH - 1)

            def f_mms(c):
                if c == LAST_NORM_ORDER[3]:
                    pe.wait_ge(ln_xT, 3 * NCH)
                pe.wait_ge(chosen_ok, 4 * (c // 2 + 1))
                for k in range(2):
                    if c:
                        pe.wait_ge(gelu_done, 2 * c - 1 + k)
                    mm(ps_wide[:, k, :], chosen[:, c // 2, k, 0:D], xnT[:, c * CH:(c + 1) * CH],
                       start=True, stop=True).then_inc(f_mm, 1)

            def y_mms(c):
                pe.wait_ge(gelu_done, 2 * c + 2)
                pe.wait_ge(b2_ok, c // 2 + 1)
                if c >= 2:
                    pe.wait_ge(y_add, c - 1)
                for t in range(TC):
                    o = ps_pair[:, c % 2, t * P:(t + 1) * P]
                    for k in range(2):
                        mm(o, pt[:, 2 * (c % 2) + k, t * P:(t + 1) * P], chosen[:, c // 2, k, D:2 * D],
                           start=(k == 0), stop=False)
                    ins = mm(o, ones[0:1, :], b2_sum[:, c // 2, :], start=False, stop=True)
                ins.then_inc(y_mm, 1)

            for c in range(NCH + 1):
                if c < NCH:
                    f_mms(c)
                if c:
                    y_mms(c - 1)

        @block.vector
        def _(dve):
            v = nc.vector

            def norm_chunk(c):
                for t in range(c * TC, (c + 1) * TC):
                    v.tensor_scalar(xn[:, t, :], x[:, t, :], mv[:, t, 0:1], lnv[:, 4, t:t + 1],
                                    ALU.subtract, ALU.mult).then_inc(ln_xn, 1)

            def layer_norm(k, ready):
                for t in range(NT + 1):
                    if t < NT:
                        ready(t)
                        v.bn_stats(stats[:, t, :], x[:, t, :]).then_inc(ln_stats, 1)
                    if t:
                        dve.wait_ge(ln_stats, k * NT + t)
                        v.bn_aggr(mv[:, t - 1, :], stats[:, t - 1, :]).then_inc(ln_aggr, 1)
                dve.wait_ge(ln_aggr, (k + 1) * NT)
                v.tensor_scalar(lnv[:, 0, :], mv[:, :, 1], EPS, None, ALU.add).then_inc(ln_var, 1)
                dve.wait_ge(ln_root, k + 1)
                s = 5 * k
                v.reciprocal(lnv[:, 2, :], lnv[:, 1, :]).then_inc(ln_step, 1)
                dve.wait_ge(ln_step, s + 1)
                v.tensor_tensor(lnv[:, 3, :], lnv[:, 2, :], lnv[:, 2, :], ALU.mult).then_inc(ln_step, 1)
                dve.wait_ge(ln_step, s + 2)
                v.tensor_tensor(lnv[:, 1, :], lnv[:, 3, :], lnv[:, 0, :], ALU.mult).then_inc(ln_step, 1)
                dve.wait_ge(ln_step, s + 3)
                v.tensor_scalar(lnv[:, 3, :], lnv[:, 1, :], -0.5, 1.5, ALU.mult, ALU.add).then_inc(ln_step, 1)
                dve.wait_ge(ln_step, s + 4)
                v.tensor_tensor(lnv[:, 4, :], lnv[:, 2, :], lnv[:, 3, :], ALU.mult).then_inc(ln_step, 1)
                dve.wait_ge(ln_step, s + 5)
                for c in LAST_NORM_ORDER[0:3] if k == 2 else range(NCH):
                    norm_chunk(c)

            v.memset(ps[:, CTX_BANK, :], 0.0).then_inc(fixed, 1)
            v.memset(ones[:], 1.0).then_inc(ones_ok, 1)
            layer_norm(0, lambda t: dve.wait_ge(x_in[t // TC], 16))
            v.memset(key_stack[0][96:NZM].bitcast(F32), 1.0).then_inc(fixed, 1)
            v.memset(query_stack[0][96:NZ].bitcast(F32), 1.0).then_inc(fixed, 1)
            v.memset(kvr[64:65, :], 1.0).then_inc(fixed, 1)
            v.memset(mstage[:, :, :, 0:3 * DC].bitcast(F32), 0.0).then_inc(fixed, 1)
            v.memset(mstage[:, :, :, 3 * DC:NZ].bitcast(F32), 1.0).then_inc(fixed, 1)
            dve.wait_ge(w0_in, 16 * W0_LOADS)
            for c in range(NCH):
                cols = slice(c * CH, (c + 1) * CH)
                dve.wait_ge(cq_hi, c + 1)
                v.scalar_tensor_tensor(out=cq[DC:2 * DC, cols], in0=ps_ctx[DC:2 * DC, :], scalar=bdq[DC:2 * DC, 0:1],
                                       in1=cq[DC:2 * DC, cols].bitcast(F32), op0=ALU.add,
                                       op1=ALU.subtract).then_inc(cq_lo, 1)
                if c == 0:
                    v.memset(key_stack[1][96:NZM].bitcast(F32), 1.0).then_inc(fixed, 1)
                if c == 1:
                    v.memset(query_stack[1][96:NZ].bitcast(F32), 1.0).then_inc(fixed, 1)
            dve.wait_ge(ckv_mm, 1)
            v.tensor_copy(ckv[:, :, :, 0:DC],
                          ps_wide[:, 0, :].rearrange("p (b t n) -> p t b n", b=B, n=DC)).then_inc(ckv_done, 1)

            def z_lo_part(u, pp, k):
                h, c = k % HP, k // HP
                cols = slice(c * CH, (c + 1) * CH)
                dve.wait_ge(z_hi, u * 4 + (k + 1))
                rows = slice(2 * DC, 3 * DC + 1)
                v.tensor_tensor(key_stack[pp][rows, h, cols], ps[rows, TURN0_BANKS[k % 2], :],
                                key_stack[pp][rows, h, cols].bitcast(F32), ALU.subtract).then_inc(z_lo, 1)

            def copy_cq(u, pp, hf, wait):
                if wait:
                    dve.wait_ge(st_mm, u * (HP * K0) + (HP * TS * (hf + 1) - 2 * HP * K0))
                src = cq[0:3 * DC, bass.ds((u // UH) * S + hf * CH, CH)]
                v.tensor_copy(query_stack[pp][0:3 * DC, :, hf * CH:(hf + 1) * CH],
                              src.unsqueeze(1).broadcast_to([3 * DC, HP, CH])).then_inc(cq_copied, 1)

            def maximum(u, pp, s, first=False):
                h, j, c = MX0[s]
                banks = MAX0_BANKS_FIRST if first else MAX0_BANKS
                dve.wait_ge(s_mm, u * len(MX0) + (s + 1))
                v.tensor_reduce(mx_part[pp][:, s:s + 1], ps[:, banks[s % len(banks)], :], AX_X, ALU.max).then_inc(max_done, 1)

            def split_max(u, pp, first):
                dve.wait_ge(max_done, u * len(MX0) + len(MX0))
                n = HP * TS
                v.tensor_tensor(mx[pp][:, 0:n], mx_part[pp][:, 0:n], mx_part[pp][:, n:2 * n],
                                ALU.max).then_inc(mx_ok, 1)
                dve.wait_ge(mx_ok, u + 1)
                m = mx[pp][:, 0:n].rearrange("p (t h) -> p h t", h=HP)
                if not first:
                    dve.wait_ge(m_turn, u * 4)
                v.tensor_scalar(mstage[:, :, :, NZ], m, -1.0, None, ALU.mult).then_inc(m_split, 1)
                dve.wait_ge(m_split, u * 2 + 1)
                v.scalar_tensor_tensor(out=mstage[:, :, :, NZ + 1], in0=m, scalar=-1.0,
                                       in1=mstage[:, :, :, NZ].bitcast(F32), op0=ALU.mult,
                                       op1=ALU.subtract).then_inc(m_split, 1)

            def max_rows(u, pp, h, hf):
                dve.wait_ge(m_turn, u * 4 + (2 * h + hf + 1))
                v.tensor_copy(query_stack[pp][96:NZM, h, hf * CH:(hf + 1) * CH],
                              ps[96:NZM, TURN0_BANKS[hf], :]).then_inc(m_rows, 1)

            ctxn = big[:].rearrange("p a t b n -> p (a t b n)").rearrange("p (t n) -> p t n", t=TS)

            def contexts_out(u, c, first=False):
                dve.wait_ge(ctx_turn, u * 2 + (c + 1))
                a = ps[:, TURN0_BANKS[1 - c], :].rearrange("p (t h n) -> p t h n", t=TC, h=HP)
                r = rden[:, 0:TC * HP].rearrange("p (t h) -> p t h", h=HP)
                if not first:
                    dve.wait_ge(ctx_out, u * 4 + 2 * c)
                v.reciprocal(r, a[:, :, :, DC]).then_inc(ctx_out, 1)
                dve.wait_ge(ctx_out, u * 4 + (2 * c + 1))
                dst = ctxn[:, c * TC:(c + 1) * TC, bass.ds(u * (HP * DC), HP * DC)].rearrange("p t (h n) -> p t h n", h=HP)
                v.tensor_tensor(dst, a[:, :, :, 0:DC], r.unsqueeze(3).broadcast_to([P, TC, HP, DC]),
                                ALU.mult).then_inc(ctx_out, 1)

            def unit0(u, pp, first=False, s=True, z=True):
                for n in range(len(MX0)):
                    if s and n == 1:
                        copy_cq(u + 1, 1 - pp, 1, not first)
                    for k in range(2):
                        if s and n == MX0_STEP * (Z0_SECOND[k] + 1):
                            z_lo_part(u + 1, 1 - pp, 2 + k)
                    if n == MX0_STEP * (CTX0_BEFORE + 1) and not first:
                        contexts_out(u - 1, 1)
                    if s:
                        maximum(u + 1, 1 - pp, n)
                if s:
                    split_max(u + 1, 1 - pp, False)
                contexts_out(u, 0, first)
                if s:
                    for h in range(HP):
                        for hf in range(2):
                            max_rows(u + 1, 1 - pp, h, hf)
                if z:
                    copy_cq(u + 2, pp, 0, True)
                    for k in range(2):
                        z_lo_part(u + 2, pp, k)

            copy_cq(0, 0, 0, False)
            copy_cq(0, 0, 1, False)
            copy_cq(1, 1, 0, False)
            for k in range(4):
                z_lo_part(0, 0, k)
            for n in range(len(MX0)):
                maximum(0, 0, n, True)
            split_max(0, 0, True)
            for h in range(HP):
                for hf in range(2):
                    max_rows(0, 0, h, hf)
            for k in range(2):
                z_lo_part(1, 1, k)
            unit0(0, 0, first=True)
            unit0(1, 1)
            with dve.Fori(1, U0 // 2 - 1) as i:
                unit0(i * 2, 0)
                unit0(i * 2 + 1, 1)
            unit0(U0 - 2, 0, z=False)
            unit0(U0 - 1, 1, s=False, z=False)
            contexts_out(U0 - 1, 1)

            def add_output1(t):
                c = t // TC
                if t % TC == 0:
                    dve.wait_ge(o_mm, c + 1)
                    xc = x[:, c * TC:(c + 1) * TC, :].rearrange("p t n -> p (t n)")
                    v.tensor_tensor(xc, ps_pair[:, c % 2, :], xc, ALU.add).then_inc(o_add, 1)
                    dve.wait_ge(o_add, c + 1)

            layer_norm(1, add_output1)
            gs = Steps(gate_step)
            dve.wait_ge(x_hi_ok, 1)
            v.tensor_tensor(x_lo[:], xnT[:, 0:CH], x_hi.bitcast(F32), ALU.subtract).then_inc(x_lo_ok, 1)
            dve.wait_ge(gate_mm, 1)
            logits = ps_ctx[:, 0:NT * E0].rearrange("p (t e) -> p t e", e=E0)
            top = g1[:, 0, :]

            def over_e(a):
                return a.unsqueeze(2).broadcast_to([P, NT, E0])

            v.tensor_reduce(top, logits, AX_X, ALU.max).then_inc(comb_ok, 1)
            dve.wait_ge(comb_ok, 1)
            gs.mark(v.tensor_tensor(g8[:, 0], logits, over_e(top), ALU.subtract))
            dve.wait_ge(gate_exp, 1)
            n = gs.mark(v.tensor_reduce(g1[:, 1, :], g8[:, 1], AX_X, ALU.add))
            dve.wait_ge(gate_step, n)
            n = gs.mark(v.reciprocal(g1[:, 2, :], g1[:, 1, :]))
            dve.wait_ge(gate_step, n)
            n = gs.mark(v.tensor_tensor(g8[:, 2], g8[:, 1], over_e(g1[:, 2, :]), ALU.mult))
            dve.wait_ge(gate_step, n)
            def hidden_piece(ch, e, f):
                n, m = 3 * e + f, FM[f]
                dve.wait_ge(silu_done, ch * (3 * NE) + (n + 1))
                dve.wait_ge(eu_mm, ch * (3 * NE) + (n + 1))
                if f == 0:
                    dve.wait_ge(ed_mm, ch * NE + max(e - 1, 0))
                v.tensor_tensor(pt[0:m, 3 * (e % 2) + f, :], ps_wide[0:m, 2 + n % 2, :], pt[0:m, 6 + n % 2, :],
                                ALU.mult).then_inc(h_done, 1)

            def hidden(ch, e):
                for f in range(3):
                    hidden_piece(ch, e, f)

            p_e = g8[:, 2].unsqueeze(3).broadcast_to([P, NT, E0, E0])
            p_j = g8[:, 2].unsqueeze(2).broadcast_to([P, NT, E0, E0])
            gs.mark(v.tensor_tensor(g64[:, 0], p_j, p_e, ALU.is_gt))
            hidden_piece(0, 0, 0)
            n = gs.mark(v.tensor_tensor(g64[:, 1], p_j, p_e, ALU.is_equal))
            hidden_piece(0, 0, 1)
            dve.wait_ge(gate_step, n)
            n = gs.mark(v.tensor_tensor(g64[:, 1], g64[:, 1], tri[:].unsqueeze(1).broadcast_to([P, NT, E0, E0]),
                                        ALU.mult))
            hidden_piece(0, 0, 2)
            dve.wait_ge(gate_step, n)
            n = gs.mark(v.tensor_tensor(g64[:, 0], g64[:, 0], g64[:, 1], ALU.add))
            hidden_piece(0, 1, 0)
            dve.wait_ge(gate_step, n)
            n = gs.mark(v.tensor_reduce(g8[:, 3], g64[:, 0], AX_X, ALU.add))
            hidden_piece(0, 1, 1)
            dve.wait_ge(gate_step, n)
            n = gs.mark(v.scalar_tensor_tensor(out=g8[:, 0], in0=g8[:, 3], scalar=1.5, in1=g8[:, 2],
                                               op0=ALU.is_lt, op1=ALU.mult))
            dve.wait_ge(gate_step, n)
            n = gs.mark(v.tensor_reduce(g1[:, 1, :], g8[:, 0], AX_X, ALU.add))
            dve.wait_ge(gate_step, n)
            n = gs.mark(v.tensor_scalar(g1[:, 2, :], g1[:, 1, :], 1e-20, None, ALU.add))
            dve.wait_ge(gate_step, n)
            n = gs.mark(v.reciprocal(g1[:, 3, :], g1[:, 2, :]))
            dve.wait_ge(gate_step, n)
            dve.wait_ge(consts, N_CONST)
            v.tensor_tensor(comb[:, :, 0:E0], g8[:, 0], over_e(g1[:, 3, :]), ALU.mult).then_inc(comb_ok, 1)
            hidden_piece(0, 1, 2)
            dve.wait_ge(comb_ok, 2)

            def accumulate(ch, e):
                dve.wait_ge(ed_mm, ch * NE + (e + 1))
                for t in range(TC):
                    dve.wait_ge(moe_add, ch * (TC * NE) + max(TC * (e - 1) + t + 1, 0))
                    xt = x[:, bass.ds(ch * TC + t, 1), :].rearrange("p o n -> p (o n)")
                    w = comb[:, bass.ds(ch * TC + t, 1), e:e + 1].rearrange("p o n -> p (o n)")
                    v.scalar_tensor_tensor(out=xt, in0=ps_pair[:, e % 2, t * P:(t + 1) * P], scalar=w, in1=xt,
                                           op0=ALU.mult, op1=ALU.add).then_inc(moe_add, 1)

            def front(c, e):
                n0 = c * N_NORM
                if e == FRONT_STATS:
                    dve.wait_ge(moe_add, c * (TC * NE) + TC * NE)
                    for t in range(TC):
                        v.bn_stats(stats[:, t, :], x[:, bass.ds(c * TC + t, 1), :].rearrange("p o n -> p (o n)")
                                   ).then_inc(norm_step, 1)
                    dve.wait_ge(norm_step, n0 + TC)
                    v.tensor_copy(norm[:, 2, :], stats[:, 0:TC, 0]).then_inc(norm_step, 1)
                    for t in range(TC):
                        v.bn_aggr(mv[:, t, :], stats[:, t, :]).then_inc(norm_step, 1)
                if e == FRONT_RSTD:
                    var, neg, tmp, r = (norm[:, k, :] for k in range(4))
                    n = 2 * TC + 1
                    dve.wait_ge(norm_step, n0 + n)
                    v.tensor_scalar(var, mv[:, 0:TC, 1], EPS, None, ALU.add).then_inc(norm_step, 1)
                    dve.wait_ge(norm_step, n0 + (n + 1))
                    v.tensor_scalar(neg, var, -0.5, None, ALU.mult).then_inc(norm_step, 1)
                    v.tensor_scalar(norm_bits[:], var.bitcast(I32), 1, None, ALU.logical_shift_right).then_inc(norm_step, 1)
                    dve.wait_ge(norm_step, n0 + (n + 3))
                    v.tensor_scalar(r.bitcast(I32), norm_bits[:], -1.0, float(0x5F3759DF), ALU.mult,
                                    ALU.add).then_inc(norm_step, 1)
                    n += 4
                    for _ in range(NEWTON):
                        dve.wait_ge(norm_step, n0 + n)
                        v.tensor_tensor(tmp, r, r, ALU.mult).then_inc(norm_step, 1)
                        dve.wait_ge(norm_step, n0 + (n + 1))
                        v.tensor_tensor(tmp, tmp, neg, ALU.mult).then_inc(norm_step, 1)
                        dve.wait_ge(norm_step, n0 + (n + 2))
                        v.scalar_tensor_tensor(out=r, in0=tmp, scalar=1.5, in1=r, op0=ALU.add,
                                               op1=ALU.mult).then_inc(norm_step, 1)
                        n += 3
                if e == FRONT_XN:
                    dve.wait_ge(norm_step, n0 + N_NORM)
                    for t in range(TC):
                        v.tensor_scalar(xn[:, t, :], x[:, bass.ds(c * TC + t, 1), :].rearrange("p o n -> p (o n)"),
                                        mv[:, t, 0:1], norm[:, 3, t:t + 1], ALU.subtract, ALU.mult).then_inc(norm_xn, 1)
                for a in range(2):
                    if e == FRONT_ROPE[a]:
                        i0, b, h = c % 2 * TC, c // 2, DH // 2
                        qk = big[:, a].rearrange("p t b n -> p t (b n)")[:, bass.ds(i0, TC), bass.ds(b * D, D)] \
                            .rearrange("p t (h w) -> p t h w", w=DH)
                        scratch = half[:, 2 * a * CH:2 * (a + 1) * CH].rearrange("p (k t h w) -> p k t h w", k=2, t=TC, w=DH)
                        ta, tb = scratch[:, 0], scratch[:, 1]

                        def over_heads(tab, lo, hi):
                            return tab[:, bass.ds(i0, TC), lo:hi].unsqueeze(2).broadcast_to([P, TC, H1, hi - lo])

                        dve.wait_ge(qk_out, c * TC + TC)
                        v.tensor_tensor(ta, qk, over_heads(cos, 0, DH), ALU.mult).then_inc(rope_mul, 1)
                        v.tensor_tensor(tb[:, :, :, 0:h], qk[:, :, :, h:DH], over_heads(sin, 0, h), ALU.mult).then_inc(rope_mul, 1)
                        v.tensor_tensor(tb[:, :, :, h:DH], qk[:, :, :, 0:h], over_heads(sin, h, DH), ALU.mult).then_inc(rope_mul, 1)
                        dve.wait_ge(rope_mul, c * 6 + (3 * a + 3))
                        v.tensor_tensor(qk, ta, tb, ALU.add).then_inc(rope_step, 1)
                        dve.wait_ge(rope_step, c * 2 + (a + 1))

            def experts(ch, beside=True, following=True):
                if beside:
                    hidden(ch, 0)
                for e in range(NE):
                    if e + 1 < NE and (beside or e):
                        hidden(ch, e + 1)
                    if following and e + 2 == E0:
                        dve.wait_ge(x_hi_ok, ch + 2)
                        v.tensor_tensor(x_lo[:], xnT[:, bass.ds((ch + 1) * CH, CH)], x_hi.bitcast(F32),
                                        ALU.subtract).then_inc(x_lo_ok, 1)
                    accumulate(ch, e)
                    if beside:
                        front(ch - 1, e)

            experts(0, beside=False)
            dve.wait_ge(w1_in, 16 * W1_LOADS)
            with dve.Fori(1, NCH - 1) as ch:
                experts(ch)
            experts(NCH - 1, following=False)
            for e in range(FRONT_ROPE[0]):
                front(NCH - 1, e)

            def maximum1(u, pp, s, first=False):
                r, c, parts = MX1[s]
                banks = MAX1_BANKS_FIRST if first else MAX1_BANKS
                dve.wait_ge(s1_mm, u * len(MX1) + (s + 1))
                for i, o, w in parts:
                    n = TS * r + (i if i < TC else 2 * (i - TC) + c)
                    dst = (mx if i < TC else mx_part)[pp][:, n:n + 1]
                    v.tensor_reduce(dst, ps[:, banks[s % len(banks)], o:o + w], AX_X, ALU.max).then_inc(max1_done, 1)

            def split_max1(u, pp):
                dve.wait_ge(max1_done, u * NMX1 + NMX1)
                part = mx_part[pp][:].rearrange("p (r t c) -> p r t c", r=HG, c=2)
                v.tensor_tensor(mx[pp][:].rearrange("p (r t) -> p r t", r=HG)[:, :, TC:TS], part[:, :, :, 0],
                                part[:, :, :, 1], ALU.max).then_inc(mx1_ok, 1)
                dve.wait_ge(mx1_ok, u + 1)
                m = mx[pp][:].rearrange("p (r t) -> p t r", r=HG)
                hi, lo = (qstage[pp][:, :, :, 3 * DH + n] for n in range(2))
                v.tensor_scalar(hi, m, -1.0, None, ALU.mult).then_inc(m1_split, 1)
                dve.wait_ge(m1_split, u * 2 + 1)
                v.scalar_tensor_tensor(out=lo, in0=m, scalar=-1.0, in1=hi.bitcast(F32), op0=ALU.mult,
                                       op1=ALU.subtract).then_inc(m1_split, 1)

            def contexts_out1(u, c):
                dve.wait_ge(ctx1_turn, u * 2 + (c + 1))
                a = ps[:, TURN1_BANK, :].rearrange("p (t r n) -> p t r n", t=TC, r=HG)
                r = rden[:].rearrange("p (t r) -> p t r", r=HG)
                v.reciprocal(r, a[:, :, :, DH]).then_inc(ctx1_out, 1)
                dve.wait_ge(ctx1_out, u * 4 + (2 * c + 1))
                dst = ao.rearrange("p t b n -> p t (b n)")[:, c * TC:(c + 1) * TC, bass.ds(u * (HG * DH), HG * DH)] \
                    .rearrange("p t (r w) -> p t r w", w=DH)
                v.tensor_tensor(dst, a[:, :, :, 0:DH], r.unsqueeze(3).broadcast_to([P, TC, HG, DH]),
                                ALU.mult).then_inc(ctx1_out, 1)

            def unit1(u, pp, first=False, s=True):
                for n in range(len(MX1)):
                    if n == MX1_UPTO[CTX1_BEFORE] and not first:
                        contexts_out1(u - 1, 1)
                    if n == MX1_UPTO[CTX1_FIRST]:
                        contexts_out1(u, 0)
                    if s:
                        maximum1(u + 1, 1 - pp, n)
                if s:
                    split_max1(u + 1, 1 - pp)

            for n in range(len(MX1)):
                maximum1(0, 0, n, True)
                if n == FIRST_QKV[1] + 2:
                    for e in FRONT_ROPE:
                        front(NCH - 1, e)
            dve.wait_ge(rope_step, 2 * NCH)
            split_max1(0, 0)
            unit1(0, 0, first=True)
            unit1(1, 1)
            with dve.Fori(1, U1 // 2 - 1) as i:
                unit1(i * 2, 0)
                unit1(i * 2 + 1, 1)
            unit1(U1 - 2, 0)
            unit1(U1 - 1, 1, s=False)
            contexts_out1(U1 - 1, 1)

            def add_output2(t):
                c = t // TC
                if t % TC == 0:
                    dve.wait_ge(o1_mm, c + 1)
                    xc = x[:, c * TC:(c + 1) * TC, :].rearrange("p t n -> p (t n)")
                    v.tensor_tensor(xc, ps_pair[:, c % 2, :], xc, ALU.add).then_inc(o1_add, 1)
                    dve.wait_ge(o1_add, c + 1)

            layer_norm(2, add_output2)

            rs = Steps(rt_step)
            dve.wait_ge(rt_mm, 1)
            n = rs.mark(v.tensor_copy(rt[:, 0], ps_ctx[0:1, 0:B * E1].rearrange("p (b e) -> p b e", b=B)))
            dve.wait_ge(rt_step, n)
            s_e = rt[:, 0].unsqueeze(3).broadcast_to([1, B, E1, E1])
            s_j = rt[:, 0].unsqueeze(2).broadcast_to([1, B, E1, E1])
            rs.mark(v.tensor_tensor(rt64[:, 0], s_j, s_e, ALU.is_gt))
            n = rs.mark(v.tensor_tensor(rt64[:, 1], s_j, s_e, ALU.is_equal))
            dve.wait_ge(rt_step, n)
            n = rs.mark(v.tensor_tensor(rt64[:, 1], rt64[:, 1], tri[0:1].unsqueeze(1).broadcast_to([1, B, E1, E1]),
                                        ALU.mult))
            dve.wait_ge(rt_step, n)
            n = rs.mark(v.tensor_tensor(rt64[:, 0], rt64[:, 0], rt64[:, 1], ALU.add))
            dve.wait_ge(rt_step, n)
            n = rs.mark(v.tensor_reduce(rt[:, 1], rt64[:, 0], AX_X, ALU.add))
            dve.wait_ge(rt_step, n)
            for k in range(2):
                n = rs.mark(v.scalar_tensor_tensor(out=rt[:, 2 + k], in0=rt[:, 1], scalar=float(k),
                                                   in1=ecount[:].unsqueeze(1).broadcast_to([1, B, E1]),
                                                   op0=ALU.is_equal, op1=ALU.mult))
            dve.wait_ge(rt_step, n)
            for k in range(2):
                n = rs.mark(v.tensor_reduce(idx_f[:, :, k], rt[:, 2 + k], AX_X, ALU.add))
            dve.wait_ge(rt_step, n)
            v.tensor_copy(idx_i[:], idx_f[:]).then_inc(idx_ok, 1)

            norm_chunk(3)
            for c in range(NCH):
                if c % (NCH // B) == 0:
                    b = c // (NCH // B)
                    dve.wait_ge(chosen_ok, 4 * (b + 1))
                    v.tensor_tensor(b2_sum[:, b, :], b2[:, b, 0, :], b2[:, b, 1, :], ALU.add).then_inc(b2_ok, 1)
                dve.wait_ge(y_mm, c + 1)
                xc = x[:, c * TC:(c + 1) * TC, :].rearrange("p t n -> p (t n)")
                v.scalar_tensor_tensor(out=xc, in0=ps_pair[:, c % 2, :], scalar=0.5, in1=xc,
                                       op0=ALU.mult, op1=ALU.add).then_inc(y_add, 1)


def lay_out(i):
    a = {k: np.asarray(v) for k, v in i.items()}
    f = np.float32

    def heads(w, b, n):
        return (w.reshape(w.shape[0], H0, n).transpose(2, 1, 0), b.reshape(1, H0, n).transpose(2, 1, 0))

    uq, ubq = heads(a["L0_attn_W_UQ"], a["L0_attn_b_UQ"], DK)
    qr, qrb = heads(a["L0_attn_W_QR"], a["L0_attn_b_QR"], DR)
    uk, ukb = heads(a["L0_attn_W_UK"], a["L0_attn_b_UK"], DK)
    uv, uvb = heads(a["L0_attn_W_UV"], a["L0_attn_b_UV"], DK)
    up = np.concatenate([a["L0_ffn_expert_gate"], a["L0_ffn_shared_gate"][None]], 0)
    uu = np.concatenate([a["L0_ffn_expert_up"], a["L0_ffn_shared_up"][None]], 0)
    dn = np.concatenate([a["L0_ffn_expert_down"], a["L0_ffn_shared_down"][None]], 0).transpose(0, 2, 1)
    dnp = np.zeros((NE, 3 * P, D), f)
    dnp[:, :F0] = dn
    dnp = dnp.reshape(NE, 3, P, D).transpose(2, 0, 1, 3).reshape(P, NE, 3 * D)
    wm = np.concatenate([up.transpose(2, 0, 1), uu.transpose(2, 0, 1), dnp], 2)

    inv = (f(1.0) / f(10000.0) ** (np.arange(0, DH, 2, dtype=f) / f(DH))).astype(f)
    fr = np.arange(S, dtype=f)[:, None] * inv[None, :]
    c, s = np.cos(fr).astype(f), np.sin(fr).astype(f)
    cos = np.concatenate([c, c], 1).reshape(TS, P, DH).transpose(1, 0, 2)
    sin = np.concatenate([-s, s], 1).reshape(TS, P, DH).transpose(1, 0, 2)
    bf = mybir.dt.np(BF16)
    later = np.triu(np.full((P, P), NEG, f), 1)
    tri = np.broadcast_to(np.tril(np.ones((E0, E0), f), -1), (P, E0, E0))
    out = {
        "x": a["L0_attn_h_t"].reshape(T, D),
        "uk": np.concatenate([uk, np.zeros((DK, H0, 64 - DC), f), ukb], 2),
        "uq": np.concatenate([uq, uq, uq, ubq, ubq], 2),
        "qr": np.concatenate([qr, qr, qr, qrb, qrb], 2),
        "uv": np.concatenate([uv, uvb], 2),
        "wo": a["L0_attn_W_O"].reshape(H0, DK, D).transpose(1, 0, 2),
        "bo": a["L0_attn_b_O"][None],
        "wdq": np.concatenate([a["L0_attn_W_DQ"]] * 3, 1),
        "bdq": np.concatenate([a["L0_attn_b_DQ"]] * 3)[:, None],
        "wkv": np.concatenate([a["L0_attn_W_DKV"], a["L0_attn_W_KR"]], 1),
        "bkv": np.concatenate([a["L0_attn_b_DKV"], a["L0_attn_b_KR"]])[:, None],
        "bkv_row": a["L0_attn_b_DKV"][None],
        "ident": np.eye(P, dtype=f), "identb": np.eye(P).astype(bf),
        "mask_qk": later.astype(bf), "mask_kq": later.T.astype(bf),
        "gw": a["L0_ffn_gate_w"].T, "tri": tri, "wm": wm,
        "wqkv": a["L1_attn_w_qkv"], "wout": a["L1_attn_w_out"], "cos": cos, "sin": sin,
        "wr": a["L1_ffn_Wr"], "br": a["L1_ffn_br"][None], "ecount": np.arange(E1, dtype=f)[None],
        "experts1": np.concatenate([a["L1_ffn_W1"], a["L1_ffn_W2"], a["L1_ffn_b1"][:, :, None]], 2).transpose(1, 0, 2),
        "b2": a["L1_ffn_b2"][None],
    }
    return {k: np.ascontiguousarray(v) for k, v in out.items()}


def kernel(**inputs):
    import concourse.bacc as bacc
    from concourse.bass_utils import run_bass_kernel_spmd

    arrays = {f"in_{k}": v for k, v in lay_out(inputs).items()}
    nc = bacc.Bacc("TRN2", target_bir_lowering=False, num_devices=1)
    d = {k[3:]: nc.dram_tensor(k, v.shape, mybir.dt.from_np(v.dtype), kind="ExternalInput").ap()
         for k, v in arrays.items()}
    out = nc.dram_tensor("out_0", (T, D), F32, kind="ExternalOutput").ap()
    build(nc, d, out)
    r = run_bass_kernel_spmd(nc, [arrays], core_ids=[0])
    return r.results[0]["out_0"].reshape(B, S, D)
```
